# Optimizing a Trainium2 kernel written in Bass

```python
import numpy as np
import jax
import jax.numpy as jnp

def _softmax(x, axis=-1):
    return jax.nn.softmax(x, axis=axis)

def _gelu(x):
    return jax.nn.gelu(x, approximate=True)

def _silu(x):
    return jax.nn.silu(x)

def _sigmoid(x):
    return jax.nn.sigmoid(x)

def _layernorm(x, axis=-1, eps=1e-05):
    m = jnp.mean(x, axis=axis, keepdims=True)
    v = jnp.var(x, axis=axis, keepdims=True)
    return (x - m) / jnp.sqrt(v + eps)

def _scatter_add(tgt, idx, src, axis=0):
    return tgt.at[idx].add(src)

def _segment_sum(src, seg, n):
    return jax.ops.segment_sum(src, seg, n)
kernel_name = 'mk_metaformer_d2_conv_nchw256_r2_059149'

def setup_inputs(seed: int=0):
    np.random.seed(seed)
    _w = jnp.asarray

    def _rec_inputs():
        import jax
        import jax.numpy as jnp
        _gk = jax.random.key(seed)
        x = -0.0002928 + 1 * jax.random.normal(jax.random.fold_in(_gk, 1), (16, 128, 32, 32), jnp.float32)
        return x
    x = _rec_inputs()

    def _L0_conv_setup():
        import jax, jax.numpy as jnp
        import numpy as np
        from jax import lax
        NUM_EXPERTS = 4
        TOP_K = 2
        NUM_GROUPS = 8
        WEIGHT_THRESHOLD = 0.01
        TEMPERATURE = 1.0
        EPS = 1e-05

        def group_norm(x, gamma, beta, groups=NUM_GROUPS, eps=EPS):
            B, C, H, W = x.shape
            xr = x.reshape(B, groups, C // groups, H, W)
            mu = jnp.mean(xr, axis=(2, 3, 4), keepdims=True)
            var = jnp.var(xr, axis=(2, 3, 4), keepdims=True)
            xn = ((xr - mu) * lax.rsqrt(var + eps)).reshape(B, C, H, W)
            return xn * gamma[None, :, None, None] + beta[None, :, None, None]
        key = jax.random.key(seed)
        ks = jax.random.split(key, 8)
        B, C, O, H, W = (16, 128, 128, 32, 32)
        E, Cr = (NUM_EXPERTS, C // 16)
        return {'x': jax.random.normal(ks[0], (B, C, H, W), jnp.float32), 'router_w1': jax.random.normal(ks[1], (Cr, C), jnp.float32) * 0.05, 'router_b1': jnp.zeros((Cr,), jnp.float32), 'router_w2': jax.random.normal(ks[2], (E, Cr), jnp.float32) * 0.01, 'router_b2': jnp.zeros((E,), jnp.float32), 'expert_w': jax.random.normal(ks[3], (E, O, C, 3, 3), jnp.float32) * 0.03, 'expert_gn_gamma': jnp.ones((E, O), jnp.float32), 'expert_gn_beta': jnp.zeros((E, O), jnp.float32), 'shared_w': jax.random.normal(ks[4], (O, C), jnp.float32) * 0.05, 'shared_gn_gamma': jnp.ones((O,), jnp.float32), 'shared_gn_beta': jnp.zeros((O,), jnp.float32)}
    _L0_conv_all = _L0_conv_setup()
    _L0_conv_in = {k: v for k, v in _L0_conv_all.items() if k in ('router_w1', 'router_b1', 'router_w2', 'router_b2', 'expert_w', 'expert_gn_gamma', 'expert_gn_beta', 'shared_w', 'shared_gn_gamma', 'shared_gn_beta')}
    del _L0_conv_all

    def _L0_ffn_setup():
        import jax, jax.numpy as jnp
        import numpy as np
        N_EXPERTS = 8
        TOP_K = 2
        key = jax.random.key(seed)
        ks = jax.random.split(key, 5)
        B, T, C, E, H = (8, 1024, 128, 8, 341)
        scale = 1.0 / np.sqrt(C)
        return {'x': jax.random.normal(ks[0], (B, T, C), dtype=jnp.float32), 'router_w': jax.random.normal(ks[1], (E, C), dtype=jnp.float32) * scale, 'w1': jax.random.normal(ks[2], (E, H, C), dtype=jnp.float32) * scale, 'w2': jax.random.normal(ks[3], (E, C, H), dtype=jnp.float32) * (1.0 / np.sqrt(H)), 'w3': jax.random.normal(ks[4], (E, H, C), dtype=jnp.float32) * scale}
    _L0_ffn_all = _L0_ffn_setup()
    _L0_ffn_in = {k: v for k, v in _L0_ffn_all.items() if k in ('router_w', 'w1', 'w2', 'w3')}
    del _L0_ffn_all

    def _L1_conv_setup():
        import jax, jax.numpy as jnp
        import numpy as np
        B, C, H, W = (32, 128, 48, 48)
        K = 3
        PAD = K // 2
        key = jax.random.key(seed)
        k1, k2, k3 = jax.random.split(key, 3)
        x = jax.random.normal(k1, (B, C, H, W), dtype=jnp.float32)
        w1 = jax.random.normal(k2, (C, C), dtype=jnp.float32) * 0.02
        b1 = jnp.zeros((C,), dtype=jnp.float32)
        w2 = jax.random.normal(k3, (C * K * K, C), dtype=jnp.float32) * 0.02
        b2 = jnp.zeros((C * K * K,), dtype=jnp.float32)
        return {'x': x, 'w1': w1, 'b1': b1, 'w2': w2, 'b2': b2}
    _L1_conv_all = _L1_conv_setup()
    _L1_conv_in = {k: v for k, v in _L1_conv_all.items() if k in ('w1', 'b1', 'w2', 'b2')}
    del _L1_conv_all

    def _L1_ffn_setup():
        import math
        import jax, jax.numpy as jnp
        import numpy as np
        CAPACITY_FACTOR = 1.25
        key = jax.random.key(seed)
        ks = jax.random.split(key, 5)
        B, L, D, F, E = (8, 4096, 128, 512, 8)
        h = jax.random.normal(ks[0], (B, L, D), dtype=jnp.float32)
        gate_w = jax.random.normal(ks[1], (D, E), dtype=jnp.float32) * 0.02
        gate_b = jnp.zeros((E,), dtype=jnp.float32)
        w1 = jax.random.normal(ks[2], (E, D, F), dtype=jnp.float32) * (1.0 / math.sqrt(D))
        b1 = jnp.zeros((E, F), dtype=jnp.float32)
        w2 = jax.random.normal(ks[3], (E, F, D), dtype=jnp.float32) * (1.0 / math.sqrt(F))
        b2 = jnp.zeros((E, D), dtype=jnp.float32)
        return {'h': h, 'gate_w': gate_w, 'gate_b': gate_b, 'w1': w1, 'b1': b1, 'w2': w2, 'b2': b2}
    _L1_ffn_all = _L1_ffn_setup()
    _L1_ffn_in = {k: v for k, v in _L1_ffn_all.items() if k in ('gate_w', 'gate_b', 'w1', 'b1', 'w2', 'b2')}
    del _L1_ffn_all
    return {'x': x, 'L0_conv_router_w1': _L0_conv_in['router_w1'], 'L0_conv_router_b1': _L0_conv_in['router_b1'], 'L0_conv_router_w2': _L0_conv_in['router_w2'], 'L0_conv_router_b2': _L0_conv_in['router_b2'], 'L0_conv_expert_w': _L0_conv_in['expert_w'], 'L0_conv_expert_gn_gamma': _L0_conv_in['expert_gn_gamma'], 'L0_conv_expert_gn_beta': _L0_conv_in['expert_gn_beta'], 'L0_conv_shared_w': _L0_conv_in['shared_w'], 'L0_conv_shared_gn_gamma': _L0_conv_in['shared_gn_gamma'], 'L0_conv_shared_gn_beta': _L0_conv_in['shared_gn_beta'], 'L0_ffn_router_w': _L0_ffn_in['router_w'], 'L0_ffn_w1': _L0_ffn_in['w1'], 'L0_ffn_w2': _L0_ffn_in['w2'], 'L0_ffn_w3': _L0_ffn_in['w3'], 'L1_conv_w1': _L1_conv_in['w1'], 'L1_conv_b1': _L1_conv_in['b1'], 'L1_conv_w2': _L1_conv_in['w2'], 'L1_conv_b2': _L1_conv_in['b2'], 'L1_ffn_gate_w': _L1_ffn_in['gate_w'], 'L1_ffn_gate_b': _L1_ffn_in['gate_b'], 'L1_ffn_w1': _L1_ffn_in['w1'], 'L1_ffn_b1': _L1_ffn_in['b1'], 'L1_ffn_w2': _L1_ffn_in['w2'], 'L1_ffn_b2': _L1_ffn_in['b2']}

def reference(x, L0_conv_router_w1, L0_conv_router_b1, L0_conv_router_w2, L0_conv_router_b2, L0_conv_expert_w, L0_conv_expert_gn_gamma, L0_conv_expert_gn_beta, L0_conv_shared_w, L0_conv_shared_gn_gamma, L0_conv_shared_gn_beta, L0_ffn_router_w, L0_ffn_w1, L0_ffn_w2, L0_ffn_w3, L1_conv_w1, L1_conv_b1, L1_conv_w2, L1_conv_b2, L1_ffn_gate_w, L1_ffn_gate_b, L1_ffn_w1, L1_ffn_b1, L1_ffn_w2, L1_ffn_b2):
    import jax
    import jax.numpy as jnp

    def _L0_conv_ref(x, router_w1, router_b1, router_w2, router_b2, expert_w, expert_gn_gamma, expert_gn_beta, shared_w, shared_gn_gamma, shared_gn_beta):
        import jax, jax.numpy as jnp
        import numpy as np
        from jax import lax
        NUM_EXPERTS = 4
        TOP_K = 2
        NUM_GROUPS = 8
        WEIGHT_THRESHOLD = 0.01
        TEMPERATURE = 1.0
        EPS = 1e-05

        def group_norm(x, gamma, beta, groups=NUM_GROUPS, eps=EPS):
            B, C, H, W = x.shape
            xr = x.reshape(B, groups, C // groups, H, W)
            mu = jnp.mean(xr, axis=(2, 3, 4), keepdims=True)
            var = jnp.var(xr, axis=(2, 3, 4), keepdims=True)
            xn = ((xr - mu) * lax.rsqrt(var + eps)).reshape(B, C, H, W)
            return xn * gamma[None, :, None, None] + beta[None, :, None, None]
        B, C, H, W = x.shape
        E = router_w2.shape[0]
        pooled = jnp.mean(x, axis=(2, 3))
        h = jax.nn.silu(pooled @ router_w1.T + router_b1)
        logits = (h @ router_w2.T + router_b2) / TEMPERATURE
        probs = jax.nn.softmax(logits, axis=-1)
        top_v, top_i = lax.top_k(probs, TOP_K)
        w = top_v / jnp.sum(top_v, axis=-1, keepdims=True)
        w = jnp.where(w >= WEIGHT_THRESHOLD, w, 0.0)
        gate = jnp.sum(jax.nn.one_hot(top_i, E, dtype=x.dtype) * w[..., None], axis=1)
        shared = jnp.einsum('oc,bchw->bohw', shared_w, x)
        shared = jax.nn.silu(group_norm(shared, shared_gn_gamma, shared_gn_beta))

        def expert_fn(we, ge, be):
            y = lax.conv_general_dilated(x, we, (1, 1), 'SAME', dimension_numbers=('NCHW', 'OIHW', 'NCHW'))
            return jax.nn.silu(group_norm(y, ge, be))
        expert_out = jax.vmap(expert_fn)(expert_w, expert_gn_gamma, expert_gn_beta)
        moe_out = jnp.einsum('be,ebohw->bohw', gate, expert_out)
        return shared + moe_out

    def _L0_ffn_ref(x, router_w, w1, w2, w3):
        import jax, jax.numpy as jnp
        import numpy as np
        N_EXPERTS = 8
        TOP_K = 2
        B, T, C = x.shape
        flat = x.reshape(-1, C)
        logits = flat @ router_w.T
        probs = jax.nn.softmax(logits, axis=-1)
        topk_probs, topk_idx = jax.lax.top_k(probs, TOP_K)
        topk_probs = topk_probs / (jnp.sum(topk_probs, axis=-1, keepdims=True) + 1e-09)
        onehot = jax.nn.one_hot(topk_idx, N_EXPERTS, dtype=flat.dtype)
        gates = jnp.einsum('nk,nke->ne', topk_probs, onehot)
        h1 = jnp.einsum('nc,ehc->neh', flat, w1)
        h3 = jnp.einsum('nc,ehc->neh', flat, w3)
        h = jax.nn.silu(h1) * h3
        y = jnp.einsum('neh,ech->nec', h, w2)
        out = jnp.einsum('ne,nec->nc', gates, y)
        return out.reshape(B, T, C)

    def _L1_conv_ref(x, w1, b1, w2, b2):
        import jax, jax.numpy as jnp
        import numpy as np
        B, C, H, W = (32, 128, 48, 48)
        K = 3
        PAD = K // 2
        Bs, Cs, Hs, Ws = x.shape
        pooled = x.mean(axis=(2, 3))
        h = jax.nn.gelu(pooled @ w1.T + b1, approximate=False)
        wdyn = (h @ w2.T + b2).reshape(Bs, Cs, K * K)
        xp = jnp.pad(x, ((0, 0), (0, 0), (PAD, PAD), (PAD, PAD)), mode='reflect')
        out = jnp.zeros_like(x)
        for i in range(K):
            for j in range(K):
                idx = i * K + j
                out = out + xp[:, :, i:i + Hs, j:j + Ws] * wdyn[:, :, idx, None, None]
        return out

    def _L1_ffn_ref(h, gate_w, gate_b, w1, b1, w2, b2):
        import math
        import jax, jax.numpy as jnp
        import numpy as np
        CAPACITY_FACTOR = 1.25
        B, L, D = h.shape
        E = gate_w.shape[1]
        T = B * L
        C = max(1, math.ceil(CAPACITY_FACTOR * T / E))
        x = h.reshape(T, D)
        logits = x @ gate_w + gate_b
        probs = jax.nn.softmax(logits, axis=-1)
        idx = jnp.argmax(probs, axis=-1)
        prb = jnp.take_along_axis(probs, idx[:, None], axis=1)[:, 0]
        one_hot = jax.nn.one_hot(idx, E, dtype=jnp.float32)
        pos = (jnp.cumsum(one_hot, axis=0) * one_hot).sum(-1).astype(jnp.int32) - 1
        kept = pos < C
        pos_safe = jnp.where(kept, pos, C)
        buf = jnp.zeros((E, C, D), dtype=h.dtype).at[idx, pos_safe].set(x, mode='drop')
        hmid = jax.nn.relu(jnp.einsum('ecd,edf->ecf', buf, w1) + b1[:, None, :])
        ybuf = jnp.einsum('ecf,efd->ecd', hmid, w2) + b2[:, None, :]
        pos_g = jnp.minimum(pos, C - 1)
        y_tok = ybuf[idx, pos_g] * (prb * kept)[:, None]
        y = y_tok.reshape(B, L, D)
        y = jnp.nan_to_num(y, nan=0.0, posinf=10000.0, neginf=-10000.0)
        return y

    def _gn(v, G=32, eps=1e-05):
        B_, C_, H_, W_ = v.shape
        g = v.reshape(B_, G, C_ // G, H_, W_)
        m = jnp.mean(g, axis=(2, 3, 4), keepdims=True)
        s = jnp.var(g, axis=(2, 3, 4), keepdims=True)
        return ((g - m) / jnp.sqrt(s + eps)).reshape(v.shape)

    def _ln_c(v, eps=1e-06):
        m = jnp.mean(v, axis=1, keepdims=True)
        s = jnp.var(v, axis=1, keepdims=True)
        return (v - m) / jnp.sqrt(s + eps)

    def _ln_t(v, eps=1e-05):
        m = jnp.mean(v, axis=-1, keepdims=True)
        s = jnp.var(v, axis=-1, keepdims=True)
        return (v - m) / jnp.sqrt(s + eps)

    def _to_tokens(v):
        B_, C_, H_, W_ = v.shape
        return v.reshape(B_, C_, H_ * W_).transpose(0, 2, 1)

    def _from_tokens(t, like):
        B_, C_, H_, W_ = like.shape
        return t.transpose(0, 2, 1).reshape(B_, C_, H_, W_)
    x = x + _L0_conv_ref(_ln_c(x), L0_conv_router_w1, L0_conv_router_b1, L0_conv_router_w2, L0_conv_router_b2, L0_conv_expert_w, L0_conv_expert_gn_gamma, L0_conv_expert_gn_beta, L0_conv_shared_w, L0_conv_shared_gn_gamma, L0_conv_shared_gn_beta)
    t = _to_tokens(x)
    t = t + _L0_ffn_ref(_ln_t(t), L0_ffn_router_w, L0_ffn_w1, L0_ffn_w2, L0_ffn_w3)
    x = _from_tokens(t, x)
    x = x + _L1_conv_ref(_ln_c(x), L1_conv_w1, L1_conv_b1, L1_conv_w2, L1_conv_b2)
    t = _to_tokens(x)
    t = t + _L1_ffn_ref(_ln_t(t), L1_ffn_gate_w, L1_ffn_gate_b, L1_ffn_w1, L1_ffn_b1, L1_ffn_w2, L1_ffn_b2)
    x = _from_tokens(t, x)
    return x

_drawn_inputs = setup_inputs


def setup_inputs(seed=0):
    import zlib

    import numpy as np

    out = dict(_drawn_inputs(seed))
    spreads = {'L0_conv_router_b1': (0.0, 0.8),
     'L0_conv_router_b2': (0.0, 0.1),
     'L0_conv_expert_gn_gamma': (1.0, 0.2),
     'L0_conv_expert_gn_beta': (0.0, 0.1),
     'L0_conv_shared_gn_gamma': (1.0, 0.2),
     'L0_conv_shared_gn_beta': (0.0, 0.1),
     'L1_conv_b1': (0.0, 0.267),
     'L1_conv_b2': (0.0, 0.1),
     'L1_ffn_gate_b': (0.0, 0.1),
     'L1_ffn_b1': (0.0, 0.8),
     'L1_ffn_b2': (0.0, 0.655)}
    factors = {'L0_conv_router_w1': 25.439, 'L0_conv_router_w2': 8.0, 'L1_conv_w1': 8.0}
    for name, (base, spread) in spreads.items():
        noise = np.random.default_rng([zlib.crc32(name.encode()), seed]).standard_normal(out[name].shape)
        drawn = base * np.exp(spread * noise) if base else spread * noise
        out[name] = jnp.asarray(drawn.astype(out[name].dtype))
    for name, factor in factors.items():
        out[name] = (out[name] * factor).astype(out[name].dtype)
    return out
```

```python
from contextlib import ExitStack

import numpy as np

import concourse.bass as bass
from concourse import mybir

F32 = mybir.dt.float32
F16 = mybir.dt.float16
BF16 = mybir.dt.bfloat16
I32 = mybir.dt.int32
ALU = mybir.AluOpType
ACT = mybir.ActivationFunctionType
AX_X = mybir.AxisListType.X

P = 128
IMAGES, C, H, W = 16, 128, 32, 32
PIX = H * W
TPI = PIX // P
TOKENS = IMAGES * PIX
NT = TOKENS // P
HP, WP = H + 2, W + 2
TAPS = 9
EC = 4
E = 8
HID0, HID0P = 341, 384
NJ0 = HID0P // P
HID1 = 512
NJ1 = HID1 // P
CAP = -(-5 * TOKENS // (4 * E))
TILE = 512
QT = TILE // P
ROW = 132
REG = TOKENS + TILE
SLOTS = E * REG + TILE
TILES0 = 2 * TOKENS // TILE + E
TILES1 = TOKENS // TILE + E
FILL_ID = 65536.0
FLT_MAX = 3.4028234663852886e38
PER_A = 288
PER_C = 98
GN_GROUP = 16
MAGIC = float(0x5F3759DF)
SA, SS, S1, S3, S2, D1, D2 = range(7)
NS = 7


class Img:

    def __init__(self, q, k, per=2):
        self.b = q * per + k
        self.h = q * (per // 2) + k // 2
        self.u = k % 2
        self.v = k % 4
        self.w = q + k // 4
        self.q, self.k, self.per = q, k, per

    def __add__(self, d):
        return Img(self.q, self.k + d, self.per)


def some(value):
    return not isinstance(value, int) or value > 0


def upto(value, last):
    return min(value, last) if isinstance(value, int) else value


def sweep(eng, n, step, line=None, count=0, per=2):
    for t in range(-1, per):
        step(Img(t // per, t % per, per))
    if line:
        line.enter(count)
    with eng.Fori(1, n // per - 1) as q:
        if line:
            line.next_pass(q - 1)
        for k in range(per):
            step(Img(q, k, per))
        if line:
            line.end_pass()
    if line:
        line.leave(n // per - 2)
    for t in range(n - per, n + 2):
        step(Img(t // per, t % per, per))


def live(i, n):
    return not isinstance(i.b, int) or 0 <= i.b < n


class Line:

    def __init__(self):
        self.base, self.n = 0, 0

    def step(self):
        self.n += 1
        return self.base + self.n

    def enter(self, per):
        self.start, self.per = self.base + self.n, per

    def next_pass(self, done):
        self.base, self.n = done * self.per + self.start, 0

    def end_pass(self):
        assert self.n == self.per, f"a pass has {self.n} steps"

    def leave(self, passes):
        self.base, self.n = self.start + passes * self.per, 0


def bcast(ap, n):
    return ap.unsqueeze(2).to_broadcast([ap.shape[0], ap.shape[1], n])


def build(nc, a, out):
    slots = nc.dram_tensor("slot_rows", (SLOTS, ROW), F32, kind="Internal").ap()
    back0 = nc.dram_tensor("ffn0_rows", (2 * TOKENS, C), F32, kind="Internal").ap()
    parked = nc.dram_tensor("conv1_weights", (P, (1 + TAPS) * P), F32, kind="Internal").ap()
    back1 = nc.dram_tensor("ffn1_rows", (TOKENS, C), F32, kind="Internal").ap()

    ctx = ExitStack()
    with ctx:
        def sb(name, shape, dt=F32):
            return ctx.enter_context(nc.sbuf_tensor(name, shape, dt))

        sems = {}

        def apart(eng):
            eng.sem_inc(sem("passed_waits"), 1)

        def sem(name):
            if name not in sems:
                sems[name] = ctx.enter_context(nc.semaphore(name))
            return sems[name]

        tokens = sb("tokens", [P, NT, C])
        wa_h = sb("wa_h", [P, EC * TAPS * P], F16)
        wa_l = sb("wa_l", [P, EC * TAPS * P], F16)
        ws_h = sb("ws_h", [P, P], F16)
        ws_l = sb("ws_l", [P, P], F16)
        wb1_h = sb("wb1_h", [P, E * HID0P], F16)
        wb1_l = sb("wb1_l", [P, E * HID0P], F16)
        wb3_h = sb("wb3_h", [P, E * HID0P], F16)
        wb3_l = sb("wb3_l", [P, E * HID0P], F16)
        wb2_h = sb("wb2_h", [P, E * NJ0 * C], F16)
        wb2_l = sb("wb2_l", [P, E * NJ0 * C], F16)
        wd1_h = sb("wd1_h", [P, E * HID1], F16)
        wd1_l = sb("wd1_l", [P, E * HID1], F16)
        wd2_h = sb("wd2_h", [P, E * NJ1 * C], F16)
        wd2_l = sb("wd2_l", [P, E * NJ1 * C], F16)
        work = sb("work", [P, 11800])
        small = sb("small", [P, 2800])

        def carve(tensor):
            used = [0]

            def take(shape, dt=F32):
                n = -(-int(np.prod(shape)) * (2 if dt in (F16, BF16) else 4) // 4)
                ap = tensor[:, used[0]:used[0] + n]
                used[0] += n
                assert used[0] <= tensor.shape[1], (used[0], tensor.shape)
                if dt != F32:
                    ap = ap.bitcast(dt)
                if len(shape) == 2:
                    ap = ap.rearrange("p (a b) -> p a b", a=shape[0])
                elif len(shape) == 3:
                    ap = ap.rearrange("p (a b c) -> p a b c", a=shape[0], b=shape[1])
                return ap
            return take

        t = carve(small)
        ident = t([P])
        upper = t([P], BF16)
        ones = t([P], BF16)
        ones_f = t([P])
        group = t([P])
        fill = t([QT, ROW])
        vecs = t([67])
        w2r = t([EC])
        b2r = t([1, EC])
        b1r = t([1])
        gate1_w = t([E])
        gate1_b = t([1, E])
        b2_taps = t([TAPS])
        desc8 = t([TPI, E])
        first_slot = t([TPI, E])
        desc4 = t([1, EC])
        iota_i = t([TILES0])
        iota_j = t([33])
        iota_t = t([TPI])
        mx = t([NS])
        scale = t([2 * NS])
        spread = t([2 * NS])
        neg_sq = t([2])
        y0_scale = t([1])
        y1_scale = t([1])
        gam = t([2, EC + 1])
        b1s = t([E * NJ1])
        pool = t([2, 1])
        h8 = t([2, 1])
        hb = t([2, P])
        sel = t([2, 2, 4])
        eidx = t([2, 2], I32)
        gst = t([2, 6])
        me2 = t([2, 2])
        gg = t([2])
        gv = t([1])
        gr = t([1])
        gt = t([1])
        gsb = t([2, 2])
        r4 = [t([1, EC]) for _ in range(8)]
        s4 = [t([1]) for _ in range(8)]
        st8 = t([TPI, 6])
        mv8 = t([TPI, 2])
        vv8 = t([TPI])
        rs8 = t([TPI])
        tt8 = t([TPI])
        r8 = [t([TPI, E]) for _ in range(8)]
        s8 = [t([TPI]) for _ in range(10)]
        mask = t([TPI, E], BF16)
        msum = t([E])
        msum16 = t([E], BF16)
        idf = t([TPI])
        slot_i = t([2, TPI], I32)
        hg = t([1])
        wd = t([TAPS])
        tab_i = t([2, TILES0], I32)
        tail_i = t([E], I32)

        tA = carve(work)
        ntm = tA([TPI, C])
        nT = ntm.rearrange("p t c -> p (t c)")
        rows = [tA([TPI, ROW]) for _ in range(2)]
        shared_end = P * TPI + 2 * TPI * ROW
        xcm = [tA([PIX]) for _ in range(2)]
        pad_h = [tA([HP, WP], F16) for _ in range(2)]
        pad_l = [tA([HP, WP], F16) for _ in range(2)]
        act_o = [tA([PIX]) for _ in range(2)]
        acc = [tA([PIX]) for _ in range(2)]

        tC = carve(work)
        tC([shared_end])
        ya = [tC([TPI, C]) for _ in range(2)]
        yb = [tC([TPI, C]) for _ in range(2)]
        vpad = [tC([HP, WP]) for _ in range(2)]
        diag = tC([TAPS, P])
        cacc = tC([PIX])

        tB = carve(work)
        xt = [tB([QT, ROW]) for _ in range(2)]
        xh = [tB([TILE], F16) for _ in range(2)]
        xl = [tB([TILE], F16) for _ in range(2)]
        sg = [tB([TILE]) for _ in range(2)]
        g32 = [tB([TILE]) for _ in range(4)]
        gh = [tB([NJ1, TILE], F16) for _ in range(2)]
        gl = [tB([NJ1, TILE], F16) for _ in range(2)]
        ysb = tB([TILE])
        yt = [tB([QT, C]) for _ in range(2)]
        idg = [tB([QT, 2]) for _ in range(4)]
        tT = carve(gl[0].rearrange("p j c -> p (j c)").bitcast(F32))
        b_big = tT([TILES0, E])
        b_thr = tT([E, 33])
        tT = carve(gl[1].rearrange("p j c -> p (j c)").bitcast(F32))
        b_one = [tT([TILES0]) for _ in range(4)]
        b_e = [tT([E]) for _ in range(4)]

        tF = carve(work)
        zf = [tF([PIX]) for _ in range(2)]
        rep = tF([PIX])
        nn = tF([PIX])
        finite = tF([PIX], I32)
        ocm = [tF([PIX]) for _ in range(2)]
        osum = [tF([PIX]) for _ in range(2)]

        tN = carve(tokens[:, :, :].rearrange("p a b -> p (a b)"))
        nat_a = tN([EC, C * TAPS])
        nat_s = tN([C])
        nat_b1 = tN([E, NJ0, C])
        nat_b3 = tN([E, NJ0, C])
        nat_b2 = tN([E, HID0P])
        nat_v = tN([P])
        nat_c1 = tN([P])
        nat_c2 = tN([TAPS, P])
        nat_r2 = tN([8])
        tD = carve(work)
        nat_d1 = tD([E, HID1])
        nat_d2 = tD([E, NJ1, C])
        cw_stage = tD([(1 + TAPS) * P])
        cw = wa_h[:, 0:2 * (1 + TAPS) * P].bitcast(F32)
        VEC = dict(eg=0, eb=4, sg=8, sb=9, cb1=10, fb2=11, rw0=19, rw1=27, fb1=35, end=67)

        def vec(name, i=0, n=1):
            return vecs[:, VEC[name] + i:VEC[name] + i + n]

        psum = ctx.enter_context(nc.psum_tensor("banks", [P, 8, 512], F32))
        tp = psum[:, 0:2, :].rearrange("p a b -> p (a b)")
        tp_tok = tp.rearrange("p (t c) -> p t c", t=TPI)
        pair = [psum[:, 2:4, :].rearrange("p a b -> p (a b)"), psum[:, 4:6, :].rearrange("p a b -> p (a b)")]
        sm_a = psum[:, 6, :]
        sm_b = psum[:, 7, :]

        block = ctx.enter_context(nc.Block())

        groups = []
        taps_of = nat_a.rearrange("p e (c k) -> p e k c", k=TAPS)
        blocks = [taps_of[:, e, k, :] for e in range(EC) for k in range(TAPS)]
        for g in range(EC * TAPS // 4):
            groups.append((blocks[4 * g:4 * g + 4], SA, wa_h[:, g * 512:(g + 1) * 512], wa_l[:, g * 512:(g + 1) * 512]))
        groups.append(([nat_s], SS, ws_h[:, :], ws_l[:, :]))
        for nat, s, hi, lo in ((nat_b1, S1, wb1_h, wb1_l), (nat_b3, S3, wb3_h, wb3_l)):
            blocks = [nat[:, e, j, :] for e in range(E) for j in range(NJ0)]
            for g in range(E * NJ0 // 4):
                groups.append((blocks[4 * g:4 * g + 4], s, hi[:, g * 512:(g + 1) * 512], lo[:, g * 512:(g + 1) * 512]))
        blocks = [nat_b2[:, e, j * P:(j + 1) * P] for e in range(E) for j in range(NJ0)]
        for g in range(E * NJ0 // 4):
            groups.append((blocks[4 * g:4 * g + 4], S2, wb2_h[:, g * 512:(g + 1) * 512], wb2_l[:, g * 512:(g + 1) * 512]))
        plain = [([nat_c1] + [nat_c2[:, k, :] for k in range(3)], cw_stage[:, 0:512]),
                 ([nat_c2[:, k, :] for k in range(3, 7)], cw_stage[:, 512:1024]),
                 ([nat_c2[:, k, :] for k in range(7, 9)], cw_stage[:, 1024:1280])]
        NG = len(groups)
        NPL = len(plain)
        LOADS = 35

        @block.sync
        def _(sp):
            sp.wait_ge(sem("stage_zeroed"), 4)
            n = 0

            def load(dst, src, slow=False):
                nonlocal n
                n += 1
                sp.dma_start(dst, src, allow_slow_non_contiguous=slow).then_inc(sem("setup_loaded"), 16)

            load(nat_a, a["L0_conv_expert_w"].rearrange("e o c y x -> o e (c y x)"))
            load(nat_s, a["L0_conv_shared_w"])
            for nat, name in ((nat_b1, "L0_ffn_w1"), (nat_b3, "L0_ffn_w3")):
                for j in range(2):
                    load(nat[:, :, j, :], a[name][:, j * P:(j + 1) * P, :].rearrange("e h c -> h e c"))
                load(nat[0:HID0 - 2 * P, :, 2, :], a[name][:, 2 * P:HID0, :].rearrange("e h c -> h e c"))
            load(nat_b2[:, :, 0:HID0], a["L0_ffn_w2"].rearrange("e c h -> c e h"))
            load(nat_c1, a["L1_conv_w1"])
            load(nat_c2, a["L1_conv_w2"].rearrange("(c k) j -> c k j", k=TAPS))
            load(nat_v[0:4, :], a["L0_conv_expert_gn_gamma"])
            load(nat_v[4:8, :], a["L0_conv_expert_gn_beta"])
            load(nat_v[8:9, :], a["L0_conv_shared_gn_gamma"].unsqueeze(0))
            load(nat_v[9:10, :], a["L0_conv_shared_gn_beta"].unsqueeze(0))
            load(nat_v[10:11, :], a["L1_conv_b1"].unsqueeze(0))
            load(nat_v[11:19, :], a["L1_ffn_b2"])
            load(nat_v[19:27, :], a["L0_ffn_router_w"])
            load(nat_v[27:35, :], a["L0_conv_router_w1"])
            load(nat_v[35:67, :], a["L1_ffn_b1"].rearrange("e (j p) -> (e j) p", p=P))
            load(nat_r2[0:EC, :], a["L0_conv_router_w2"])
            load(b1r[0:8, :], a["L0_conv_router_b1"].unsqueeze(1), slow=True)
            load(b2r[:, 0, :], a["L0_conv_router_b2"].unsqueeze(0).to_broadcast([P, EC]))
            load(gate1_w, a["L1_ffn_gate_w"])
            load(gate1_b[:, 0, :], a["L1_ffn_gate_b"].unsqueeze(0).to_broadcast([P, E]))
            load(b2_taps, a["L1_conv_b2"].rearrange("(c k) -> c k", k=TAPS))
            load(nat_d1, a["L1_ffn_w1"].rearrange("e c f -> c e f"))
            for e in range(E):
                load(nat_d2[:, e, :, :], a["L1_ffn_w2"][e].rearrange("(j p) c -> p j c", p=P))
            assert n == LOADS, n

            sp.wait_ge(sem("fill_ready"), 1)
            for i in range(TOKENS // TILE):
                sp.dma_start(back1[i * TILE:(i + 1) * TILE, :].rearrange("(q p) c -> p q c", p=P),
                             fill[:, :, 0:C]).then_inc(sem("zeroed"), 16)
            sp.dma_start(slots[E * REG:SLOTS, :].rearrange("(q p) c -> p q c", p=P), fill).then_inc(sem("zeroed"), 16)

            sp.wait_ge(sem("plain_copied"), NPL)
            sp.dma_start(parked, cw_stage).then_inc(sem("parked"), 16)
            sp.wait_ge(sem("parked"), 16)
            sp.wait_ge(sem("setup_done"), 1)
            x_img = a["x"].rearrange("b c h w -> b c (h w)")
            for b in range(2):
                sp.dma_start(xcm[b], x_img[b]).then_inc(sem(f"x_loaded{b}"), 16)
            with sp.Fori(1, IMAGES // 2) as q:
                for u in range(2):
                    if some(q * 2 + u - 1):
                        sp.wait_ge(sem("A_residual_read"), q * 2 + u - 1)
                    sp.dma_start(xcm[u], x_img[bass.ds(q * 2 + u, 1)].rearrange("b c n -> (b c) n")).then_inc(sem(f"x_loaded{u}"), 16)

            def tile_loads(p, n, before, choices):
                sp.wait_ge(sem(p + "table_ready"), 1)
                for e in range(E):
                    at_slot = sp.value_load(tail_i[0:1, e:e + 1], min_val=0, max_val=SLOTS - TILE)
                    sp.dma_start(slots[bass.ds(at_slot, TILE), :].rearrange("(q p) c -> p q c", p=P),
                                 fill).then_inc(sem(p + "tails"), 16)
                sp.wait_ge(sem(p + "tails"), 16 * E)
                sp.wait_ge(sem("zeroed"), 16 * (TOKENS // TILE + 1))
                if some(16 * choices * NT):
                    sp.wait_ge(sem(before + "scattered_rows"), 16 * choices * NT)

                def load_tile(i):
                    if some(i.b * 2 - 2):
                        sp.wait_ge(sem(p + "ids_copied"), i.b * 2 - 2)
                    apart(sp)
                    if some(i.b - 1):
                        sp.wait_ge(sem(p + "xt_done"), i.b - 1)
                    apart(sp)
                    row = sp.value_load(tab_i[0:1, 0, bass.ds(i.b, 1)], min_val=0, max_val=SLOTS - TILE)
                    sp.dma_start(xt[i.u], slots[bass.ds(row, TILE), :].rearrange("(q p) c -> p q c", p=P)).then_inc(sem(f"{p}xt_loaded{i.u}"), 16)

                for k in range(2):
                    load_tile(Img(0, k))
                with sp.Fori(1, n // 2) as q:
                    for k in range(2):
                        load_tile(Img(q, k))

            sp.wait_ge(sem("A_conv_done"), 3 * IMAGES)
            sp.dma_start(cw, parked).then_inc(sem("cw_loaded"), 16)

            tile_loads("B_", TILES0, "A_", 2)

            for v in range(4):
                sp.wait_ge(sem(f"B_scattered{v}"), 16 * QT * TILES0 // 4)

            def load_rows(i):
                if some(i.b - 1):
                    sp.wait_ge(sem("C_added"), i.b - 1)
                for k, dst in ((0, ya), (1, yb)):
                    src = back0[bass.ds(i.b * PIX + k * TOKENS, PIX), :]
                    sp.dma_start(dst[i.u], src.rearrange("(t p) c -> p t c", p=P)).then_inc(sem(f"C_rows_loaded{i.u}"), 16)

            for k in range(2):
                load_rows(Img(0, k))
            with sp.Fori(1, IMAGES // 2) as q:
                for k in range(2):
                    load_rows(Img(q, k))

            tile_loads("D_", TILES1, "C_", 1)

            for v in range(4):
                sp.wait_ge(sem(f"D_scattered{v}"), 16 * QT * TILES1 // 4)
            out_img = out.rearrange("b c h w -> b c (h w)")

            def final(i):
                nxt = i
                if live(nxt, IMAGES):
                    if some(nxt.b - 1):
                        sp.wait_ge(sem("F_added"), nxt.b - 1)
                    src = back1[bass.ds(nxt.b * PIX, PIX), :]
                    sp.dma_start(zf[nxt.u].rearrange("p (t c) -> p t c", t=TPI),
                                 src.rearrange("(t p) c -> p t c", p=P)).then_inc(sem(f"F_loaded{nxt.u}"), 16)
                old = i + (-2)
                if live(old, IMAGES):
                    sp.wait_ge(sem("F_out_ready"), old.b + 1)
                    dst = out_img[bass.ds(old.b, 1)].rearrange("b c n -> (b c) n")
                    sp.dma_start(dst, ocm[old.u]).then_inc(sem(f"F_stored{old.u}"), 16)

            sweep(sp, IMAGES, final)
            for u in range(2):
                sp.wait_ge(sem(f"F_stored{u}"), 16 * IMAGES // 2)

        @block.gpsimd
        def _(pool_e):
            line = Line()
            for nat in (nat_b1, nat_b3):
                pool_e.memset(nat[:, :, 2, :], 0.0).then_inc(sem("stage_zeroed"), 1)
            pool_e.memset(nat_b2[:, :, HID0:HID0P], 0.0).then_inc(sem("stage_zeroed"), 1)
            pool_e.memset(nat_v, 0.0).then_inc(sem("stage_zeroed"), 1)
            pool_e.memset(fill, 0.0).then_inc(sem("pool_steps"), 1)
            pool_e.wait_ge(sem("pool_steps"), line.step())
            pool_e.memset(fill[:, :, C:C + 1], FILL_ID).then_inc(sem("fill_ready"), 1)
            pool_e.memset(ident, 0.0).then_inc(sem("pool_steps"), 1)
            pool_e.wait_ge(sem("pool_steps"), line.step())
            pool_e.affine_select(out=ident, in_=ident, compare_op=ALU.not_equal, fill=1.0, base=0,
                                 pattern=[[-1, P]], channel_multiplier=1).then_inc(sem("pool_steps"), 1)
            pool_e.wait_ge(sem("pool_steps"), line.step())
            pool_e.memset(ones, 1.0).then_inc(sem("const_ready"), 1)
            pool_e.memset(ones_f, 1.0).then_inc(sem("pool_steps"), 1)
            pool_e.wait_ge(sem("pool_steps"), line.step())
            pool_e.affine_select(out=upper, in_=ones_f, compare_op=ALU.is_gt, fill=0.0, base=0,
                                 pattern=[[1, P]], channel_multiplier=-1).then_inc(sem("const_ready"), 1)
            pool_e.memset(group, 1.0 / GN_GROUP).then_inc(sem("pool_steps"), 1)
            pool_e.wait_ge(sem("pool_steps"), line.step())
            pattern = [[-GN_GROUP, P // GN_GROUP], [0, GN_GROUP]]
            pool_e.affine_select(out=group, in_=group, compare_op=ALU.is_ge, fill=0.0, base=0,
                                 pattern=pattern, channel_multiplier=1).then_inc(sem("pool_steps"), 1)
            pool_e.wait_ge(sem("pool_steps"), line.step())
            pattern = [[GN_GROUP, P // GN_GROUP], [0, GN_GROUP]]
            pool_e.affine_select(out=group, in_=group, compare_op=ALU.is_ge, fill=0.0, base=GN_GROUP - 1,
                                 pattern=pattern, channel_multiplier=-1).then_inc(sem("const_ready"), 1)
            for dst, pattern, base, mult in (
                    (desc8, [[0, TPI], [-1, E]], E, 0), (first_slot, [[0, TPI], [REG // 2, E]], 0, 0),
                    (desc4, [[0, 1], [-1, EC]], EC, 0), (iota_i, [[1, TILES0]], 0, 0),
                    (iota_j, [[TILE, 33]], 0, 0), (iota_t, [[P, TPI]], 0, 1)):
                pool_e.iota(dst, pattern=pattern, base=base, channel_multiplier=mult,
                            allow_small_or_imprecise_dtypes=True).then_inc(sem("const_ready"), 1)
            pool_e.wait_ge(sem("setup_done"), 1)
            for x in (*pad_h, *pad_l):
                pool_e.memset(x, 0.0).then_inc(sem("pads_zeroed"), 1)

            def scatters(p, i, choices):
                if not live(i, IMAGES):
                    return
                pool_e.wait_ge(sem(p + "slots_known"), i.b + 1)
                if choices == 2:
                    pool_e.wait_ge(sem(p + "rows2_ready"), i.b + 1)
                apart(pool_e)
                for k in range(choices):
                    for tt in range(TPI):
                        pool_e.indirect_dma_start(
                            slots, bass.IndirectOffsetOnAxis(ap=slot_i[:, k, tt:tt + 1], axis=0),
                            rows[k][:, tt, :], None, bounds_check=SLOTS - 1, oob_is_err=False
                        ).then_inc(sem(p + "scattered_rows"), 16)

            def tile_step(p, i, n, dst, limit):
                if live(i, n):
                    pool_e.wait_ge(sem(f"{p}xt_loaded{i.u}"), i.h * 16 + 16)
                    apart(pool_e)
                    if some(i.w):
                        pool_e.wait_ge(sem(f"{p}scattered{i.v}"), i.w * (16 * QT))
                    apart(pool_e)
                    pool_e.tensor_copy(idg[i.v][:, :, 0:1].bitcast(I32), xt[i.u][:, :, C:C + 1]).then_inc(sem(p + "ids_copied"), 1)
                    pool_e.tensor_copy(idg[i.v][:, :, 1:2], xt[i.u][:, :, C + 1:C + 2]).then_inc(sem(p + "ids_copied"), 1)
                old = i + (-2)
                if live(old, n):
                    pool_e.wait_ge(sem(p + "ids_copied"), old.b * 2 + 2)
                    pool_e.wait_ge(sem(p + "yt_ready"), old.b + 1)
                    apart(pool_e)
                    for qq in range(QT):
                        pool_e.indirect_dma_start(
                            dst, bass.IndirectOffsetOnAxis(ap=idg[old.v][:, qq, 0:1].bitcast(I32), axis=0),
                            yt[old.u][:, qq, :], None, bounds_check=limit - 1, oob_is_err=False
                        ).then_inc(sem(f"{p}scattered{old.v}"), 16)

            sweep(pool_e, IMAGES, lambda i: scatters("A_", i + (-1), 2))
            sweep(pool_e, TILES0, lambda i: tile_step("B_", i, TILES0, back0, 2 * TOKENS), per=4)

            def c_step(i):
                nxt = i + 1
                if live(nxt, IMAGES):
                    pool_e.wait_ge(sem(f"C_rows_loaded{nxt.u}"), nxt.h * 32 + 32)
                    pool_e.tensor_tensor(ya[nxt.u], ya[nxt.u], yb[nxt.u], ALU.add).then_inc(sem("C_y_summed"), 1)
                    pool_e.wait_ge(sem("C_inside"), nxt.b + 1)
                    apart(pool_e)
                    v = vpad[nxt.u]
                    pool_e.tensor_copy(v[:, 0:1, 1:W + 1], v[:, 2:3, 1:W + 1]).then_inc(sem("C_border_rows"), 1)
                    pool_e.tensor_copy(v[:, H + 1:H + 2, 1:W + 1], v[:, H - 1:H, 1:W + 1]).then_inc(sem("C_border_rows"), 1)
                    pool_e.wait_ge(sem("C_border_rows"), nxt.b * 2 + 2)
                    apart(pool_e)
                    pool_e.tensor_copy(v[:, :, 0:1], v[:, :, 2:3]).then_inc(sem("C_border_done"), 1)
                    pool_e.tensor_copy(v[:, :, W + 1:W + 2], v[:, :, W - 1:W]).then_inc(sem("C_border_done"), 1)
                scatters("C_", i + (-1), 1)

            sweep(pool_e, IMAGES, c_step)
            sweep(pool_e, TILES1, lambda i: tile_step("D_", i, TILES1, back1, TOKENS), per=4)

        @block.tensor
        def _(pe):
            pe.wait_ge(sem("pool_steps"), 6)
            pe.wait_ge(sem("const_ready"), 3)
            pe.wait_ge(sem("setup_loaded"), 16 * LOADS)
            pe.transpose(sm_a[:, 0:VEC["end"]], nat_v[0:VEC["end"], :], ident[0:VEC["end"], 0:VEC["end"]])
            pe.transpose(sm_a[0:8, 128:128 + EC], nat_r2[0:EC, :], ident[0:EC, 0:EC]).then_inc(sem("vecs_done"), 1)
            for g, (ins, _) in enumerate(plain):
                for j, x in enumerate(ins):
                    ins_ = pe.transpose(psum[:, g, j * P:(j + 1) * P], x, ident)
                ins_.then_inc(sem("plain_done"), 1)
            pe.wait_ge(sem("max_found"), 1)
            pe.transpose(sm_b[0:NS, 0:P], mx, ident).then_inc(sem("max_turned"), 1)
            pe.wait_ge(sem("spread_ready"), 1)
            pe.matmul(sm_b[:, 128:128 + 2 * NS], ones_f[0:NS, :], spread[0:NS, :], start=True, stop=True).then_inc(sem("scale_done"), 1)
            for g, (ins, _, _, _) in enumerate(groups):
                if g < NPL:
                    pe.wait_ge(sem("plain_copied"), g + 1)
                if some(g - 5):
                    pe.wait_ge(sem("group_split"), g - 5)
                for j, x in enumerate(ins):
                    ins_ = pe.transpose(psum[:, g % 6, j * P:(j + 1) * P], x, ident)
                ins_.then_inc(sem("group_done"), 1)
            pe.wait_ge(sem("group_split"), NG)
            pe.wait_ge(sem("setup_done"), 1)

            def turn(dst, blocks):
                for tt, x in enumerate(blocks):
                    last = pe.transpose(dst[:, tt * P:(tt + 1) * P], x, ident)
                return last

            def three(dst, wh, wl, nh, nl, start, stop):
                pe.matmul(dst, wh, nh, start=start, stop=False)
                pe.matmul(dst, wh, nl, start=False, stop=False)
                return pe.matmul(dst, wl, nh, start=False, stop=stop)

            def route_turn(p, i):
                pe.wait_ge(sem(p + "rows_ready"), i.b + 1)
                turn(tp, [rows[0][:, tt, 0:C] for tt in range(TPI)]).then_inc(sem(p + "nT_done"), 1)

            def logits(p, i, w):
                pe.wait_ge(sem(p + "nT_copied"), i.b + 1)
                if some(i.b):
                    pe.wait_ge(sem(p + "slots_known"), i.b)
                for tt in range(TPI):
                    last = pe.matmul(sm_b[:, tt * E:(tt + 1) * E], nT[:, tt * P:(tt + 1) * P], w, start=True, stop=True)
                last.then_inc(sem(p + "logits_done"), 1)

            def positions(p, i):
                pe.wait_ge(sem(p + "mask_ready"), i.b + 1)
                pos = sm_b[:, 64:64 + TPI * E]
                m = mask.rearrange("p t e -> p (t e)")
                pe.matmul(pos, upper, m, start=True, stop=False)
                for tt in range(TPI - 1):
                    later = mask[:, tt:tt + 1, :].to_broadcast([P, TPI - 1 - tt, E])
                    pe.matmul(pos[:, (tt + 1) * E:].rearrange("p (t e) -> p t e", e=E), ones, later, start=False, stop=False)
                before = msum16.unsqueeze(1).to_broadcast([P, TPI, E])
                pe.matmul(pos.rearrange("p (t e) -> p t e", e=E), ones, before, start=False, stop=True).then_inc(sem(p + "pos_done"), 1)

            def group_mean(i, j):
                n = i.b * 3 + j
                pe.wait_ge(sem("A_gstat"), n + 1)
                if some(n):
                    pe.wait_ge(sem("A_gsb"), n)
                pe.matmul(sm_a[:, 0:2], group, me2[:, (i.u + j) % 2, :], start=True, stop=True).then_inc(sem("A_gn_done"), 1)

            def conv_half(i, j, half, regs):
                dst = pair[(i.u + j) % 2][:, half * 512:(half + 1) * 512]
                h0 = half * (H // 2)
                if j == 0:
                    rhs = [x[i.u][:, h0 + 1:h0 + 1 + H // 2, 1:1 + W] for x in (pad_h, pad_l)]
                    return three(dst, ws_h[:, :], ws_l[:, :], *rhs, True, True)
                e = regs[j - 1]
                for k in range(TAPS):
                    dy, dx = k // 3, k % 3
                    rhs = [x[i.u][:, h0 + dy:h0 + dy + H // 2, dx:dx + W] for x in (pad_h, pad_l)]
                    ws = [x[:, bass.ds(e * (TAPS * P) + k * P, P)] for x in (wa_h, wa_l)]
                    last = three(dst, *ws, *rhs, k == 0, k == TAPS - 1)
                return last

            def a_step(i):
                old, nxt = i + (-1), i + 1
                regs = []
                if live(i, IMAGES):
                    pe.wait_ge(sem("A_padl_done"), i.b + 1)
                    if some(i.b * 3 - 1):
                        pe.wait_ge(sem("A_silu"), i.b * 3 - 1)
                    conv_half(i, 0, 0, regs)
                    conv_half(i, 0, 1, regs).then_inc(sem("A_conv_done"), 1)
                if live(nxt, IMAGES):
                    pe.wait_ge(sem(f"x_loaded{nxt.u}"), nxt.h * 16 + 16)
                    if some(nxt.b - 2):
                        pe.wait_ge(sem("A_nT_copied"), nxt.b - 2)
                    turn(tp, [xcm[nxt.u][:, tt * P:(tt + 1) * P] for tt in range(TPI)]).then_inc(sem("A_xt_done"), 1)
                if live(old, IMAGES):
                    if live(i, IMAGES):
                        pe.wait_ge(sem("A_r2_read"), i.b + 1)
                    group_mean(old, 2)
                if live(i, IMAGES):
                    pe.wait_ge(sem("A_gate_ready"), i.b + 1)
                    apart(pe)
                    regs += [pe.value_load(eidx[0:1, i.u, k:k + 1], min_val=0, max_val=EC - 1) for k in range(2)]
                    if some(i.b * 3):
                        pe.wait_ge(sem("A_silu"), i.b * 3)
                    conv_half(i, 1, 0, regs)
                    group_mean(i, 0)
                if live(old, IMAGES):
                    pe.wait_ge(sem("A_acc"), old.b * 3 + 3)
                    pe.wait_ge(sem("A_ntm"), upto(old.b + 3, IMAGES))
                    turn(tp, [acc[old.u][:, tt * P:(tt + 1) * P] for tt in range(TPI)]).then_inc(sem("A_tok_done"), 1)
                if live(i, IMAGES):
                    conv_half(i, 1, 1, regs).then_inc(sem("A_conv_done"), 1)
                if live(nxt, IMAGES):
                    pe.wait_ge(sem("A_ntm"), nxt.b + 1)
                    if some(nxt.b - 1):
                        pe.wait_ge(sem("A_tok_copied"), nxt.b - 1)
                    turn(tp, [ntm[:, tt, :] for tt in range(TPI)]).then_inc(sem("A_cm_done"), 1)
                if live(i, IMAGES):
                    pe.wait_ge(sem("A_silu"), i.b * 3 + 1)
                    conv_half(i, 2, 0, regs)
                    group_mean(i, 1)
                if live(old, IMAGES):
                    pe.wait_ge(sem("A_padl_done"), upto(old.b + 3, IMAGES))
                    route_turn("A_", old)
                if live(nxt, IMAGES):
                    pe.wait_ge(sem("A_padh_done"), nxt.b + 1)
                    if some(nxt.b * 3 - 1):
                        pe.wait_ge(sem("A_gsb"), nxt.b * 3 - 1)
                    pe.matmul(sm_a[0:8, 8:9], vec("rw1", 0, 8), pool[:, nxt.u, :], start=True, stop=True).then_inc(sem("A_r1_done"), 1)
                if live(i, IMAGES):
                    conv_half(i, 2, 1, regs).then_inc(sem("A_conv_done"), 1)
                if live(old, IMAGES):
                    logits("A_", old, vec("rw0", 0, E))
                if live(nxt, IMAGES):
                    pe.wait_ge(sem("A_hb"), nxt.b + 1)
                    pe.matmul(sm_a[:, 16:16 + EC], hb[0:8, nxt.u, :], w2r[0:8, :], start=True, stop=True).then_inc(sem("A_r2_done"), 1)
                if live(old, IMAGES):
                    positions("A_", old)

            sweep(pe, IMAGES, a_step)

            def counts(p):
                pe.wait_ge(sem(p + "msum"), IMAGES)
                pe.matmul(sm_a[:, 32:32 + E], ones, msum16, start=True, stop=True).then_inc(sem(p + "counts_done"), 1)

            def ffn(p, n, nj, gated, w1, w3, w2):
                tbank = [psum[:, 0, :], psum[:, 1, :]]
                ybank, ytbank = psum[:, 6, :], psum[:, 7, :]
                nb = 2 if gated else 4

                def up(i, j, e):
                    c = i.b * nj + j
                    m = (i.u * nj + j) % nb
                    if some(c + 1 - nb):
                        pe.wait_ge(sem(p + ("g_done" if gated else "up_read")), c + 1 - nb)
                    dst = psum[:, 2 + 2 * m, :] if gated else psum[:, 2 + m, :]
                    ws = [x[:, bass.ds(e * (nj * P) + j * P, P)] for x in w1]
                    last = three(dst, *ws, xh[i.u], xl[i.u], True, True)
                    if gated:
                        ws = [x[:, bass.ds(e * (nj * P) + j * P, P)] for x in w3]
                        last = three(psum[:, 3 + 2 * m, :], *ws, xh[i.u], xl[i.u], True, True)
                    last.then_inc(sem(p + "up_done"), 1)

                def step(i):
                    nxt, old, older = i + 1, i + (-1), i + (-2)
                    if live(nxt, n):
                        pe.wait_ge(sem(f"{p}xt_loaded{nxt.u}"), nxt.h * 16 + 16)
                        if some(nxt.b - 1):
                            pe.wait_ge(sem(p + "xl_done"), nxt.b - 1)
                        turn(tbank[nxt.u], [xt[nxt.u][:, qq, 0:C] for qq in range(QT)]).then_inc(sem(p + "xt_done"), 1)
                    if live(i, n):
                        e = pe.value_load(tab_i[0:1, 1, bass.ds(i.b, 1)], min_val=0, max_val=E - 1)
                        pe.wait_ge(sem(p + "xl_done"), i.b + 1)
                        up(i, 0, e)
                    if live(older, n):
                        pe.wait_ge(sem(p + "y_copied"), older.b + 1)
                        if some(older.b):
                            pe.wait_ge(sem(p + "yt_ready"), older.b)
                        turn(ytbank, [ysb[:, qq * P:(qq + 1) * P] for qq in range(QT)]).then_inc(sem(p + "yt_done"), 1)
                    if live(i, n):
                        for j in range(1, nj):
                            up(i, j, e)
                    if live(old, n):
                        f = pe.value_load(tab_i[0:1, 1, bass.ds(old.b, 1)], min_val=0, max_val=E - 1)
                        pe.wait_ge(sem(p + "gl_done"), (old.b + 1) * nj)
                        if some(old.b):
                            pe.wait_ge(sem(p + "y_copied"), old.b)
                        for j in range(nj):
                            ws = [x[:, bass.ds(f * (nj * C) + j * C, C)] for x in w2]
                            last = three(ybank, *ws, gh[old.u][:, j, :], gl[old.u][:, j, :], j == 0, j == nj - 1)
                        last.then_inc(sem(p + "y_done"), 1)

                pe.wait_ge(sem(p + "table_ready"), 1)
                sweep(pe, n, step, per=4)

            counts("A_")
            ffn("B_", TILES0, NJ0, True, (wb1_h, wb1_l), (wb3_h, wb3_l), (wb2_h, wb2_l))

            def tap_half(i, half):
                h0 = half * (H // 2)
                for k in range(TAPS):
                    dy, dx = k // 3, k % 3
                    last = pe.matmul(pair[i.u][:, half * 512:(half + 1) * 512], diag[:, k, :],
                                     vpad[i.u][:, h0 + dy:h0 + dy + H // 2, dx:dx + W],
                                     start=(k == 0), stop=(k == TAPS - 1))
                return last

            def c_step(i):
                old, nxt = i + (-1), i + 1
                if live(old, IMAGES):
                    pe.wait_ge(sem("C_conv_copied"), old.b + 1)
                    if some(old.b):
                        pe.wait_ge(sem("C_nT_copied"), old.b)
                    turn(tp, [cacc[:, tt * P:(tt + 1) * P] for tt in range(TPI)]).then_inc(sem("C_tok_done"), 1)
                if live(nxt, IMAGES):
                    pe.wait_ge(sem("C_ntm"), nxt.b + 1)
                    if some(nxt.b - 1):
                        pe.wait_ge(sem("C_tok_added"), nxt.b - 1)
                    turn(tp, [ntm[:, tt, :] for tt in range(TPI)]).then_inc(sem("C_cm_done"), 1)
                if live(i, IMAGES):
                    pe.wait_ge(sem("C_diag"), i.b + 1)
                    pe.wait_ge(sem("C_border_done"), i.b * 2 + 2)
                    if some(i.b - 1):
                        pe.wait_ge(sem("C_conv_copied"), i.b - 1)
                    tap_half(i, 0)
                if live(old, IMAGES):
                    pe.wait_ge(sem("C_inside"), upto(old.b + 3, IMAGES))
                    route_turn("C_", old)
                if live(nxt, IMAGES):
                    pe.wait_ge(sem("C_inside"), nxt.b + 1)
                    if some(nxt.b):
                        pe.wait_ge(sem("C_wd_read"), nxt.b)
                    pe.matmul(sm_a[:, 0:1], cw[:, 0:P], pool[:, nxt.u, :], start=True, stop=True).then_inc(sem("C_h_done"), 1)
                if live(i, IMAGES):
                    tap_half(i, 1).then_inc(sem("C_conv_done"), 1)
                if live(old, IMAGES):
                    logits("C_", old, gate1_w)
                if live(nxt, IMAGES):
                    pe.wait_ge(sem("C_gelu"), nxt.b + 1)
                    for k in range(TAPS):
                        last = pe.matmul(sm_a[:, 8 + k:9 + k], cw[:, (1 + k) * P:(2 + k) * P], hg, start=True, stop=True)
                    last.then_inc(sem("C_wd_done"), 1)
                if live(old, IMAGES):
                    positions("C_", old)

            pe.wait_ge(sem("cw_loaded"), 16)
            sweep(pe, IMAGES, c_step)
            counts("C_")
            ffn("D_", TILES1, NJ1, False, (wd1_h, wd1_l), None, (wd2_h, wd2_l))

            def f_step(i):
                if live(i, IMAGES):
                    pe.wait_ge(sem("F_added"), i.b + 1)
                    if some(i.b - 1):
                        pe.wait_ge(sem("F_out_ready"), i.b - 1)
                    turn(pair[i.u], [osum[i.u][:, tt * P:(tt + 1) * P] for tt in range(TPI)]).then_inc(sem("F_turned"), 1)

            sweep(pe, IMAGES, f_step)

        @block.scalar
        def _(act):
            act.wait_ge(sem("vecs_done"), 1)
            act.activation(vecs, sm_a[:, 0:VEC["end"]], ACT.Copy)
            act.activation(w2r[0:8, :], sm_a[0:8, 128:128 + EC], ACT.Copy).then_inc(sem("vecs_ready"), 1)
            for g, (ins, dst) in enumerate(plain):
                act.wait_ge(sem("plain_done"), g + 1)
                act.activation(dst, psum[:, g, 0:len(ins) * P], ACT.Copy).then_inc(sem("plain_copied"), 1)
            act.wait_ge(sem("scale_ready"), 1)
            for nat, s, hi in ((nat_d1.rearrange("p e f -> p (e f)"), D1, wd1_h), (nat_d2.rearrange("p e j c -> p (e j c)"), D2, wd2_h)):
                act.activation(hi[:, :], nat, ACT.Copy, scale=scale[:, NS + s:NS + s + 1]).then_inc(sem("direct_hi"), 1)
            for g, (ins, s, hi, _) in enumerate(groups):
                act.wait_ge(sem("group_done"), g + 1)
                act.activation(hi, psum[:, g % 6, 0:len(ins) * P], ACT.Copy, scale=scale[:, NS + s:NS + s + 1]).then_inc(sem("group_hi"), 1)

            def route_copy(p, i, choices):
                if choices == 2:
                    act.wait_ge(sem(p + "rows_ready"), i.b + 1)
                    act.activation(rows[1][:, :, 0:C], rows[0][:, :, 0:C], ACT.Copy).then_inc(sem(p + "rows2_ready"), 1)
                act.wait_ge(sem(p + "nT_done"), i.b + 1)
                act.activation(nT, tp, ACT.Copy).then_inc(sem(p + "nT_copied"), 1)

            def route_exp(p, i):
                act.wait_ge(sem(p + "shifted"), i.b + 1)
                act.activation(r8[1], r8[0], ACT.Exp).then_inc(sem(p + "exped"), 1)

            def a_silu(i, j):
                n = i.b * 3 + j
                act.wait_ge(sem("A_gsb"), n + 1)
                if some(n - 1):
                    act.wait_ge(sem("A_acc"), n - 1)
                par = (i.u + j) % 2
                act.activation(act_o[par], pair[par], ACT.Silu, scale=gsb[:, par, 0:1], bias=gsb[:, par, 1:2]).then_inc(sem("A_silu"), 1)

            def a_step(i):
                old, nxt = i + (-1), i + 1
                if live(old, IMAGES):
                    a_silu(old, 2)
                if live(i, IMAGES):
                    a_silu(i, 0)
                if live(old, IMAGES):
                    act.wait_ge(sem("A_tok_done"), old.b + 1)
                    dst = tokens[:, bass.ds(old.b * TPI, TPI), :]
                    act.activation(dst, tp_tok, ACT.Copy).then_inc(sem("A_tok_copied"), 1)
                if live(nxt, IMAGES):
                    act.wait_ge(sem("A_cm_done"), nxt.b + 1)
                    if some(nxt.b * 3 - 3):
                        act.wait_ge(sem("A_conv_done"), nxt.b * 3 - 3)
                    if not isinstance(nxt.b, int) or nxt.b < 2:
                        act.wait_ge(sem("pads_zeroed"), 4)
                    act.activation(pad_h[nxt.u][:, 1:H + 1, 1:W + 1], tp.rearrange("p (h w) -> p h w", h=H), ACT.Copy,
                                   accum_out=pool[:, nxt.u, :]).then_inc(sem("A_padh_done"), 1)
                if live(old, IMAGES):
                    route_copy("A_", old, 2)
                if live(i, IMAGES):
                    a_silu(i, 1)
                if live(nxt, IMAGES):
                    act.wait_ge(sem("A_r1_done"), nxt.b + 1)
                    act.activation(h8[0:8, nxt.u, :], sm_a[0:8, 8:9], ACT.Silu, scale=1.0 / PIX, bias=b1r[0:8, :]).then_inc(sem("A_h8"), 1)
                if live(old, IMAGES):
                    route_exp("A_", old)
                if live(nxt, IMAGES):
                    act.wait_ge(sem("A_gshift"), nxt.b + 1)
                    act.activation(r4[1], r4[0], ACT.Exp).then_inc(sem("A_gexp"), 1)

            sweep(act, IMAGES, a_step)

            def ffn(p, n, nj, gated, out_scale):
                nb = 2 if gated else 4

                def step(i):
                    nxt, old, older = i + 1, i + (-1), i + (-2)
                    if live(older, n):
                        act.wait_ge(sem(p + "y_done"), older.b + 1)
                        if some(older.b):
                            act.wait_ge(sem(p + "yt_done"), older.b)
                        if gated:
                            act.activation(ysb, psum[:, 6, :], ACT.Copy, scale=out_scale).then_inc(sem(p + "y_copied"), 1)
                        else:
                            apart(act)
                            f = act.value_load(tab_i[0:1, 1, bass.ds(older.b, 1)], min_val=0, max_val=E - 1)
                            act.activation(ysb, psum[:, 6, :], ACT.Identity, scale=out_scale,
                                           bias=vecs[:, bass.ds(f + VEC["fb2"], 1)]).then_inc(sem(p + "y_copied"), 1)
                    if live(nxt, n):
                        act.wait_ge(sem(p + "xt_done"), nxt.b + 1)
                        if some((nxt.b - 1) * nj):
                            act.wait_ge(sem(p + "up_done"), (nxt.b - 1) * nj)
                        act.activation(xh[nxt.u], psum[:, nxt.u, :], ACT.Copy).then_inc(sem(p + "xh_done"), 1)
                    if live(i, n):
                        if not gated:
                            e = act.value_load(tab_i[0:1, 1, bass.ds(i.b, 1)], min_val=0, max_val=E - 1)
                        for j in range(nj):
                            c = i.b * nj + j
                            m = (i.u * nj + j) % nb
                            act.wait_ge(sem(p + "up_done"), c + 1)
                            if gated:
                                if some(c - 1):
                                    act.wait_ge(sem(p + "g_done"), c - 1)
                                act.activation(sg[m], psum[:, 2 + 2 * m, :], ACT.Silu, scale=scale[:, S1:S1 + 1]).then_inc(sem(p + "silu"), 1)
                                if j:
                                    high(i, j - 1, c - 1)
                            else:
                                if some(c + 1 - nj):
                                    act.wait_ge(sem(p + "gl_done"), c + 1 - nj)
                                act.activation(g32[j], psum[:, 2 + m, :], ACT.Relu,
                                               bias=b1s[:, bass.ds(e * nj + j, 1)]).then_inc(sem(p + "up_read"), 1)
                        if gated:
                            high(i, nj - 1, i.b * nj + nj - 1)

                def high(i, j, c):
                    act.wait_ge(sem(p + "g_done"), c + 1)
                    if some(i.b - 1):
                        act.wait_ge(sem(p + "y_done"), i.b - 1)
                    act.activation(gh[i.u][:, j, :], g32[j], ACT.Copy).then_inc(sem(p + "gh_done"), 1)

                sweep(act, n, step, per=4)

            ffn("B_", TILES0, NJ0, True, y0_scale)

            def c_step(i):
                old, nxt = i + (-1), i + 1
                if live(nxt, IMAGES):
                    act.wait_ge(sem("C_cm_done"), nxt.b + 1)
                    if some(nxt.b - 1):
                        act.wait_ge(sem("C_conv_done"), nxt.b - 1)
                    act.activation(vpad[nxt.u][:, 1:H + 1, 1:W + 1], tp.rearrange("p (h w) -> p h w", h=H), ACT.Copy,
                                   accum_out=pool[:, nxt.u, :]).then_inc(sem("C_inside"), 1)
                if live(old, IMAGES):
                    route_copy("C_", old, 1)
                if live(nxt, IMAGES):
                    act.wait_ge(sem("C_h_done"), nxt.b + 1)
                    act.activation(hg, sm_a[:, 0:1], ACT.Gelu, scale=1.0 / PIX, bias=vec("cb1")).then_inc(sem("C_gelu"), 1)
                if live(i, IMAGES):
                    act.wait_ge(sem("C_conv_done"), i.b + 1)
                    if some(i.b):
                        act.wait_ge(sem("C_tok_done"), i.b)
                    act.activation(cacc, pair[i.u], ACT.Copy).then_inc(sem("C_conv_copied"), 1)
                if live(old, IMAGES):
                    route_exp("C_", old)

            sweep(act, IMAGES, c_step)
            ffn("D_", TILES1, NJ1, False, y1_scale)

            def f_step(i):
                if live(i, IMAGES):
                    act.wait_ge(sem("F_turned"), i.b + 1)
                    if some(i.h * 16):
                        act.wait_ge(sem(f"F_stored{i.u}"), i.h * 16)
                    act.activation(ocm[i.u], pair[i.u], ACT.Copy).then_inc(sem("F_out_ready"), 1)

            sweep(act, IMAGES, f_step)

        @block.vector
        def _(dve):
            L = Line()

            def rsqrt(r, v, tmp):
                dve.tensor_scalar(r.bitcast(I32), v.bitcast(I32), -0.5, MAGIC, ALU.mult, ALU.add).then_inc(sem("dve_steps"), 1)
                dve.wait_ge(sem("dve_steps"), L.step())
                for _ in range(3):
                    dve.scalar_tensor_tensor(out=tmp, in0=r, scalar=-0.5, in1=r, op0=ALU.mult, op1=ALU.mult).then_inc(sem("dve_steps"), 1)
                    dve.wait_ge(sem("dve_steps"), L.step())
                    dve.tensor_tensor(tmp, tmp, v, ALU.mult).then_inc(sem("dve_steps"), 1)
                    dve.wait_ge(sem("dve_steps"), L.step())
                    dve.scalar_tensor_tensor(out=r, in0=tmp, scalar=1.5, in1=r, op0=ALU.add, op1=ALU.mult).then_inc(sem("dve_steps"), 1)
                    dve.wait_ge(sem("dve_steps"), L.step())

            dve.wait_ge(sem("setup_loaded"), 16 * LOADS)
            dve.wait_ge(sem("stage_zeroed"), 4)
            dve.wait_ge(sem("vecs_ready"), 1)
            for col, x in ((SA, nat_a), (SS, nat_s), (S1, nat_b1), (S3, nat_b3), (S2, nat_b2), (D1, nat_d1), (D2, nat_d2)):
                x = x if len(x.shape) == 2 else x.rearrange("p a b -> p (a b)") if len(x.shape) == 3 else x.rearrange("p a b c -> p (a b c)")
                dve.tensor_reduce(mx[:, col:col + 1], x, AX_X, ALU.max, apply_absolute_value=True).then_inc(sem("dve_steps"), 1)
                dve.wait_ge(sem("dve_steps"), L.step())
            dve.tensor_reduce(gt, vec("fb1", 0, 32), AX_X, ALU.max, apply_absolute_value=True).then_inc(sem("dve_steps"), 1)
            dve.wait_ge(sem("dve_steps"), L.step())
            dve.tensor_tensor(mx[:, D1:D1 + 1], mx[:, D1:D1 + 1], gt, ALU.max).then_inc(sem("max_found"), 1)
            dve.wait_ge(sem("max_turned"), 1)
            m = gv[0:NS, :]
            mi = m.bitcast(I32)
            sc, si = gg[0:NS, 0:1], gg[0:NS, 1:2]
            dve.reduce_max(m, sm_b[0:NS, 0:P], AX_X).then_inc(sem("dve_steps"), 1)
            dve.wait_ge(sem("dve_steps"), L.step())
            dve.tensor_scalar(m, m, 1e-30, None, ALU.max).then_inc(sem("dve_steps"), 1)
            dve.wait_ge(sem("dve_steps"), L.step())
            dve.tensor_scalar(mi, mi, 0x7F800000, None, ALU.bitwise_and).then_inc(sem("dve_steps"), 1)
            dve.wait_ge(sem("dve_steps"), L.step())
            dve.tensor_scalar(sc, m, 2.0, None, ALU.mult).then_inc(sem("dve_steps"), 1)
            dve.wait_ge(sem("dve_steps"), L.step())
            dve.tensor_scalar(si.bitcast(I32), sc.bitcast(I32), -1.0, float(0x7F000000), ALU.mult, ALU.add).then_inc(sem("dve_steps"), 1)
            dve.wait_ge(sem("dve_steps"), L.step())
            dve.tensor_scalar(spread[0:NS, 0:NS], ident[0:NS, 0:NS], sc, None, ALU.mult).then_inc(sem("dve_steps"), 1)
            dve.wait_ge(sem("dve_steps"), L.step())
            dve.tensor_scalar(spread[0:NS, NS:2 * NS], ident[0:NS, 0:NS], si, None, ALU.mult).then_inc(sem("spread_ready"), 1)
            dve.wait_ge(sem("scale_done"), 1)
            dve.tensor_copy(scale, sm_b[:, 128:128 + 2 * NS]).then_inc(sem("scale_ready"), 1)
            dve.wait_ge(sem("scale_ready"), 1)

            def s_(c):
                return scale[:, c:c + 1]

            for n, c in enumerate((SA, SS)):
                dve.scalar_tensor_tensor(out=neg_sq[:, n:n + 1], in0=s_(c), scalar=-1.0, in1=s_(c), op0=ALU.mult, op1=ALU.mult).then_inc(sem("dve_steps"), 1)
                dve.wait_ge(sem("dve_steps"), L.step())
            dve.tensor_tensor(y0_scale, s_(S1), s_(S3), ALU.mult).then_inc(sem("dve_steps"), 1)
            dve.wait_ge(sem("dve_steps"), L.step())
            dve.tensor_tensor(y0_scale, y0_scale, s_(S2), ALU.mult).then_inc(sem("dve_steps"), 1)
            dve.wait_ge(sem("dve_steps"), L.step())
            dve.tensor_tensor(y1_scale, s_(D1), s_(D2), ALU.mult).then_inc(sem("dve_steps"), 1)
            dve.wait_ge(sem("dve_steps"), L.step())
            dve.tensor_scalar(gam[:, 0, 0:EC], vec("eg", 0, EC), s_(SA), None, ALU.mult).then_inc(sem("dve_steps"), 1)
            dve.wait_ge(sem("dve_steps"), L.step())
            dve.tensor_scalar(gam[:, 0, EC:EC + 1], vec("sg"), s_(SS), None, ALU.mult).then_inc(sem("dve_steps"), 1)
            dve.wait_ge(sem("dve_steps"), L.step())
            dve.tensor_scalar(gam[:, 1, :], gam[:, 0, :], -1.0, None, ALU.mult).then_inc(sem("dve_steps"), 1)
            dve.wait_ge(sem("dve_steps"), L.step())
            dve.tensor_scalar(b1s, vec("fb1", 0, E * NJ1), scale[:, NS + D1:NS + D1 + 1], None, ALU.mult).then_inc(sem("dve_steps"), 1)
            dve.wait_ge(sem("dve_steps"), L.step())
            dve.wait_ge(sem("const_ready"), 9)
            dve.tensor_scalar(first_slot, first_slot, 2.0, None, ALU.mult).then_inc(sem("dve_steps"), 1)
            dve.wait_ge(sem("dve_steps"), L.step())
            dve.memset(msum, 0.0).then_inc(sem("dve_steps"), 1)
            dve.wait_ge(sem("dve_steps"), L.step())
            dve.memset(msum16, 0.0).then_inc(sem("dve_steps"), 1)
            dve.wait_ge(sem("dve_steps"), L.step())
            dve.tensor_copy(idf, iota_t).then_inc(sem("dve_steps"), 1)
            dve.wait_ge(sem("dve_steps"), L.step())
            for n, (nat, s, hi, lo) in enumerate(((nat_d1.rearrange("p e f -> p (e f)"), D1, wd1_h, wd1_l),
                                                  (nat_d2.rearrange("p e j c -> p (e j c)"), D2, wd2_h, wd2_l))):
                dve.wait_ge(sem("direct_hi"), n + 1)
                dve.scalar_tensor_tensor(out=lo[:, :], in0=nat, scalar=scale[:, NS + s:NS + s + 1], in1=hi[:, :], op0=ALU.mult, op1=ALU.subtract).then_inc(sem("dve_steps"), 1)
                dve.wait_ge(sem("dve_steps"), L.step())
            for g, (ins, s, hi, lo) in enumerate(groups):
                dve.wait_ge(sem("group_hi"), g + 1)
                dve.scalar_tensor_tensor(out=lo, in0=psum[:, g % 6, 0:len(ins) * P], scalar=scale[:, NS + s:NS + s + 1],
                                         in1=hi, op0=ALU.mult, op1=ALU.subtract).then_inc(sem("group_split"), 1)
            dve.wait_ge(sem("group_split"), NG)
            dve.wait_ge(sem("plain_copied"), NPL)
            dve.sem_inc(sem("setup_done"), 1)

            def token_stats(x, eps):
                apart(dve)
                for tt in range(TPI):
                    last = dve.bn_stats(st8[:, tt, :], x(tt))
                last.then_inc(sem("dve_steps"), 1)
                dve.wait_ge(sem("dve_steps"), L.step())
                apart(dve)
                for tt in range(TPI):
                    last = dve.bn_aggr(mv8[:, tt, :], st8[:, tt, :])
                last.then_inc(sem("dve_steps"), 1)
                dve.wait_ge(sem("dve_steps"), L.step())
                dve.tensor_scalar(vv8, mv8[:, :, 1], eps, None, ALU.add).then_inc(sem("dve_steps"), 1)
                dve.wait_ge(sem("dve_steps"), L.step())
                rsqrt(rs8, vv8, tt8)

            def top(view, width, desc, tmp, hot, best, first):
                dve.tensor_reduce(best, view, AX_X, ALU.max).then_inc(sem("dve_steps"), 1)
                dve.wait_ge(sem("dve_steps"), L.step())
                dve.tensor_tensor(tmp, view, bcast(best, width), ALU.is_equal).then_inc(sem("dve_steps"), 1)
                dve.wait_ge(sem("dve_steps"), L.step())
                dve.tensor_tensor(tmp, tmp, desc, ALU.mult).then_inc(sem("dve_steps"), 1)
                dve.wait_ge(sem("dve_steps"), L.step())
                dve.tensor_reduce(first, tmp, AX_X, ALU.max).then_inc(sem("dve_steps"), 1)
                dve.wait_ge(sem("dve_steps"), L.step())
                dve.tensor_tensor(hot, tmp, bcast(first, width), ALU.is_equal).then_inc(sem("dve_steps"), 1)
                dve.wait_ge(sem("dve_steps"), L.step())

            def route_rows(p, i, choices):
                dve.wait_ge(sem("A_tok_copied" if p == "A_" else "C_tok_added"), i.b + 1)
                base = i.b * TPI
                tok = lambda tt: tokens[:, bass.ds(base + tt, 1), :].rearrange("p a c -> p (a c)")
                token_stats(tok, 1e-5)
                if some(i.b * (16 * TPI * choices)):
                    dve.wait_ge(sem(p + "scattered_rows"), i.b * (16 * TPI * choices))
                for tt in range(TPI):
                    last = dve.tensor_scalar(rows[0][:, tt, 0:C], tok(tt), mv8[:, tt, 0:1], rs8[:, tt:tt + 1], ALU.subtract, ALU.mult)
                last.then_inc(sem(p + "rows_ready"), 1)

            def route_choose(p, i, choices):
                lg = sm_b[:, 0:TPI * E].rearrange("p (t e) -> p t e", e=E)
                dve.wait_ge(sem(p + "logits_done"), i.b + 1)
                if choices == 1:
                    dve.tensor_tensor(r8[0], lg, gate1_b.to_broadcast([P, TPI, E]), ALU.add).then_inc(sem("dve_steps"), 1)
                    dve.wait_ge(sem("dve_steps"), L.step())
                    lg = r8[0]
                dve.tensor_reduce(s8[0], lg, AX_X, ALU.max).then_inc(sem("dve_steps"), 1)
                dve.wait_ge(sem("dve_steps"), L.step())
                dve.tensor_tensor(r8[0], lg, bcast(s8[0], E), ALU.subtract).then_inc(sem(p + "shifted"), 1)
                dve.wait_ge(sem(p + "exped"), i.b + 1)
                dve.tensor_reduce(s8[1], r8[1], AX_X, ALU.add).then_inc(sem("dve_steps"), 1)
                dve.wait_ge(sem("dve_steps"), L.step())
                dve.reciprocal(s8[2], s8[1]).then_inc(sem("dve_steps"), 1)
                dve.wait_ge(sem("dve_steps"), L.step())
                dve.tensor_tensor(r8[2], r8[1], bcast(s8[2], E), ALU.mult).then_inc(sem("dve_steps"), 1)
                dve.wait_ge(sem("dve_steps"), L.step())
                top(r8[2], E, desc8, r8[3], r8[4], s8[3], s8[4])
                hots, bests = [r8[4]], [s8[3]]
                if choices == 2:
                    dve.scalar_tensor_tensor(out=r8[5], in0=r8[4], scalar=-2.0, in1=r8[2], op0=ALU.mult, op1=ALU.add).then_inc(sem("dve_steps"), 1)
                    dve.wait_ge(sem("dve_steps"), L.step())
                    top(r8[5], E, desc8, r8[3], r8[6], s8[5], s8[6])
                    hots, bests = [r8[4], r8[6]], [s8[3], s8[5]]
                if choices == 2:
                    dve.tensor_tensor(mask, r8[4], r8[6], ALU.add).then_inc(sem(p + "mask_ready"), 1)
                else:
                    dve.tensor_copy(mask, r8[4]).then_inc(sem(p + "mask_ready"), 1)
                if choices == 2:
                    dve.tensor_tensor(s8[7], bests[0], bests[1], ALU.add).then_inc(sem("dve_steps"), 1)
                    dve.wait_ge(sem("dve_steps"), L.step())
                    dve.tensor_scalar(s8[7], s8[7], 1e-9, None, ALU.add).then_inc(sem("dve_steps"), 1)
                    dve.wait_ge(sem("dve_steps"), L.step())
                    dve.reciprocal(s8[8], s8[7]).then_inc(sem("dve_steps"), 1)
                    dve.wait_ge(sem("dve_steps"), L.step())
                    dve.wait_ge(sem(p + "rows2_ready"), i.b + 1)
                for k in range(choices):
                    dve.tensor_scalar(rows[k][:, :, C], idf, float(k * TOKENS), None, ALU.add).then_inc(sem("dve_steps"), 1)
                    dve.wait_ge(sem("dve_steps"), L.step())
                    if choices == 2:
                        dve.tensor_tensor(rows[k][:, :, C + 1], bests[k], s8[8], ALU.mult).then_inc(sem("dve_steps"), 1)
                        dve.wait_ge(sem("dve_steps"), L.step())
                    else:
                        dve.tensor_copy(rows[k][:, :, C + 1], bests[k]).then_inc(sem("dve_steps"), 1)
                        dve.wait_ge(sem("dve_steps"), L.step())
                    if isinstance(i.b, int) and i.b == 0:
                        dve.memset(rows[k][:, :, C + 2:ROW], 0.0).then_inc(sem("dve_steps"), 1)
                        dve.wait_ge(sem("dve_steps"), L.step())
                dve.tensor_scalar(idf, idf, float(PIX), None, ALU.add).then_inc(sem("dve_steps"), 1)
                dve.wait_ge(sem("dve_steps"), L.step())
                dve.wait_ge(sem(p + "pos_done"), i.b + 1)
                pos = sm_b[:, 64:64 + TPI * E].rearrange("p (t e) -> p t e", e=E)
                dve.tensor_reduce(s8[9], mask.rearrange("p t e -> p e t"), AX_X, ALU.add).then_inc(sem("dve_steps"), 1)
                dve.wait_ge(sem("dve_steps"), L.step())
                dve.tensor_tensor(msum, msum, s8[9], ALU.add).then_inc(sem("dve_steps"), 1)
                dve.wait_ge(sem("dve_steps"), L.step())
                dve.tensor_copy(msum16, msum).then_inc(sem(p + "msum"), 1)
                dve.wait_ge(sem(p + "msum"), i.b + 1)
                dve.tensor_tensor(r8[7], pos, first_slot, ALU.add).then_inc(sem("dve_steps"), 1)
                dve.wait_ge(sem("dve_steps"), L.step())
                for k in range(choices):
                    dve.tensor_tensor(r8[3], r8[7], hots[k], ALU.mult).then_inc(sem("dve_steps"), 1)
                    dve.wait_ge(sem("dve_steps"), L.step())
                    dve.tensor_reduce(s8[4], r8[3], AX_X, ALU.add).then_inc(sem("dve_steps"), 1)
                    dve.wait_ge(sem("dve_steps"), L.step())
                    if choices == 1:
                        dve.tensor_tensor(r8[3], pos, hots[k], ALU.mult).then_inc(sem("dve_steps"), 1)
                        dve.wait_ge(sem("dve_steps"), L.step())
                        dve.tensor_reduce(s8[5], r8[3], AX_X, ALU.add).then_inc(sem("dve_steps"), 1)
                        dve.wait_ge(sem("dve_steps"), L.step())
                        dve.tensor_scalar(s8[5], s8[5], float(CAP), float(2 * SLOTS), ALU.is_ge, ALU.mult).then_inc(sem("dve_steps"), 1)
                        dve.wait_ge(sem("dve_steps"), L.step())
                        dve.tensor_tensor(s8[4], s8[4], s8[5], ALU.add).then_inc(sem("dve_steps"), 1)
                        dve.wait_ge(sem("dve_steps"), L.step())
                    last = dve.tensor_copy(slot_i[:, k, :], s8[4])
                    if k < choices - 1:
                        last.then_inc(sem("dve_steps"), 1)
                        dve.wait_ge(sem("dve_steps"), L.step())
                last.then_inc(sem(p + "slots_known"), 1)
                dve.wait_ge(sem(p + "slots_known"), i.b + 1)

            def group_stats(i, j):
                par = (i.u + j) % 2
                dve.wait_ge(sem("A_conv_done"), i.b * 3 + j + 1)
                dve.bn_stats(gst[:, 0, :], pair[par][:, 0:512])
                dve.bn_stats(gst[:, 1, :], pair[par][:, 512:1024]).then_inc(sem("dve_steps"), 1)
                dve.wait_ge(sem("dve_steps"), L.step())
                apart(dve)
                dve.bn_aggr(me2[:, par, :], gst.rearrange("p a b -> p (a b)")).then_inc(sem("dve_steps"), 1)
                dve.wait_ge(sem("dve_steps"), L.step())
                m = me2[:, par, 0:1]
                dve.scalar_tensor_tensor(out=me2[:, par, 1:2], in0=m, scalar=m, in1=me2[:, par, 1:2],
                                         op0=ALU.mult, op1=ALU.add).then_inc(sem("A_gstat"), 1)

            def group_affine(i, j):
                n = i.b * 3 + j
                par = (i.u + j) % 2
                dve.wait_ge(sem("A_gn_done"), n + 1)
                if j == 0:
                    gs, ngs, beta = gam[:, 0, EC:EC + 1], gam[:, 1, EC:EC + 1], vec("sb")
                else:
                    gs, ngs, beta = (sel[:, i.u, j - 1, c:c + 1] for c in range(3))
                dve.tensor_copy(gg, sm_a[:, 0:2]).then_inc(sem("dve_steps"), 1)
                dve.wait_ge(sem("dve_steps"), L.step())
                dve.scalar_tensor_tensor(out=gv, in0=gg[:, 0:1], scalar=gg[:, 0:1], in1=gg[:, 1:2], op0=ALU.mult, op1=ALU.subtract).then_inc(sem("dve_steps"), 1)
                dve.wait_ge(sem("dve_steps"), L.step())
                dve.tensor_scalar(gv, gv, neg_sq[:, (0 if j else 1):(1 if j else 2)], 1e-5, ALU.mult, ALU.add).then_inc(sem("dve_steps"), 1)
                dve.wait_ge(sem("dve_steps"), L.step())
                rsqrt(gr, gv, gt)
                dve.tensor_tensor(gsb[:, par, 0:1], gr, gs, ALU.mult).then_inc(sem("dve_steps"), 1)
                dve.wait_ge(sem("dve_steps"), L.step())
                dve.tensor_tensor(gt, gr, ngs, ALU.mult).then_inc(sem("dve_steps"), 1)
                dve.wait_ge(sem("dve_steps"), L.step())
                dve.scalar_tensor_tensor(out=gsb[:, par, 1:2], in0=gg[:, 0:1], scalar=gt, in1=beta,
                                         op0=ALU.mult, op1=ALU.add).then_inc(sem("A_gsb"), 1)

            def accumulate(i, j):
                n = i.b * 3 + j
                par = (i.u + j) % 2
                dve.wait_ge(sem("A_silu"), n + 1)
                if j == 0:
                    if some(i.b - 1):
                        dve.wait_ge(sem("A_tok_done"), i.b - 1)
                    dve.tensor_tensor(acc[i.u], act_o[par], xcm[i.u], ALU.add).then_inc(sem("A_acc"), 1)
                    dve.wait_ge(sem("A_acc"), n + 1)
                    dve.sem_inc(sem("A_residual_read"), 1)
                else:
                    dve.scalar_tensor_tensor(out=acc[i.u], in0=act_o[par], scalar=sel[:, i.u, j - 1, 3:4], in1=acc[i.u],
                                             op0=ALU.mult, op1=ALU.add).then_inc(sem("A_acc"), 1)
                    dve.wait_ge(sem("A_acc"), n + 1)

            def a_gates(i):
                dve.wait_ge(sem("A_r2_done"), i.b + 1)
                dve.tensor_tensor(r4[2], sm_a[:, 16:16 + EC].unsqueeze(1), b2r, ALU.add).then_inc(sem("dve_steps"), 1)
                dve.wait_ge(sem("dve_steps"), L.step())
                dve.sem_inc(sem("A_r2_read"), 1)
                dve.tensor_reduce(s4[0], r4[2], AX_X, ALU.max).then_inc(sem("dve_steps"), 1)
                dve.wait_ge(sem("dve_steps"), L.step())
                dve.tensor_tensor(r4[0], r4[2], bcast(s4[0], EC), ALU.subtract).then_inc(sem("A_gshift"), 1)
                dve.wait_ge(sem("A_gexp"), i.b + 1)
                dve.tensor_reduce(s4[1], r4[1], AX_X, ALU.add).then_inc(sem("dve_steps"), 1)
                dve.wait_ge(sem("dve_steps"), L.step())
                dve.reciprocal(s4[2], s4[1]).then_inc(sem("dve_steps"), 1)
                dve.wait_ge(sem("dve_steps"), L.step())
                dve.tensor_tensor(r4[3], r4[1], bcast(s4[2], EC), ALU.mult).then_inc(sem("dve_steps"), 1)
                dve.wait_ge(sem("dve_steps"), L.step())
                top(r4[3], EC, desc4, r4[4], r4[5], s4[3], s4[4])
                dve.scalar_tensor_tensor(out=r4[6], in0=r4[5], scalar=-2.0, in1=r4[3], op0=ALU.mult, op1=ALU.add).then_inc(sem("dve_steps"), 1)
                dve.wait_ge(sem("dve_steps"), L.step())
                top(r4[6], EC, desc4, r4[4], r4[7], s4[5], s4[6])
                dve.tensor_tensor(s4[7], s4[3], s4[5], ALU.add).then_inc(sem("dve_steps"), 1)
                dve.wait_ge(sem("dve_steps"), L.step())
                dve.reciprocal(s4[7], s4[7]).then_inc(sem("dve_steps"), 1)
                dve.wait_ge(sem("dve_steps"), L.step())
                for k, (hot, best, first) in enumerate(((r4[5], s4[3], s4[4]), (r4[7], s4[5], s4[6]))):
                    dve.tensor_tensor(best, best, s4[7], ALU.mult).then_inc(sem("dve_steps"), 1)
                    dve.wait_ge(sem("dve_steps"), L.step())
                    dve.scalar_tensor_tensor(out=sel[:, i.u, k, 3:4], in0=best, scalar=0.01, in1=best, op0=ALU.is_ge, op1=ALU.mult).then_inc(sem("dve_steps"), 1)
                    dve.wait_ge(sem("dve_steps"), L.step())
                    for c, table in enumerate((gam[:, 0, 0:EC], gam[:, 1, 0:EC], vec("eb", 0, EC))):
                        dve.tensor_tensor(r4[4], hot, table.unsqueeze(1), ALU.mult).then_inc(sem("dve_steps"), 1)
                        dve.wait_ge(sem("dve_steps"), L.step())
                        dve.tensor_reduce(sel[:, i.u, k, c:c + 1], r4[4], AX_X, ALU.add).then_inc(sem("dve_steps"), 1)
                        dve.wait_ge(sem("dve_steps"), L.step())
                    dve.tensor_scalar(eidx[:, i.u, k:k + 1], first, -1.0, float(EC), ALU.mult, ALU.add).then_inc(sem("dve_steps"), 1)
                    dve.wait_ge(sem("dve_steps"), L.step())
                dve.sem_inc(sem("A_gate_ready"), 1)

            def a_step(i):
                old, nxt = i + (-1), i + 1
                if live(old, IMAGES):
                    group_stats(old, 2)
                if live(i, IMAGES):
                    group_stats(i, 0)
                if live(nxt, IMAGES):
                    dve.wait_ge(sem("A_xt_done"), nxt.b + 1)
                    token_stats(lambda tt: tp_tok[:, tt, :], 1e-6)
                    for tt in range(TPI):
                        last = dve.tensor_scalar(ntm[:, tt, :], tp_tok[:, tt, :], mv8[:, tt, 0:1], rs8[:, tt:tt + 1], ALU.subtract, ALU.mult)
                    last.then_inc(sem("A_ntm"), 1)
                if live(old, IMAGES):
                    group_affine(old, 2)
                    accumulate(old, 2)
                if live(i, IMAGES):
                    group_affine(i, 0)
                    accumulate(i, 0)
                if live(nxt, IMAGES):
                    dve.wait_ge(sem("A_padh_done"), nxt.b + 1)
                    inside = [x[nxt.u][:, 1:H + 1, 1:W + 1] for x in (pad_h, pad_l)]
                    dve.tensor_tensor(inside[1], tp.rearrange("p (h w) -> p h w", h=H), inside[0], ALU.subtract).then_inc(sem("A_padl_done"), 1)
                if live(i, IMAGES):
                    group_stats(i, 1)
                if live(old, IMAGES):
                    route_rows("A_", old, 2)
                if live(i, IMAGES):
                    group_affine(i, 1)
                    accumulate(i, 1)
                if live(nxt, IMAGES):
                    dve.wait_ge(sem("A_h8"), nxt.b + 1)
                    dve.tensor_scalar(hb[0:8, nxt.u, :], ones_f[0:8, :], h8[0:8, nxt.u, :], None, ALU.mult).then_inc(sem("A_hb"), 1)
                if live(old, IMAGES):
                    route_choose("A_", old, 2)
                if live(nxt, IMAGES):
                    a_gates(nxt)

            sweep(dve, IMAGES, a_step, L, PER_A)

            def table(p, src, limit):
                dve.wait_ge(sem(src + "counts_done"), 1)
                one = slice(0, 1)
                cnt, til, cum, ones8 = (x[one] for x in b_e)
                big, thr = b_big[one], b_thr[one]
                o1, o2, o3, o4 = (x[one] for x in b_one)
                dve.tensor_scalar(cnt, sm_a[one, 32:32 + E], float(limit), None, ALU.min).then_inc(sem("dve_steps"), 1)
                dve.wait_ge(sem("dve_steps"), L.step())
                dve.tensor_tensor(ones8, cnt, first_slot[one, 0, :], ALU.add).then_inc(sem("dve_steps"), 1)
                dve.wait_ge(sem("dve_steps"), L.step())
                dve.tensor_copy(tail_i[one], ones8).then_inc(sem("dve_steps"), 1)
                dve.wait_ge(sem("dve_steps"), L.step())
                dve.tensor_tensor(thr, bcast(cnt, 33), iota_j[one].unsqueeze(1).to_broadcast([1, E, 33]), ALU.is_gt).then_inc(sem("dve_steps"), 1)
                dve.wait_ge(sem("dve_steps"), L.step())
                dve.tensor_reduce(til, thr, AX_X, ALU.add).then_inc(sem("dve_steps"), 1)
                dve.wait_ge(sem("dve_steps"), L.step())
                dve.memset(ones8, 1.0).then_inc(sem("dve_steps"), 1)
                dve.wait_ge(sem("dve_steps"), L.step())
                dve.tensor_tensor_scan(cum, ones8, til, 0.0, ALU.mult, ALU.add).then_inc(sem("dve_steps"), 1)
                dve.wait_ge(sem("dve_steps"), L.step())
                dve.tensor_tensor(big, bcast(iota_i[one], E), cum.unsqueeze(1).to_broadcast([1, TILES0, E]), ALU.is_ge).then_inc(sem("dve_steps"), 1)
                dve.wait_ge(sem("dve_steps"), L.step())
                dve.tensor_reduce(o1, big, AX_X, ALU.add).then_inc(sem("dve_steps"), 1)
                dve.wait_ge(sem("dve_steps"), L.step())
                dve.tensor_tensor(big, big, til.unsqueeze(1).to_broadcast([1, TILES0, E]), ALU.mult).then_inc(sem("dve_steps"), 1)
                dve.wait_ge(sem("dve_steps"), L.step())
                dve.tensor_reduce(o2, big, AX_X, ALU.add).then_inc(sem("dve_steps"), 1)
                dve.wait_ge(sem("dve_steps"), L.step())
                dve.tensor_tensor(o3, iota_i[one], o2, ALU.subtract).then_inc(sem("dve_steps"), 1)
                dve.wait_ge(sem("dve_steps"), L.step())
                dve.tensor_scalar(o3, o3, float(TILE), None, ALU.mult).then_inc(sem("dve_steps"), 1)
                dve.wait_ge(sem("dve_steps"), L.step())
                dve.scalar_tensor_tensor(out=o4, in0=o1, scalar=float(REG), in1=o3, op0=ALU.mult, op1=ALU.add).then_inc(sem("dve_steps"), 1)
                dve.wait_ge(sem("dve_steps"), L.step())
                dve.tensor_scalar(tab_i[one, 0, :], o4, float(E * REG), None, ALU.min).then_inc(sem("dve_steps"), 1)
                dve.wait_ge(sem("dve_steps"), L.step())
                dve.tensor_scalar(tab_i[one, 1, :], o1, float(E - 1), None, ALU.min).then_inc(sem(p + "table_ready"), 1)

            def ffn(p, n, nj, gated, count):
                def low(i, j):
                    c = i.b * nj + j
                    if gated:
                        dve.wait_ge(sem(p + "gh_done"), c + 1)
                    dve.tensor_tensor(gl[i.u][:, j, :], g32[j], gh[i.u][:, j, :], ALU.subtract).then_inc(sem(p + "gl_done"), 1)

                def step(i):
                    nxt, older = i + 1, i + (-2)
                    if live(nxt, n):
                        dve.wait_ge(sem(p + "xh_done"), nxt.b + 1)
                        dve.tensor_tensor(xl[nxt.u], psum[:, nxt.u, :], xh[nxt.u], ALU.subtract).then_inc(sem(p + "xl_done"), 1)
                    for j in range(nj):
                        if live(i, n):
                            c = i.b * nj + j
                            m = (i.u * nj + j) % 2
                            if gated:
                                dve.wait_ge(sem(p + "silu"), c + 1)
                                if some(c + 1 - nj):
                                    dve.wait_ge(sem(p + "gl_done"), c + 1 - nj)
                                dve.scalar_tensor_tensor(out=g32[j], in0=psum[:, 3 + 2 * m, :], scalar=scale[:, NS + S1:NS + S1 + 1],
                                                         in1=sg[m], op0=ALU.mult, op1=ALU.mult).then_inc(sem(p + "g_done"), 1)
                                if j:
                                    low(i, j - 1)
                            else:
                                dve.wait_ge(sem(p + "up_read"), c + 1)
                                if some(i.b - 1):
                                    dve.wait_ge(sem(p + "y_done"), i.b - 1)
                                dve.tensor_copy(gh[i.u][:, j, :], g32[j]).then_inc(sem("dve_steps"), 1)
                                dve.wait_ge(sem("dve_steps"), L.step())
                                low(i, j)
                        if j == 0 and live(older, n):
                            dve.wait_ge(sem(p + "yt_done"), older.b + 1)
                            dve.wait_ge(sem(p + "ids_copied"), older.b * 2 + 2)
                            last = older + (-2)
                            if live(last, n):
                                dve.wait_ge(sem(f"{p}scattered{last.v}"), (last.w + 1) * (16 * QT))
                            gate = idg[older.v][:, :, 1:2].to_broadcast([P, QT, C])
                            dve.tensor_tensor(yt[older.u], psum[:, 7, :].rearrange("p (q c) -> p q c", q=QT), gate, ALU.mult).then_inc(sem(p + "yt_ready"), 1)
                    if live(i, n) and gated:
                        low(i, nj - 1)

                sweep(dve, n, step, L, count, per=4)

            table("B_", "A_", TOKENS)
            ffn("B_", TILES0, NJ0, True, 0)

            dve.memset(msum, 0.0).then_inc(sem("dve_steps"), 1)
            dve.wait_ge(sem("dve_steps"), L.step())
            dve.memset(msum16, 0.0).then_inc(sem("dve_steps"), 1)
            dve.wait_ge(sem("dve_steps"), L.step())
            dve.tensor_copy(idf, iota_t).then_inc(sem("dve_steps"), 1)
            dve.wait_ge(sem("dve_steps"), L.step())

            def c_step(i):
                old, nxt = i + (-1), i + 1
                if live(old, IMAGES):
                    dve.wait_ge(sem("C_tok_done"), old.b + 1)
                    dst = tokens[:, bass.ds(old.b * TPI, TPI), :]
                    dve.tensor_tensor(dst, dst, tp_tok, ALU.add).then_inc(sem("C_tok_added"), 1)
                if live(nxt, IMAGES):
                    dve.wait_ge(sem("C_y_summed"), nxt.b + 1)
                    base = nxt.b * TPI
                    dst = tokens[:, bass.ds(base, TPI), :]
                    dve.tensor_tensor(dst, dst, ya[nxt.u], ALU.add).then_inc(sem("C_added"), 1)
                    dve.wait_ge(sem("C_added"), nxt.b + 1)
                    tok = lambda tt: tokens[:, bass.ds(base + tt, 1), :].rearrange("p a c -> p (a c)")
                    token_stats(tok, 1e-6)
                    for tt in range(TPI):
                        last = dve.tensor_scalar(ntm[:, tt, :], tok(tt), mv8[:, tt, 0:1], rs8[:, tt:tt + 1], ALU.subtract, ALU.mult)
                    last.then_inc(sem("C_ntm"), 1)
                if live(old, IMAGES):
                    route_rows("C_", old, 1)
                    route_choose("C_", old, 1)
                if live(nxt, IMAGES):
                    dve.wait_ge(sem("C_wd_done"), nxt.b + 1)
                    dve.tensor_tensor(wd, sm_a[:, 8:8 + TAPS], b2_taps, ALU.add).then_inc(sem("dve_steps"), 1)
                    dve.wait_ge(sem("dve_steps"), L.step())
                    dve.sem_inc(sem("C_wd_read"), 1)
                    if some(nxt.b):
                        dve.wait_ge(sem("C_conv_done"), nxt.b)
                    dve.tensor_tensor(diag, ident.unsqueeze(1).to_broadcast([P, TAPS, P]), bcast(wd, P), ALU.mult).then_inc(sem("C_diag"), 1)

            sweep(dve, IMAGES, c_step, L, PER_C)
            table("D_", "C_", CAP)
            ffn("D_", TILES1, NJ1, False, 4 * NJ1)

            def f_step(i):
                if not live(i, IMAGES):
                    return
                z = zf[i.u]
                dve.wait_ge(sem(f"F_loaded{i.u}"), i.h * 16 + 16)
                if some(i.b):
                    dve.wait_ge(sem("F_added"), i.b)
                dve.tensor_scalar(rep, z, FLT_MAX, 1e4, ALU.is_gt, ALU.mult).then_inc(sem("dve_steps"), 1)
                dve.wait_ge(sem("dve_steps"), L.step())
                dve.tensor_scalar(nn, z, -FLT_MAX, 1e4, ALU.is_lt, ALU.mult).then_inc(sem("dve_steps"), 1)
                dve.wait_ge(sem("dve_steps"), L.step())
                dve.tensor_tensor(rep, rep, nn, ALU.subtract).then_inc(sem("dve_steps"), 1)
                dve.wait_ge(sem("dve_steps"), L.step())
                dve.tensor_scalar(finite, z, 0.0, 0.0, ALU.mult, ALU.is_equal).then_inc(sem("dve_steps"), 1)
                dve.wait_ge(sem("dve_steps"), L.step())
                apart(dve)
                dve.copy_predicated(rep, finite, z).then_inc(sem("dve_steps"), 1)
                dve.wait_ge(sem("dve_steps"), L.step())
                if some(i.b - 1):
                    dve.wait_ge(sem("F_turned"), i.b - 1)
                dve.tensor_tensor(osum[i.u].rearrange("p (t c) -> p t c", t=TPI), tokens[:, bass.ds(i.b * TPI, TPI), :],
                                  rep.rearrange("p (t c) -> p t c", t=TPI), ALU.add).then_inc(sem("F_added"), 1)

            sweep(dve, IMAGES, f_step, L, 10)


_INS = ['x', 'L0_conv_router_w1', 'L0_conv_router_b1', 'L0_conv_router_w2', 'L0_conv_router_b2', 'L0_conv_expert_w',
        'L0_conv_expert_gn_gamma', 'L0_conv_expert_gn_beta', 'L0_conv_shared_w', 'L0_conv_shared_gn_gamma',
        'L0_conv_shared_gn_beta', 'L0_ffn_router_w', 'L0_ffn_w1', 'L0_ffn_w2', 'L0_ffn_w3', 'L1_conv_w1', 'L1_conv_b1',
        'L1_conv_w2', 'L1_conv_b2', 'L1_ffn_gate_w', 'L1_ffn_gate_b', 'L1_ffn_w1', 'L1_ffn_b1', 'L1_ffn_w2', 'L1_ffn_b2']


def kernel(**inputs):
    import concourse.bacc as bacc
    from concourse.bass_utils import run_bass_kernel_spmd

    nc = bacc.Bacc("TRN2", target_bir_lowering=False, num_devices=1)
    arrays, aps = {}, {}
    for name in _INS:
        x = np.ascontiguousarray(inputs[name])
        arrays[f"in_{name}"] = x
        aps[name] = nc.dram_tensor(f"in_{name}", x.shape, mybir.dt.from_np(x.dtype), kind="ExternalInput").ap()
    out = nc.dram_tensor("out_image", (IMAGES, C, H, W), F32, kind="ExternalOutput").ap()
    build(nc, aps, out)
    r = run_bass_kernel_spmd(nc, [arrays], core_ids=[0])
    return r.results[0]["out_image"]
```

```python
from contextlib import ExitStack

import numpy as np

import concourse.bass as bass
from concourse import mybir

F32 = mybir.dt.float32
F16 = mybir.dt.float16
BF16 = mybir.dt.bfloat16
I32 = mybir.dt.int32
ALU = mybir.AluOpType
ACT = mybir.ActivationFunctionType
AX_X = mybir.AxisListType.X

P = 128
IMAGES, C, H, W = 16, 128, 32, 32
PIX = H * W
TPI = PIX // P
TOKENS = IMAGES * PIX
NT = TOKENS // P
HP, WP = H + 2, W + 2
TAPS = 9
EC = 4
E = 8
HID0, HID0P = 341, 384
NJ0 = HID0P // P
HID1 = 512
NJ1 = HID1 // P
CAP = -(-5 * TOKENS // (4 * E))
TILE = 512
QT = TILE // P
ROW = 132
REG = TOKENS + TILE
SLOTS = E * REG + TILE
TILES0 = 2 * TOKENS // TILE + E
TILES1 = TOKENS // TILE + E
FILL_ID = 65536.0
FLT_MAX = 3.4028234663852886e38
STEPS_A, STEPS_C = 212, 90
GN_GROUP = 16
MAGIC = float(0x5F3759DF)
SA, SS, S1, S3, S2, D1, D2 = range(7)
NS = 7


class Img:

    def __init__(self, q, k, per=2):
        self.b = q * per + k
        self.h = q * (per // 2) + k // 2
        self.u = k % 2
        self.v = k % 4
        self.w = q + k // 4
        self.q, self.k, self.per = q, k, per

    def __add__(self, d):
        return Img(self.q, self.k + d, self.per)


def some(value):
    return not isinstance(value, int) or value > 0


def upto(value, last):
    return min(value, last) if isinstance(value, int) else value


def sweep(eng, n, step, line=None, count=0, per=2):
    for t in range(-1, per):
        step(Img(t // per, t % per, per))
    if line:
        line.enter(count)
    with eng.Fori(1, n // per - 1) as q:
        if line:
            line.next_pass(q - 1)
        for k in range(per):
            step(Img(q, k, per))
        if line:
            line.end_pass()
    if line:
        line.leave(n // per - 2)
    for t in range(n - per, n + 2):
        step(Img(t // per, t % per, per))


def weave(*chains):
    chains = [c for c in chains if c]
    while chains:
        for c in list(chains):
            if next(c, chains) is chains:
                chains.remove(c)


def live(i, n):
    return not isinstance(i.b, int) or 0 <= i.b < n


class Line:

    def __init__(self):
        self.base, self.n = 0, 0

    def step(self):
        self.n += 1
        return self.base + self.n

    def enter(self, per):
        self.start, self.per = self.base + self.n, per

    def next_pass(self, done):
        self.base, self.n = done * self.per + self.start, 0

    def end_pass(self):
        assert self.n == self.per, f"a pass has {self.n} steps"

    def leave(self, passes):
        self.base, self.n = self.start + passes * self.per, 0


def bcast(ap, n):
    return ap.unsqueeze(2).to_broadcast([ap.shape[0], ap.shape[1], n])


def build(nc, a, out):
    slots = nc.dram_tensor("slot_rows", (SLOTS, ROW), F32, kind="Internal").ap()
    back0 = nc.dram_tensor("ffn0_rows", (2 * TOKENS, C), F32, kind="Internal").ap()
    parked = nc.dram_tensor("conv1_weights", (P, (1 + TAPS) * P), F32, kind="Internal").ap()
    back1 = nc.dram_tensor("ffn1_rows", (TOKENS, C), F32, kind="Internal").ap()

    ctx = ExitStack()
    with ctx:
        def sb(name, shape, dt=F32):
            return ctx.enter_context(nc.sbuf_tensor(name, shape, dt))

        sems = {}

        def apart(eng):
            eng.sem_inc(sem("passed_waits"), 1)

        def sem(name):
            if name not in sems:
                sems[name] = ctx.enter_context(nc.semaphore(name))
            return sems[name]

        tokens = sb("tokens", [P, NT, C])
        wa_h = sb("wa_h", [P, EC * TAPS * P], F16)
        wa_l = sb("wa_l", [P, EC * TAPS * P], F16)
        ws_h = sb("ws_h", [P, P], F16)
        ws_l = sb("ws_l", [P, P], F16)
        wb1_h = sb("wb1_h", [P, E * HID0P], F16)
        wb1_l = sb("wb1_l", [P, E * HID0P], F16)
        wb3_h = sb("wb3_h", [P, E * HID0P], F16)
        wb3_l = sb("wb3_l", [P, E * HID0P], F16)
        wb2_h = sb("wb2_h", [P, E * NJ0 * C], F16)
        wb2_l = sb("wb2_l", [P, E * NJ0 * C], F16)
        wd1_h = sb("wd1_h", [P, E * HID1], F16)
        wd1_l = sb("wd1_l", [P, E * HID1], F16)
        wd2_h = sb("wd2_h", [P, E * NJ1 * C], F16)
        wd2_l = sb("wd2_l", [P, E * NJ1 * C], F16)
        work = sb("work", [P, 11800])
        small = sb("small", [P, 2800])

        def carve(tensor):
            used = [0]

            def take(shape, dt=F32):
                n = -(-int(np.prod(shape)) * (2 if dt in (F16, BF16) else 4) // 4)
                ap = tensor[:, used[0]:used[0] + n]
                used[0] += n
                assert used[0] <= tensor.shape[1], (used[0], tensor.shape)
                if dt != F32:
                    ap = ap.bitcast(dt)
                if len(shape) == 2:
                    ap = ap.rearrange("p (a b) -> p a b", a=shape[0])
                elif len(shape) == 3:
                    ap = ap.rearrange("p (a b c) -> p a b c", a=shape[0], b=shape[1])
                return ap
            return take

        t = carve(small)
        ident = t([P])
        upper = t([P], BF16)
        ones = t([P], BF16)
        ones_f = t([P])
        group = t([P])
        fill = t([1, ROW])
        vecs = t([67])
        w2r = t([EC])
        b2r = t([1, EC])
        b1r = t([1])
        gate1_w = t([E])
        gate1_b = t([1, E])
        b2_taps = t([TAPS])
        desc8 = t([TPI, E])
        first_slot = t([TPI, E])
        desc4 = t([1, EC])
        fills = fill.to_broadcast([P, QT, ROW])
        iota_i = t([TILES0])
        iota_j = t([33])
        iota_t = t([TPI])
        mx = t([NS])
        scale = t([2 * NS])
        spread = t([2 * NS])
        neg_sq = t([2])
        y0_scale = t([1])
        y1_scale = t([1])
        gam = t([3, EC + 1])
        b1s = t([E * NJ1])
        pool = t([2, 1])
        h8 = t([2, 1])
        hb = t([2, P])
        sel = t([2, 2, 3])
        gates = t([2, 2])
        eidx = t([2, 2], I32)
        gst = t([2, 12])
        me2 = t([2, 2])
        gmean, gvar, gneg, grstd, gtmp = t([2, 2]), t([2, 1]), t([2, 1]), t([2, 1]), t([2, 1])
        gsb = t([2, 2])
        g_logit, g_shift, g_exp, g_prob, g_tmp = (t([1, EC]) for _ in range(5))
        g_hot, g_best, g_first, g_pick = t([2, EC]), t([2]), t([2]), t([2, 3, EC])
        s4 = [t([1]) for _ in range(3)]

        class Stats:

            def __init__(self):
                self.st, self.mv = t([TPI, 6]), t([TPI, 2])
                self.var, self.rstd, self.tmp, self.bias = (t([TPI]) for _ in range(4))

        image_stats, row_stats = Stats(), Stats()
        shifted, exped, probs, tmp8, place = (t([TPI, E]) for _ in range(5))
        hots, prod2 = t([2, TPI, E]), t([2, TPI, E])
        bests, slot_f = t([2, TPI]), t([2, TPI])
        s8 = [t([TPI]) for _ in range(8)]
        mask = t([TPI, E], BF16)
        msum = t([E])
        msum16 = t([E], BF16)
        idf = t([TPI])
        slot_i = t([2, TPI], I32)
        hg = t([1])
        wd = t([TAPS])
        tab_i = t([2, TILES0], I32)
        tail_i = t([E], I32)

        tA = carve(work)
        ntm = tA([TPI, C])
        nT = ntm.rearrange("p t c -> p (t c)")
        rows = [tA([TPI, ROW]) for _ in range(2)]
        shared_end = P * TPI + 2 * TPI * ROW

        def row_buffer(p, i, k):
            return k if p == "A_" else i.u
        xcm = [tA([PIX]) for _ in range(2)]
        pad_h = [tA([HP, WP], F16) for _ in range(2)]
        pad_l = [tA([HP, WP], F16) for _ in range(2)]
        act_o = [tA([PIX]) for _ in range(2)]
        acc = [tA([PIX]) for _ in range(2)]

        tC = carve(work)
        tC([shared_end])
        ya = [tC([TPI, C]) for _ in range(2)]
        yb = [tC([TPI, C]) for _ in range(2)]
        vpad = [tC([HP, WP]) for _ in range(2)]
        diag = tC([TAPS, P])
        cacc = tC([PIX])

        tB = carve(work)
        xt = [tB([QT, ROW]) for _ in range(2)]
        xh = [tB([TILE], F16) for _ in range(2)]
        xl = [tB([TILE], F16) for _ in range(2)]
        sg = [tB([TILE]) for _ in range(2)]
        g32 = [tB([TILE]) for _ in range(4)]
        gh = [tB([NJ1, TILE], F16) for _ in range(2)]
        gl = [tB([NJ1, TILE], F16) for _ in range(2)]
        ysb = tB([TILE])
        yt = [tB([QT, C]) for _ in range(2)]
        idg = [tB([QT, 2]) for _ in range(4)]
        tT = carve(gl[0].rearrange("p j c -> p (j c)").bitcast(F32))
        b_big = tT([TILES0, E])
        b_thr = tT([E, 33])
        tT = carve(gl[1].rearrange("p j c -> p (j c)").bitcast(F32))
        b_one = [tT([TILES0]) for _ in range(4)]
        b_e = [tT([E]) for _ in range(4)]

        tF = carve(work)
        zf = [tF([PIX]) for _ in range(2)]
        rep = tF([PIX])
        nn = tF([PIX])
        finite = tF([PIX], I32)
        ocm = [tF([PIX]) for _ in range(2)]
        osum = [tF([PIX]) for _ in range(2)]

        tN = carve(tokens[:, :, :].rearrange("p a b -> p (a b)"))
        nat_a = tN([EC, C * TAPS])
        nat_s = tN([C])
        nat_b1 = tN([E, NJ0, C])
        nat_b3 = tN([E, NJ0, C])
        nat_b2 = tN([E, HID0P])
        nat_v = tN([P])
        nat_c1 = tN([P])
        nat_c2 = tN([TAPS, P])
        nat_r2 = tN([8])
        tD = carve(work)
        nat_d1 = tD([E, HID1])
        nat_d2 = tD([E, NJ1, C])
        cw_stage = tD([(1 + TAPS) * P])
        cw = wa_h[:, 0:2 * (1 + TAPS) * P].bitcast(F32)
        VEC = dict(eg=0, eb=4, sg=8, sb=9, cb1=10, fb2=11, rw0=19, rw1=27, fb1=35, end=67)

        def vec(name, i=0, n=1):
            return vecs[:, VEC[name] + i:VEC[name] + i + n]

        psum = ctx.enter_context(nc.psum_tensor("banks", [P, 8, 512], F32))
        tp = psum[:, 0:2, :].rearrange("p a b -> p (a b)")
        tp_tok = tp.rearrange("p (t c) -> p t c", t=TPI)
        pair = [psum[:, 2:4, :].rearrange("p a b -> p (a b)"), psum[:, 4:6, :].rearrange("p a b -> p (a b)")]


        def of(j):
            return 0 if j == 2 else 1

        sm_a = psum[:, 6, :]
        sm_b = psum[:, 7, :]

        block = ctx.enter_context(nc.Block())

        groups = []
        taps_of = nat_a.rearrange("p e (c k) -> p e k c", k=TAPS)
        blocks = [taps_of[:, e, k, :] for e in range(EC) for k in range(TAPS)]
        for g in range(EC * TAPS // 4):
            groups.append((blocks[4 * g:4 * g + 4], SA, wa_h[:, g * 512:(g + 1) * 512], wa_l[:, g * 512:(g + 1) * 512]))
        groups.append(([nat_s], SS, ws_h[:, :], ws_l[:, :]))
        for nat, s, hi, lo in ((nat_b1, S1, wb1_h, wb1_l), (nat_b3, S3, wb3_h, wb3_l)):
            blocks = [nat[:, e, j, :] for e in range(E) for j in range(NJ0)]
            for g in range(E * NJ0 // 4):
                groups.append((blocks[4 * g:4 * g + 4], s, hi[:, g * 512:(g + 1) * 512], lo[:, g * 512:(g + 1) * 512]))
        blocks = [nat_b2[:, e, j * P:(j + 1) * P] for e in range(E) for j in range(NJ0)]
        for g in range(E * NJ0 // 4):
            groups.append((blocks[4 * g:4 * g + 4], S2, wb2_h[:, g * 512:(g + 1) * 512], wb2_l[:, g * 512:(g + 1) * 512]))
        plain = [([nat_c1] + [nat_c2[:, k, :] for k in range(3)], cw_stage[:, 0:512]),
                 ([nat_c2[:, k, :] for k in range(3, 7)], cw_stage[:, 512:1024]),
                 ([nat_c2[:, k, :] for k in range(7, 9)], cw_stage[:, 1024:1280])]
        NG = len(groups)
        NPL = len(plain)
        LOADS = 35

        @block.sync
        def _(sp):
            sp.wait_ge(sem("stage_zeroed"), 4)
            n = 0

            def load(dst, src, slow=False):
                nonlocal n
                n += 1
                sp.dma_start(dst, src, allow_slow_non_contiguous=slow).then_inc(sem("setup_loaded"), 16)

            load(nat_a, a["L0_conv_expert_w"].rearrange("e o c y x -> o e (c y x)"))
            load(nat_s, a["L0_conv_shared_w"])
            for nat, name in ((nat_b1, "L0_ffn_w1"), (nat_b3, "L0_ffn_w3")):
                for j in range(2):
                    load(nat[:, :, j, :], a[name][:, j * P:(j + 1) * P, :].rearrange("e h c -> h e c"))
                load(nat[0:HID0 - 2 * P, :, 2, :], a[name][:, 2 * P:HID0, :].rearrange("e h c -> h e c"))
            load(nat_b2[:, :, 0:HID0], a["L0_ffn_w2"].rearrange("e c h -> c e h"))
            load(nat_c1, a["L1_conv_w1"])
            load(nat_c2, a["L1_conv_w2"].rearrange("(c k) j -> c k j", k=TAPS))
            load(nat_v[0:4, :], a["L0_conv_expert_gn_gamma"])
            load(nat_v[4:8, :], a["L0_conv_expert_gn_beta"])
            load(nat_v[8:9, :], a["L0_conv_shared_gn_gamma"].unsqueeze(0))
            load(nat_v[9:10, :], a["L0_conv_shared_gn_beta"].unsqueeze(0))
            load(nat_v[10:11, :], a["L1_conv_b1"].unsqueeze(0))
            load(nat_v[11:19, :], a["L1_ffn_b2"])
            load(nat_v[19:27, :], a["L0_ffn_router_w"])
            load(nat_v[27:35, :], a["L0_conv_router_w1"])
            load(nat_v[35:67, :], a["L1_ffn_b1"].rearrange("e (j p) -> (e j) p", p=P))
            load(nat_r2[0:EC, :], a["L0_conv_router_w2"])
            load(b1r[0:8, :], a["L0_conv_router_b1"].unsqueeze(1), slow=True)
            load(b2r[:, 0, :], a["L0_conv_router_b2"].unsqueeze(0).to_broadcast([P, EC]))
            load(gate1_w, a["L1_ffn_gate_w"])
            load(gate1_b[:, 0, :], a["L1_ffn_gate_b"].unsqueeze(0).to_broadcast([P, E]))
            load(b2_taps, a["L1_conv_b2"].rearrange("(c k) -> c k", k=TAPS))
            load(nat_d1, a["L1_ffn_w1"].rearrange("e c f -> c e f"))
            for e in range(E):
                load(nat_d2[:, e, :, :], a["L1_ffn_w2"][e].rearrange("(j p) c -> p j c", p=P))
            assert n == LOADS, n

            sp.wait_ge(sem("fill_ready"), 1)
            for i in range(TOKENS // TILE):
                sp.dma_start(back1[i * TILE:(i + 1) * TILE, :].rearrange("(q p) c -> p q c", p=P),
                             fill[:, :, 0:C].to_broadcast([P, QT, C])).then_inc(sem("zeroed"), 16)
            sp.dma_start(slots[E * REG:SLOTS, :].rearrange("(q p) c -> p q c", p=P), fills).then_inc(sem("zeroed"), 16)

            sp.wait_ge(sem("plain_copied"), NPL)
            sp.dma_start(parked, cw_stage).then_inc(sem("parked"), 16)
            sp.wait_ge(sem("parked"), 16)
            sp.wait_ge(sem("setup_done"), 1)
            x_img = a["x"].rearrange("b c h w -> b c (h w)")
            for b in range(2):
                sp.dma_start(xcm[b], x_img[b]).then_inc(sem(f"x_loaded{b}"), 16)
            with sp.Fori(1, IMAGES // 2) as q:
                for u in range(2):
                    if some(q * 2 + u - 1):
                        sp.wait_ge(sem("A_acc0"), q * 2 + u - 1)
                    sp.dma_start(xcm[u], x_img[bass.ds(q * 2 + u, 1)].rearrange("b c n -> (b c) n")).then_inc(sem(f"x_loaded{u}"), 16)

            def tile_loads(p, n, before, choices):
                sp.wait_ge(sem(p + "table_ready"), 1)
                for e in range(E):
                    at_slot = sp.value_load(tail_i[0:1, e:e + 1], min_val=0, max_val=SLOTS - TILE)
                    sp.dma_start(slots[bass.ds(at_slot, TILE), :].rearrange("(q p) c -> p q c", p=P),
                                   fills).then_inc(sem(p + "tails"), 16)
                sp.wait_ge(sem(p + "tails"), 16 * E)
                sp.wait_ge(sem("zeroed"), 16 * (TOKENS // TILE + 1))
                for k in range(2):
                    sp.wait_ge(sem(f"{before}scattered_rows{k}"), 16 * NT * choices // 2)

                def load_tile(i):
                    if some(i.b * 2 - 2):
                        sp.wait_ge(sem(p + "ids_copied"), i.b * 2 - 2)
                    apart(sp)
                    if some(i.b - 1):
                        sp.wait_ge(sem(p + "xt_done"), i.b - 1)
                    apart(sp)
                    row = sp.value_load(tab_i[0:1, 0, bass.ds(i.b, 1)], min_val=0, max_val=SLOTS - TILE)
                    sp.dma_start(xt[i.u], slots[bass.ds(row, TILE), :].rearrange("(q p) c -> p q c", p=P)).then_inc(sem(f"{p}xt_loaded{i.u}"), 16)

                for k in range(2):
                    load_tile(Img(0, k))
                with sp.Fori(1, n // 2) as q:
                    for k in range(2):
                        load_tile(Img(q, k))

            sp.wait_ge(sem("A_conv_done2"), IMAGES)
            sp.dma_start(cw, parked).then_inc(sem("parked"), 16)

            tile_loads("B_", TILES0, "A_", 2)

            for v in range(4):
                sp.wait_ge(sem(f"B_scattered{v}"), 16 * QT * TILES0 // 4)

            def load_rows(i):
                if some(i.b - 1):
                    sp.wait_ge(sem("C_added"), i.b - 1)
                for k, dst in ((0, ya), (1, yb)):
                    src = back0[bass.ds(i.b * PIX + k * TOKENS, PIX), :]
                    sp.dma_start(dst[i.u], src.rearrange("(t p) c -> p t c", p=P)).then_inc(sem(f"C_rows_loaded{i.u}"), 16)

            for k in range(2):
                load_rows(Img(0, k))
            with sp.Fori(1, IMAGES // 2) as q:
                for k in range(2):
                    load_rows(Img(q, k))

            tile_loads("D_", TILES1, "C_", 1)

            for v in range(4):
                sp.wait_ge(sem(f"D_scattered{v}"), 16 * QT * TILES1 // 4)
            out_img = out.rearrange("b c h w -> b c (h w)")

            def final(i):
                nxt = i
                if live(nxt, IMAGES):
                    if some(nxt.b - 1):
                        sp.wait_ge(sem("F_added"), nxt.b - 1)
                    src = back1[bass.ds(nxt.b * PIX, PIX), :]
                    sp.dma_start(zf[nxt.u].rearrange("p (t c) -> p t c", t=TPI),
                                 src.rearrange("(t p) c -> p t c", p=P)).then_inc(sem(f"F_loaded{nxt.u}"), 16)
                old = i + (-2)
                if live(old, IMAGES):
                    sp.wait_ge(sem("F_out_ready"), old.b + 1)
                    dst = out_img[bass.ds(old.b, 1)].rearrange("b c n -> (b c) n")
                    sp.dma_start(dst, ocm[old.u]).then_inc(sem(f"F_stored{old.u}"), 16)

            sweep(sp, IMAGES, final)
            for u in range(2):
                sp.wait_ge(sem(f"F_stored{u}"), 16 * IMAGES // 2)

        @block.gpsimd
        def _(pool_e):
            line = Line()
            for nat in (nat_b1, nat_b3):
                pool_e.memset(nat[:, :, 2, :], 0.0).then_inc(sem("stage_zeroed"), 1)
            pool_e.memset(nat_b2[:, :, HID0:HID0P], 0.0).then_inc(sem("stage_zeroed"), 1)
            pool_e.memset(nat_v, 0.0).then_inc(sem("stage_zeroed"), 1)
            pool_e.memset(fill, 0.0).then_inc(sem("pool_steps"), 1)
            pool_e.wait_ge(sem("pool_steps"), line.step())
            pool_e.memset(fill[:, :, C:C + 1], FILL_ID).then_inc(sem("fill_ready"), 1)
            pool_e.memset(ident, 0.0).then_inc(sem("pool_steps"), 1)
            pool_e.wait_ge(sem("pool_steps"), line.step())
            pool_e.affine_select(out=ident, in_=ident, compare_op=ALU.not_equal, fill=1.0, base=0,
                                 pattern=[[-1, P]], channel_multiplier=1).then_inc(sem("pool_steps"), 1)
            pool_e.wait_ge(sem("pool_steps"), line.step())
            pool_e.memset(ones, 1.0).then_inc(sem("const_ready"), 1)
            pool_e.memset(ones_f, 1.0).then_inc(sem("pool_steps"), 1)
            pool_e.wait_ge(sem("pool_steps"), line.step())
            pool_e.affine_select(out=upper, in_=ones_f, compare_op=ALU.is_gt, fill=0.0, base=0,
                                 pattern=[[1, P]], channel_multiplier=-1).then_inc(sem("const_ready"), 1)
            pool_e.memset(group, 1.0 / GN_GROUP).then_inc(sem("pool_steps"), 1)
            pool_e.wait_ge(sem("pool_steps"), line.step())
            pattern = [[-GN_GROUP, P // GN_GROUP], [0, GN_GROUP]]
            pool_e.affine_select(out=group, in_=group, compare_op=ALU.is_ge, fill=0.0, base=0,
                                 pattern=pattern, channel_multiplier=1).then_inc(sem("pool_steps"), 1)
            pool_e.wait_ge(sem("pool_steps"), line.step())
            pattern = [[GN_GROUP, P // GN_GROUP], [0, GN_GROUP]]
            pool_e.affine_select(out=group, in_=group, compare_op=ALU.is_ge, fill=0.0, base=GN_GROUP - 1,
                                 pattern=pattern, channel_multiplier=-1).then_inc(sem("const_ready"), 1)
            for dst, pattern, base, mult in (
                    (desc8, [[0, TPI], [-1, E]], E, 0), (first_slot, [[0, TPI], [REG // 2, E]], 0, 0),
                    (desc4, [[0, 1], [-1, EC]], EC, 0), (iota_i, [[1, TILES0]], 0, 0),
                    (iota_j, [[TILE, 33]], 0, 0), (iota_t, [[P, TPI]], 0, 1)):
                pool_e.iota(dst, pattern=pattern, base=base, channel_multiplier=mult,
                            allow_small_or_imprecise_dtypes=True).then_inc(sem("const_ready"), 1)
            pool_e.wait_ge(sem("setup_done"), 1)
            for x in (*pad_h, *pad_l):
                pool_e.memset(x, 0.0).then_inc(sem("pads_zeroed"), 1)

            def scatters(p, i, choices):
                if not live(i, IMAGES):
                    return
                pool_e.wait_ge(sem(p + "slots_known"), i.b + 1)
                apart(pool_e)
                for k in range(choices):
                    for tt in range(TPI):
                        pool_e.indirect_dma_start(
                            slots, bass.IndirectOffsetOnAxis(ap=slot_i[:, row_buffer(p, i, k), tt:tt + 1], axis=0),
                            rows[row_buffer(p, i, k)][:, tt, :], None, bounds_check=SLOTS - 1, oob_is_err=False
                        ).then_inc(sem(f"{p}scattered_rows{row_buffer(p, i, k)}"), 16)

            def tile_step(p, i, n, dst, limit):
                if live(i, n):
                    pool_e.wait_ge(sem(f"{p}xt_loaded{i.u}"), i.h * 16 + 16)
                    apart(pool_e)
                    if some(i.w):
                        pool_e.wait_ge(sem(f"{p}scattered{i.v}"), i.w * (16 * QT))
                    apart(pool_e)
                    pool_e.tensor_copy(idg[i.v][:, :, 0:1].bitcast(I32), xt[i.u][:, :, C:C + 1]).then_inc(sem(p + "ids_copied"), 1)
                    pool_e.tensor_copy(idg[i.v][:, :, 1:2], xt[i.u][:, :, C + 1:C + 2]).then_inc(sem(p + "ids_copied"), 1)
                old = i + (-2)
                if live(old, n):
                    pool_e.wait_ge(sem(p + "ids_copied"), old.b * 2 + 2)
                    pool_e.wait_ge(sem(p + "yt_ready"), old.b + 1)
                    apart(pool_e)
                    for qq in range(QT):
                        pool_e.indirect_dma_start(
                            dst, bass.IndirectOffsetOnAxis(ap=idg[old.v][:, qq, 0:1].bitcast(I32), axis=0),
                            yt[old.u][:, qq, :], None, bounds_check=limit - 1, oob_is_err=False
                        ).then_inc(sem(f"{p}scattered{old.v}"), 16)

            def a_step(i):
                scatters("A_", i + (-2), 2)
                nxt = i + 1
                if live(nxt, IMAGES):
                    pool_e.wait_ge(sem("A_silu0"), nxt.b + 1)
                    if some(nxt.b - 1):
                        pool_e.wait_ge(sem("A_tok_done"), nxt.b - 1)
                    pool_e.tensor_tensor(acc[nxt.u], act_o[of(0)], xcm[nxt.u], ALU.add).then_inc(sem("A_acc0"), 1)

            sweep(pool_e, IMAGES, a_step)
            sweep(pool_e, TILES0, lambda i: tile_step("B_", i, TILES0, back0, 2 * TOKENS), per=4)

            def sum_rows(i):
                pool_e.wait_ge(sem(f"C_rows_loaded{i.u}"), i.h * 32 + 32)
                pool_e.tensor_tensor(ya[i.u], ya[i.u], yb[i.u], ALU.add).then_inc(sem("C_y_summed"), 1)

            def c_step(i):
                nxt = i + 1
                if isinstance(i.b, int) and i.b == -1:
                    sum_rows(nxt)
                if live(i + 2, IMAGES):
                    sum_rows(i + 2)
                scatters("C_", i + (-2), 1)
                if live(nxt, IMAGES):
                    pool_e.wait_ge(sem("C_inside"), nxt.b + 1)
                    apart(pool_e)
                    v = vpad[nxt.u]
                    pool_e.tensor_copy(v[:, 0:1, 1:W + 1], v[:, 2:3, 1:W + 1]).then_inc(sem("C_border_done"), 1)
                    pool_e.tensor_copy(v[:, H + 1:H + 2, 1:W + 1], v[:, H - 1:H, 1:W + 1]).then_inc(sem("C_border_done"), 1)
                    pool_e.wait_ge(sem("C_border_done"), nxt.b * 4 + 2)
                    apart(pool_e)
                    pool_e.tensor_copy(v[:, :, 0:1], v[:, :, 2:3]).then_inc(sem("C_border_done"), 1)
                    pool_e.tensor_copy(v[:, :, W + 1:W + 2], v[:, :, W - 1:W]).then_inc(sem("C_border_done"), 1)

            sweep(pool_e, IMAGES, c_step)
            sweep(pool_e, TILES1, lambda i: tile_step("D_", i, TILES1, back1, TOKENS), per=4)

        @block.tensor
        def _(pe):
            pe.wait_ge(sem("pool_steps"), 6)
            pe.wait_ge(sem("const_ready"), 3)
            pe.wait_ge(sem("setup_loaded"), 16 * LOADS)
            pe.transpose(sm_a[:, 0:VEC["end"]], nat_v[0:VEC["end"], :], ident[0:VEC["end"], 0:VEC["end"]])
            pe.transpose(sm_a[0:8, 128:128 + EC], nat_r2[0:EC, :], ident[0:EC, 0:EC]).then_inc(sem("pe_turned"), 1)
            for g, (ins, _) in enumerate(plain):
                for j, x in enumerate(ins):
                    ins_ = pe.transpose(psum[:, g, j * P:(j + 1) * P], x, ident)
                ins_.then_inc(sem("plain_done"), 1)
            pe.wait_ge(sem("scale_steps"), 1)
            pe.transpose(sm_b[0:NS, 0:P], mx, ident).then_inc(sem("pe_turned"), 1)
            pe.wait_ge(sem("scale_steps"), 2)
            pe.matmul(sm_b[:, 128:128 + 2 * NS], ones_f[0:NS, :], spread[0:NS, :], start=True, stop=True).then_inc(sem("pe_turned"), 1)
            for g, (ins, _, _, _) in enumerate(groups):
                if g < NPL:
                    pe.wait_ge(sem("plain_copied"), g + 1)
                if some(g - 5):
                    pe.wait_ge(sem("group_split"), g - 5)
                for j, x in enumerate(ins):
                    ins_ = pe.transpose(psum[:, g % 6, j * P:(j + 1) * P], x, ident)
                ins_.then_inc(sem("group_done"), 1)
            pe.wait_ge(sem("group_split"), NG)
            pe.wait_ge(sem("setup_done"), 1)

            def turn(dst, blocks):
                for tt, x in enumerate(blocks):
                    last = pe.transpose(dst[:, tt * P:(tt + 1) * P], x, ident)
                return last

            def three(dst, wh, wl, nh, nl, start, stop):
                pe.matmul(dst, wh, nh, start=start, stop=False)
                pe.matmul(dst, wh, nl, start=False, stop=False)
                return pe.matmul(dst, wl, nh, start=False, stop=stop)

            def route_turn(p, i):
                pe.wait_ge(sem(p + "rows_ready"), i.b + 1)
                turn(tp, [rows[row_buffer(p, i, 0)][:, tt, 0:C] for tt in range(TPI)]).then_inc(sem(p + "nT_done"), 1)

            def logits(p, i, w):
                pe.wait_ge(sem(p + "nT_copied"), i.b + 1)
                if some(i.b):
                    pe.wait_ge(sem(p + "slots_known"), i.b)
                for tt in range(TPI):
                    last = pe.matmul(sm_b[:, tt * E:(tt + 1) * E], nT[:, tt * P:(tt + 1) * P], w, start=True, stop=True)
                last.then_inc(sem(p + "logits_done"), 1)

            def positions(p, i):
                pe.wait_ge(sem(p + "mask_ready"), i.b + 1)
                pos = sm_b[:, 64:64 + TPI * E]
                m = mask.rearrange("p t e -> p (t e)")
                pe.matmul(pos, upper, m, start=True, stop=False)
                for tt in range(TPI - 1):
                    later = mask[:, tt:tt + 1, :].to_broadcast([P, TPI - 1 - tt, E])
                    pe.matmul(pos[:, (tt + 1) * E:].rearrange("p (t e) -> p t e", e=E), ones, later, start=False, stop=False)
                before = msum16.unsqueeze(1).to_broadcast([P, TPI, E])
                pe.matmul(pos.rearrange("p (t e) -> p t e", e=E), ones, before, start=False, stop=True).then_inc(sem(p + "pos_done"), 1)

            def group_mean(i, j):
                pe.wait_ge(sem(f"A_gstat{j}"), i.b + 1)
                if j == 0:
                    pe.wait_ge(sem("A_gshift"), i.b + 1)
                elif j == 1:
                    pe.wait_ge(sem("A_h8"), upto(i.b + 2, IMAGES))
                elif j == 2:
                    pe.wait_ge(sem("A_gn_read0"), upto(i.b + 2, IMAGES))
                pe.matmul(sm_a[:, 0:2], group, me2[:, of(j), :], start=True, stop=True).then_inc(sem(f"A_gn_done{j}"), 1)

            def conv_half(i, j, half, regs, taps=range(TAPS)):
                dst = pair[of(j)][:, half * 512:(half + 1) * 512]
                h0 = half * (H // 2)
                if j == 0:
                    rhs = [x[i.u][:, h0 + 1:h0 + 1 + H // 2, 1:1 + W] for x in (pad_h, pad_l)]
                    return three(dst, ws_h[:, :], ws_l[:, :], *rhs, True, True)
                e = regs[j - 1]
                for k in taps:
                    dy, dx = k // 3, k % 3
                    rhs = [x[i.u][:, h0 + dy:h0 + dy + H // 2, dx:dx + W] for x in (pad_h, pad_l)]
                    ws = [x[:, bass.ds(e * (TAPS * P) + k * P, P)] for x in (wa_h, wa_l)]
                    last = three(dst, *ws, *rhs, k == 0, k == TAPS - 1)
                return last

            def a_step(i):
                older, old, nxt = i + (-2), i + (-1), i + 1
                regs = []
                if live(nxt, IMAGES):
                    pe.wait_ge(sem(f"x_loaded{nxt.u}"), nxt.h * 16 + 16)
                    if some(nxt.b - 2):
                        pe.wait_ge(sem("A_nT_copied"), nxt.b - 2)
                    turn(tp, [xcm[nxt.u][:, tt * P:(tt + 1) * P] for tt in range(TPI)]).then_inc(sem("A_xt_done"), 1)
                if live(i, IMAGES):
                    pe.wait_ge(sem("A_gate_ready"), i.b + 1)
                    apart(pe)
                    regs += [pe.value_load(eidx[0:1, i.u, k:k + 1], min_val=0, max_val=EC - 1) for k in range(2)]
                    pe.wait_ge(sem("A_silu0"), i.b + 1)
                    conv_half(i, 1, 0, regs, range(3))
                if live(old, IMAGES):
                    group_mean(old, 2)
                if live(i, IMAGES):
                    conv_half(i, 1, 0, regs, range(3, TAPS))
                if live(older, IMAGES):
                    positions("A_", older)
                if live(i, IMAGES):
                    conv_half(i, 1, 1, regs, range(5))
                if live(old, IMAGES):
                    pe.wait_ge(sem("A_acc2"), old.b + 1)
                    pe.wait_ge(sem("A_ntm"), upto(old.b + 3, IMAGES))
                    turn(tp, [acc[old.u][:, tt * P:(tt + 1) * P] for tt in range(TPI)]).then_inc(sem("A_tok_done"), 1)
                if live(i, IMAGES):
                    conv_half(i, 1, 1, regs, range(5, TAPS)).then_inc(sem("A_conv_done1"), 1)
                if live(nxt, IMAGES):
                    pe.wait_ge(sem("A_ntm"), nxt.b + 1)
                    if some(nxt.b - 1):
                        pe.wait_ge(sem("A_tok_copied"), nxt.b - 1)
                    turn(tp, [ntm[:, tt, :] for tt in range(TPI)]).then_inc(sem("A_cm_done"), 1)
                if live(i, IMAGES):
                    if some(i.b):
                        pe.wait_ge(sem("A_silu2"), i.b)
                    conv_half(i, 2, 0, regs, range(3))
                if live(nxt, IMAGES):
                    pe.wait_ge(sem("A_padh_done"), nxt.b + 1)
                    if some(nxt.b - 1):
                        pe.wait_ge(sem("A_gn_read2"), nxt.b - 1)
                    pe.matmul(sm_a[0:8, 8:9], vec("rw1", 0, 8), pool[:, nxt.u, :], start=True, stop=True).then_inc(sem("A_r1_done"), 1)
                if live(i, IMAGES):
                    conv_half(i, 2, 0, regs, range(3, 5))
                    group_mean(i, 1)
                    conv_half(i, 2, 0, regs, range(5, 8))
                if live(nxt, IMAGES):
                    pe.wait_ge(sem("A_hb"), nxt.b + 1)
                    if some(nxt.b):
                        pe.wait_ge(sem("A_gn_read1"), nxt.b)
                    pe.matmul(sm_a[:, 16:16 + EC], hb[0:8, nxt.u, :], w2r[0:8, :], start=True, stop=True).then_inc(sem("A_r2_done"), 1)
                if live(i, IMAGES):
                    conv_half(i, 2, 0, regs, range(8, TAPS))
                    conv_half(i, 2, 1, regs, range(1))
                if live(old, IMAGES):
                    pe.wait_ge(sem("A_padl_done"), upto(old.b + 3, IMAGES))
                    route_turn("A_", old)
                if live(nxt, IMAGES):
                    pe.wait_ge(sem("A_padl_done"), nxt.b + 1)
                    if some(nxt.b):
                        pe.wait_ge(sem("A_silu1"), nxt.b)
                    conv_half(nxt, 0, 0, regs)
                    conv_half(nxt, 0, 1, regs).then_inc(sem("A_conv_done0"), 1)
                if live(i, IMAGES):
                    conv_half(i, 2, 1, regs, range(1, 4))
                if live(nxt, IMAGES):
                    group_mean(nxt, 0)
                if live(old, IMAGES):
                    logits("A_", old, vec("rw0", 0, E))
                if live(i, IMAGES):
                    conv_half(i, 2, 1, regs, range(4, TAPS)).then_inc(sem("A_conv_done2"), 1)

            sweep(pe, IMAGES, a_step)

            def counts(p):
                pe.wait_ge(sem(p + "msum"), IMAGES)
                pe.matmul(sm_a[:, 32:32 + E], ones, msum16, start=True, stop=True).then_inc(sem(p + "counts_done"), 1)

            def ffn(p, n, nj, gated, w1, w3, w2):
                tbank = [psum[:, 0, :], psum[:, 1, :]]
                ybank, ytbank = psum[:, 6, :], psum[:, 7, :]
                nb = 2 if gated else 4

                def up(i, j, e):
                    c = i.b * nj + j
                    m = (i.u * nj + j) % nb
                    if some(c + 1 - nb):
                        pe.wait_ge(sem(p + ("g_done" if gated else "up_read")), c + 1 - nb)
                    dst = psum[:, 2 + 2 * m, :] if gated else psum[:, 2 + m, :]
                    ws = [x[:, bass.ds(e * (nj * P) + j * P, P)] for x in w1]
                    last = three(dst, *ws, xh[i.u], xl[i.u], True, True)
                    if gated:
                        ws = [x[:, bass.ds(e * (nj * P) + j * P, P)] for x in w3]
                        last = three(psum[:, 3 + 2 * m, :], *ws, xh[i.u], xl[i.u], True, True)
                    last.then_inc(sem(p + "up_done"), 1)

                def step(i):
                    nxt, old, older = i + 1, i + (-1), i + (-2)
                    if live(nxt, n):
                        pe.wait_ge(sem(f"{p}xt_loaded{nxt.u}"), nxt.h * 16 + 16)
                        if some(nxt.b - 1):
                            pe.wait_ge(sem(p + "xl_done"), nxt.b - 1)
                        turn(tbank[nxt.u], [xt[nxt.u][:, qq, 0:C] for qq in range(QT)]).then_inc(sem(p + "xt_done"), 1)
                    if live(i, n):
                        e = pe.value_load(tab_i[0:1, 1, bass.ds(i.b, 1)], min_val=0, max_val=E - 1)
                        pe.wait_ge(sem(p + "xl_done"), i.b + 1)
                        up(i, 0, e)
                    if live(older, n):
                        pe.wait_ge(sem(p + "y_copied"), older.b + 1)
                        if some(older.b):
                            pe.wait_ge(sem(p + "yt_ready"), older.b)
                        turn(ytbank, [ysb[:, qq * P:(qq + 1) * P] for qq in range(QT)]).then_inc(sem(p + "yt_done"), 1)
                    if live(i, n):
                        for j in range(1, nj):
                            up(i, j, e)
                    if live(old, n):
                        f = pe.value_load(tab_i[0:1, 1, bass.ds(old.b, 1)], min_val=0, max_val=E - 1)
                        pe.wait_ge(sem(p + "gl_done"), (old.b + 1) * nj)
                        if some(old.b):
                            pe.wait_ge(sem(p + "y_copied"), old.b)
                        for j in range(nj):
                            ws = [x[:, bass.ds(f * (nj * C) + j * C, C)] for x in w2]
                            last = three(ybank, *ws, gh[old.u][:, j, :], gl[old.u][:, j, :], j == 0, j == nj - 1)
                        last.then_inc(sem(p + "y_done"), 1)

                pe.wait_ge(sem(p + "table_ready"), 1)
                sweep(pe, n, step, per=4)

            counts("A_")
            ffn("B_", TILES0, NJ0, True, (wb1_h, wb1_l), (wb3_h, wb3_l), (wb2_h, wb2_l))

            def tap(i, k):
                if k % 3 == 0:
                    pe.wait_ge(sem("C_diag"), i.b * 3 + k // 3 + 1)
                dy, dx = k // 3, k % 3
                for half in range(2):
                    h0 = half * (H // 2)
                    last = pe.matmul(pair[i.u][:, half * 512:(half + 1) * 512], diag[:, k, :],
                                     vpad[i.u][:, h0 + dy:h0 + dy + H // 2, dx:dx + W],
                                     start=(k == 0), stop=(k == TAPS - 1))
                if k % 3 == 2:
                    last.then_inc(sem("C_taps_done"), 1)

            def c_step(i):
                older, old, nxt = i + (-2), i + (-1), i + 1
                if live(i, IMAGES):
                    pe.wait_ge(sem("C_border_done"), i.b * 4 + 4)
                    if some(i.b - 1):
                        pe.wait_ge(sem("C_conv_copied"), i.b - 1)
                    tap(i, 0)
                if live(old, IMAGES):
                    pe.wait_ge(sem("C_conv_copied"), old.b + 1)
                    if some(old.b):
                        pe.wait_ge(sem("C_nT_copied"), old.b)
                    turn(tp, [cacc[:, tt * P:(tt + 1) * P] for tt in range(TPI)]).then_inc(sem("C_tok_done"), 1)
                if live(older, IMAGES):
                    positions("C_", older)
                if live(i, IMAGES):
                    for k in (1, 2, 3):
                        tap(i, k)
                if live(nxt, IMAGES):
                    pe.wait_ge(sem("C_ntm"), nxt.b + 1)
                    if some(nxt.b - 1):
                        pe.wait_ge(sem("C_tok_added"), nxt.b - 1)
                    turn(tp, [ntm[:, tt, :] for tt in range(TPI)]).then_inc(sem("C_cm_done"), 1)
                if live(i, IMAGES):
                    tap(i, 4)
                    tap(i, 5)
                if live(nxt, IMAGES):
                    pe.wait_ge(sem("C_inside"), nxt.b + 1)
                    if some(nxt.b):
                        pe.wait_ge(sem("C_wd_read"), nxt.b)
                    pe.matmul(sm_a[:, 0:1], cw[:, 0:P], pool[:, nxt.u, :], start=True, stop=True).then_inc(sem("C_h_done"), 1)
                if live(i, IMAGES):
                    tap(i, 6)
                if live(nxt, IMAGES):
                    pe.wait_ge(sem("C_gelu"), nxt.b + 1)
                    for k in range(TAPS):
                        last = pe.matmul(sm_a[:, 8 + k:9 + k], cw[:, (1 + k) * P:(2 + k) * P], hg, start=True, stop=True)
                    last.then_inc(sem("C_wd_done"), 1)
                if live(old, IMAGES):
                    pe.wait_ge(sem("C_inside"), upto(old.b + 3, IMAGES))
                    route_turn("C_", old)
                if live(i, IMAGES):
                    tap(i, 7)
                if live(old, IMAGES):
                    logits("C_", old, gate1_w)
                if live(i, IMAGES):
                    tap(i, 8)

            pe.wait_ge(sem("parked"), 32)
            sweep(pe, IMAGES, c_step)
            counts("C_")
            ffn("D_", TILES1, NJ1, False, (wd1_h, wd1_l), None, (wd2_h, wd2_l))

            def f_step(i):
                if live(i, IMAGES):
                    pe.wait_ge(sem("F_added"), i.b + 1)
                    if some(i.b - 1):
                        pe.wait_ge(sem("F_out_ready"), i.b - 1)
                    turn(pair[i.u], [osum[i.u][:, tt * P:(tt + 1) * P] for tt in range(TPI)]).then_inc(sem("F_turned"), 1)

            sweep(pe, IMAGES, f_step)

        @block.scalar
        def _(act):
            act.wait_ge(sem("pe_turned"), 1)
            act.activation(vecs, sm_a[:, 0:VEC["end"]], ACT.Copy)
            act.activation(w2r[0:8, :], sm_a[0:8, 128:128 + EC], ACT.Copy).then_inc(sem("vecs_ready"), 1)
            for g, (ins, dst) in enumerate(plain):
                act.wait_ge(sem("plain_done"), g + 1)
                act.activation(dst, psum[:, g, 0:len(ins) * P], ACT.Copy).then_inc(sem("plain_copied"), 1)
            act.wait_ge(sem("scale_steps"), 3)
            for nat, s, hi in ((nat_d1.rearrange("p e f -> p (e f)"), D1, wd1_h), (nat_d2.rearrange("p e j c -> p (e j c)"), D2, wd2_h)):
                act.activation(hi[:, :], nat, ACT.Copy, scale=scale[:, NS + s:NS + s + 1]).then_inc(sem("direct_hi"), 1)
            for g, (ins, s, hi, _) in enumerate(groups):
                act.wait_ge(sem("group_done"), g + 1)
                act.activation(hi, psum[:, g % 6, 0:len(ins) * P], ACT.Copy, scale=scale[:, NS + s:NS + s + 1]).then_inc(sem("group_hi"), 1)

            def normalise(p, i, dst, src, s, what):
                for tt in range(TPI):
                    last = act.activation(dst(tt), src(tt), ACT.Identity, scale=s.rstd[:, tt:tt + 1], bias=s.bias[:, tt:tt + 1])
                last.then_inc(sem(p + what), 1)

            def route_rows(p, i):
                act.wait_ge(sem(p + "row_stats"), i.b + 1)
                apart(act)
                buf = row_buffer(p, i, 0)
                earlier = i.b if p == "A_" else i.h
                if some(earlier):
                    act.wait_ge(sem(f"{p}scattered_rows{buf}"), earlier * (16 * TPI))
                apart(act)
                tok = lambda tt: tokens[:, bass.ds(i.b * TPI + tt, 1), :].rearrange("p a c -> p (a c)")
                normalise(p, i, lambda tt: rows[buf][:, tt, 0:C], tok, row_stats, "rows_ready")

            def route_copy(p, i):
                act.wait_ge(sem(p + "nT_done"), i.b + 1)
                act.activation(nT, tp, ACT.Copy).then_inc(sem(p + "nT_copied"), 1)

            def route_exp(p, i):
                act.wait_ge(sem(p + "shifted"), i.b + 1)
                act.activation(exped, shifted, ACT.Exp).then_inc(sem(p + "exped"), 1)

            def a_silu(i, j):
                act.wait_ge(sem(f"A_gsb{j}"), i.b + 1)
                if j == 1:
                    act.wait_ge(sem("A_acc0"), i.b + 1)
                elif some(i.b):
                    act.wait_ge(sem(f"A_acc{(1, 0, 2)[j]}"), i.b)
                par = of(j)
                act.activation(act_o[par], pair[par], ACT.Silu, scale=gsb[:, par, 0:1], bias=gsb[:, par, 1:2]).then_inc(sem(f"A_silu{j}"), 1)

            def a_step(i):
                old, nxt = i + (-1), i + 1
                if live(old, IMAGES):
                    a_silu(old, 2)
                if live(nxt, IMAGES):
                    act.wait_ge(sem("A_image_stats"), nxt.b + 1)
                    if some(nxt.b):
                        act.wait_ge(sem("A_cm_done"), nxt.b)
                    normalise("A_", nxt, lambda tt: ntm[:, tt, :], lambda tt: tp_tok[:, tt, :], image_stats, "ntm")
                if live(old, IMAGES):
                    act.wait_ge(sem("A_tok_done"), old.b + 1)
                    apart(act)
                    dst = tokens[:, bass.ds(old.b * TPI, TPI), :]
                    act.activation(dst, tp_tok, ACT.Copy).then_inc(sem("A_tok_copied"), 1)
                if live(nxt, IMAGES):
                    act.wait_ge(sem("A_cm_done"), nxt.b + 1)
                    if some(nxt.b - 1):
                        act.wait_ge(sem("A_conv_done2"), nxt.b - 1)
                    if not isinstance(nxt.b, int) or nxt.b < 2:
                        act.wait_ge(sem("pads_zeroed"), 4)
                    act.activation(pad_h[nxt.u][:, 1:H + 1, 1:W + 1], tp.rearrange("p (h w) -> p h w", h=H), ACT.Copy,
                                   accum_out=pool[:, nxt.u, :]).then_inc(sem("A_padh_done"), 1)
                if live(nxt, IMAGES):
                    act.wait_ge(sem("A_r1_done"), nxt.b + 1)
                    act.activation(h8[0:8, nxt.u, :], sm_a[0:8, 8:9], ACT.Silu, scale=1.0 / PIX, bias=b1r[0:8, :]).then_inc(sem("A_h8"), 1)
                if live(old, IMAGES):
                    route_rows("A_", old)
                if live(i, IMAGES):
                    a_silu(i, 1)
                if live(nxt, IMAGES):
                    act.wait_ge(sem("A_gshift"), nxt.b + 1)
                    act.activation(g_exp, g_shift, ACT.Exp).then_inc(sem("A_gexp"), 1)
                if live(old, IMAGES):
                    route_copy("A_", old)
                if live(old, IMAGES):
                    route_exp("A_", old)
                if live(nxt, IMAGES):
                    a_silu(nxt, 0)
                if live(old, IMAGES):
                    if some(old.b):
                        act.wait_ge(sem("A_scattered_rows1"), old.b * (16 * TPI))
                    act.activation(rows[1][:, :, 0:C], rows[0][:, :, 0:C], ACT.Copy).then_inc(sem("A_rows2_ready"), 1)

            sweep(act, IMAGES, a_step)

            def ffn(p, n, nj, gated, out_scale):
                nb = 2 if gated else 4

                def step(i):
                    nxt, old, older = i + 1, i + (-1), i + (-2)
                    if live(older, n):
                        act.wait_ge(sem(p + "y_done"), older.b + 1)
                        if some(older.b):
                            act.wait_ge(sem(p + "yt_done"), older.b)
                        if gated:
                            act.activation(ysb, psum[:, 6, :], ACT.Copy, scale=out_scale).then_inc(sem(p + "y_copied"), 1)
                        else:
                            apart(act)
                            f = act.value_load(tab_i[0:1, 1, bass.ds(older.b, 1)], min_val=0, max_val=E - 1)
                            act.activation(ysb, psum[:, 6, :], ACT.Identity, scale=out_scale,
                                           bias=vecs[:, bass.ds(f + VEC["fb2"], 1)]).then_inc(sem(p + "y_copied"), 1)
                    if live(nxt, n):
                        act.wait_ge(sem(p + "xt_done"), nxt.b + 1)
                        if some((nxt.b - 1) * nj):
                            act.wait_ge(sem(p + "up_done"), (nxt.b - 1) * nj)
                        act.activation(xh[nxt.u], psum[:, nxt.u, :], ACT.Copy).then_inc(sem(p + "xh_done"), 1)
                    if live(i, n):
                        if not gated:
                            e = act.value_load(tab_i[0:1, 1, bass.ds(i.b, 1)], min_val=0, max_val=E - 1)
                        for j in range(nj):
                            c = i.b * nj + j
                            m = (i.u * nj + j) % nb
                            act.wait_ge(sem(p + "up_done"), c + 1)
                            if gated:
                                if some(c - 1):
                                    act.wait_ge(sem(p + "g_done"), c - 1)
                                act.activation(sg[m], psum[:, 2 + 2 * m, :], ACT.Silu, scale=scale[:, S1:S1 + 1]).then_inc(sem(p + "silu"), 1)
                                if j:
                                    high(i, j - 1, c - 1)
                            else:
                                if some(c + 1 - nj):
                                    act.wait_ge(sem(p + "gl_done"), c + 1 - nj)
                                act.activation(g32[j], psum[:, 2 + m, :], ACT.Relu,
                                               bias=b1s[:, bass.ds(e * nj + j, 1)]).then_inc(sem(p + "up_read"), 1)
                        if gated:
                            high(i, nj - 1, i.b * nj + nj - 1)

                def high(i, j, c):
                    act.wait_ge(sem(p + "g_done"), c + 1)
                    if some(i.b - 1):
                        act.wait_ge(sem(p + "y_done"), i.b - 1)
                    act.activation(gh[i.u][:, j, :], g32[j], ACT.Copy).then_inc(sem(p + "gh_done"), 1)

                sweep(act, n, step, per=4)

            ffn("B_", TILES0, NJ0, True, y0_scale)

            def c_step(i):
                old, nxt = i + (-1), i + 1
                if live(nxt, IMAGES):
                    act.wait_ge(sem("C_image_stats"), nxt.b + 1)
                    apart(act)
                    if some(nxt.b - 2):
                        act.wait_ge(sem("C_logits_done"), nxt.b - 2)
                    apart(act)
                    if some(nxt.b):
                        act.wait_ge(sem("C_cm_done"), nxt.b)
                    apart(act)
                    tok = lambda tt: tokens[:, bass.ds(nxt.b * TPI + tt, 1), :].rearrange("p a c -> p (a c)")
                    normalise("C_", nxt, lambda tt: ntm[:, tt, :], tok, image_stats, "ntm")
                    act.wait_ge(sem("C_cm_done"), nxt.b + 1)
                    if some(nxt.b * 3 - 3):
                        act.wait_ge(sem("C_taps_done"), nxt.b * 3 - 3)
                    act.activation(vpad[nxt.u][:, 1:H + 1, 1:W + 1], tp.rearrange("p (h w) -> p h w", h=H), ACT.Copy,
                                   accum_out=pool[:, nxt.u, :]).then_inc(sem("C_inside"), 1)
                    act.wait_ge(sem("C_h_done"), nxt.b + 1)
                    act.activation(hg, sm_a[:, 0:1], ACT.Gelu, scale=1.0 / PIX, bias=vec("cb1")).then_inc(sem("C_gelu"), 1)
                if live(old, IMAGES):
                    route_rows("C_", old)
                    route_copy("C_", old)
                if live(i, IMAGES):
                    act.wait_ge(sem("C_taps_done"), i.b * 3 + 3)
                    if some(i.b):
                        act.wait_ge(sem("C_tok_done"), i.b)
                    act.activation(cacc, pair[i.u], ACT.Copy).then_inc(sem("C_conv_copied"), 1)
                if live(old, IMAGES):
                    route_exp("C_", old)

            sweep(act, IMAGES, c_step)
            ffn("D_", TILES1, NJ1, False, y1_scale)

            def f_step(i):
                if live(i, IMAGES):
                    act.wait_ge(sem("F_turned"), i.b + 1)
                    if some(i.h * 16):
                        act.wait_ge(sem(f"F_stored{i.u}"), i.h * 16)
                    act.activation(ocm[i.u], pair[i.u], ACT.Copy).then_inc(sem("F_out_ready"), 1)

            sweep(act, IMAGES, f_step)

        @block.vector
        def _(dve):
            L = Line()

            dve.wait_ge(sem("setup_loaded"), 16 * LOADS)
            dve.wait_ge(sem("stage_zeroed"), 4)
            dve.wait_ge(sem("vecs_ready"), 1)
            for col, x in ((SA, nat_a), (SS, nat_s), (S1, nat_b1), (S3, nat_b3), (S2, nat_b2), (D1, nat_d1), (D2, nat_d2)):
                x = x if len(x.shape) == 2 else x.rearrange("p a b -> p (a b)") if len(x.shape) == 3 else x.rearrange("p a b c -> p (a b c)")
                dve.tensor_reduce(mx[:, col:col + 1], x, AX_X, ALU.max, apply_absolute_value=True).then_inc(sem("dve_steps"), 1)
                dve.wait_ge(sem("dve_steps"), L.step())
            dve.tensor_reduce(gtmp[:, 0, :], vec("fb1", 0, 32), AX_X, ALU.max, apply_absolute_value=True).then_inc(sem("dve_steps"), 1)
            dve.wait_ge(sem("dve_steps"), L.step())
            dve.tensor_tensor(mx[:, D1:D1 + 1], mx[:, D1:D1 + 1], gtmp[:, 0, :], ALU.max).then_inc(sem("scale_steps"), 1)
            dve.wait_ge(sem("pe_turned"), 2)
            m = gvar[0:NS, 0, :]
            mi = m.bitcast(I32)
            sc, si = gmean[0:NS, 0, 0:1], gmean[0:NS, 0, 1:2]
            dve.reduce_max(m, sm_b[0:NS, 0:P], AX_X).then_inc(sem("dve_steps"), 1)
            dve.wait_ge(sem("dve_steps"), L.step())
            dve.tensor_scalar(m, m, 1e-30, None, ALU.max).then_inc(sem("dve_steps"), 1)
            dve.wait_ge(sem("dve_steps"), L.step())
            dve.tensor_scalar(mi, mi, 0x7F800000, None, ALU.bitwise_and).then_inc(sem("dve_steps"), 1)
            dve.wait_ge(sem("dve_steps"), L.step())
            dve.tensor_scalar(sc, m, 2.0, None, ALU.mult).then_inc(sem("dve_steps"), 1)
            dve.wait_ge(sem("dve_steps"), L.step())
            dve.tensor_scalar(si.bitcast(I32), sc.bitcast(I32), -1.0, float(0x7F000000), ALU.mult, ALU.add).then_inc(sem("dve_steps"), 1)
            dve.wait_ge(sem("dve_steps"), L.step())
            dve.tensor_scalar(spread[0:NS, 0:NS], ident[0:NS, 0:NS], sc, None, ALU.mult).then_inc(sem("dve_steps"), 1)
            dve.wait_ge(sem("dve_steps"), L.step())
            dve.tensor_scalar(spread[0:NS, NS:2 * NS], ident[0:NS, 0:NS], si, None, ALU.mult).then_inc(sem("scale_steps"), 1)
            dve.wait_ge(sem("pe_turned"), 3)
            dve.tensor_copy(scale, sm_b[:, 128:128 + 2 * NS]).then_inc(sem("scale_steps"), 1)
            dve.wait_ge(sem("scale_steps"), 3)

            def s_(c):
                return scale[:, c:c + 1]

            for n, c in enumerate((SA, SS)):
                dve.scalar_tensor_tensor(out=neg_sq[:, n:n + 1], in0=s_(c), scalar=-1.0, in1=s_(c), op0=ALU.mult, op1=ALU.mult).then_inc(sem("dve_steps"), 1)
                dve.wait_ge(sem("dve_steps"), L.step())
            dve.tensor_tensor(y0_scale, s_(S1), s_(S3), ALU.mult).then_inc(sem("dve_steps"), 1)
            dve.wait_ge(sem("dve_steps"), L.step())
            dve.tensor_tensor(y0_scale, y0_scale, s_(S2), ALU.mult).then_inc(sem("dve_steps"), 1)
            dve.wait_ge(sem("dve_steps"), L.step())
            dve.tensor_tensor(y1_scale, s_(D1), s_(D2), ALU.mult).then_inc(sem("dve_steps"), 1)
            dve.wait_ge(sem("dve_steps"), L.step())
            dve.tensor_scalar(gam[:, 0, 0:EC], vec("eg", 0, EC), s_(SA), None, ALU.mult).then_inc(sem("dve_steps"), 1)
            dve.wait_ge(sem("dve_steps"), L.step())
            dve.tensor_scalar(gam[:, 0, EC:EC + 1], vec("sg"), s_(SS), None, ALU.mult).then_inc(sem("dve_steps"), 1)
            dve.wait_ge(sem("dve_steps"), L.step())
            dve.tensor_copy(gam[:, 2, 0:EC], vec("eb", 0, EC))
            dve.tensor_copy(gam[:, 2, EC:EC + 1], vec("sb"))
            dve.tensor_scalar(gam[:, 1, :], gam[:, 0, :], -1.0, None, ALU.mult).then_inc(sem("dve_steps"), 1)
            dve.wait_ge(sem("dve_steps"), L.step())
            dve.tensor_scalar(b1s, vec("fb1", 0, E * NJ1), scale[:, NS + D1:NS + D1 + 1], None, ALU.mult).then_inc(sem("dve_steps"), 1)
            dve.wait_ge(sem("dve_steps"), L.step())
            dve.wait_ge(sem("const_ready"), 9)
            dve.tensor_scalar(first_slot, first_slot, 2.0, None, ALU.mult).then_inc(sem("dve_steps"), 1)
            dve.wait_ge(sem("dve_steps"), L.step())
            dve.memset(msum, 0.0).then_inc(sem("dve_steps"), 1)
            dve.wait_ge(sem("dve_steps"), L.step())
            dve.memset(msum16, 0.0).then_inc(sem("dve_steps"), 1)
            dve.wait_ge(sem("dve_steps"), L.step())
            dve.tensor_copy(idf, iota_t).then_inc(sem("dve_steps"), 1)
            dve.wait_ge(sem("dve_steps"), L.step())
            for n, (nat, s, hi, lo) in enumerate(((nat_d1.rearrange("p e f -> p (e f)"), D1, wd1_h, wd1_l),
                                                  (nat_d2.rearrange("p e j c -> p (e j c)"), D2, wd2_h, wd2_l))):
                dve.wait_ge(sem("direct_hi"), n + 1)
                dve.scalar_tensor_tensor(out=lo[:, :], in0=nat, scalar=scale[:, NS + s:NS + s + 1], in1=hi[:, :], op0=ALU.mult, op1=ALU.subtract).then_inc(sem("dve_steps"), 1)
                dve.wait_ge(sem("dve_steps"), L.step())
            for g, (ins, s, hi, lo) in enumerate(groups):
                dve.wait_ge(sem("group_hi"), g + 1)
                dve.scalar_tensor_tensor(out=lo, in0=psum[:, g % 6, 0:len(ins) * P], scalar=scale[:, NS + s:NS + s + 1],
                                         in1=hi, op0=ALU.mult, op1=ALU.subtract).then_inc(sem("group_split"), 1)
            dve.wait_ge(sem("group_split"), NG)
            dve.wait_ge(sem("plain_copied"), NPL)
            dve.sem_inc(sem("setup_done"), 1)

            def rsqrt(r, v, tmp):
                dve.tensor_scalar(r.bitcast(I32), v.bitcast(I32), -0.5, MAGIC, ALU.mult, ALU.add).then_inc(sem("dve_steps"), 1)
                seen = L.step()
                yield
                dve.wait_ge(sem("dve_steps"), seen)
                for _ in range(3):
                    dve.scalar_tensor_tensor(out=tmp, in0=r, scalar=-0.5, in1=r, op0=ALU.mult, op1=ALU.mult).then_inc(sem("dve_steps"), 1)
                    seen = L.step()
                    yield
                    dve.wait_ge(sem("dve_steps"), seen)
                    dve.tensor_tensor(tmp, tmp, v, ALU.mult).then_inc(sem("dve_steps"), 1)
                    seen = L.step()
                    yield
                    dve.wait_ge(sem("dve_steps"), seen)
                    dve.scalar_tensor_tensor(out=r, in0=tmp, scalar=1.5, in1=r, op0=ALU.add, op1=ALU.mult).then_inc(sem("dve_steps"), 1)
                    seen = L.step()
                    yield
                    dve.wait_ge(sem("dve_steps"), seen)

            def rsqrt_column(r, v, half, tmp):
                dve.tensor_scalar(r.bitcast(I32), v.bitcast(I32), -0.5, MAGIC, ALU.mult, ALU.add)
                dve.tensor_scalar(half, v, -0.5, None, ALU.mult).then_inc(sem("dve_steps"), 1)
                seen = L.step()
                yield
                dve.wait_ge(sem("dve_steps"), seen)
                for _ in range(3):
                    dve.scalar_tensor_tensor(out=tmp, in0=r, scalar=half, in1=r, op0=ALU.mult, op1=ALU.mult).then_inc(sem("dve_steps"), 1)
                    seen = L.step()
                    yield
                    dve.wait_ge(sem("dve_steps"), seen)
                    dve.scalar_tensor_tensor(out=r, in0=tmp, scalar=1.5, in1=r, op0=ALU.add, op1=ALU.mult).then_inc(sem("dve_steps"), 1)
                    seen = L.step()
                    yield
                    dve.wait_ge(sem("dve_steps"), seen)

            def token_stats(x, eps, s, done):
                for tt in range(TPI):
                    last = dve.bn_stats(s.st[:, tt, :], x(tt))
                last.then_inc(sem("dve_steps"), 1)
                seen = L.step()
                yield
                dve.wait_ge(sem("dve_steps"), seen)
                apart(dve)
                for tt in range(TPI):
                    last = dve.bn_aggr(s.mv[:, tt, :], s.st[:, tt, :])
                last.then_inc(sem("dve_steps"), 1)
                seen = L.step()
                yield
                dve.wait_ge(sem("dve_steps"), seen)
                dve.tensor_scalar(s.var, s.mv[:, :, 1], eps, None, ALU.add).then_inc(sem("dve_steps"), 1)
                seen = L.step()
                yield
                dve.wait_ge(sem("dve_steps"), seen)
                yield from rsqrt(s.rstd, s.var, s.tmp)
                dve.scalar_tensor_tensor(out=s.bias, in0=s.mv[:, :, 0], scalar=-1.0, in1=s.rstd,
                                         op0=ALU.mult, op1=ALU.mult).then_inc(done, 1)

            def top(view, width, desc, tmp, hot, best, first):
                dve.tensor_reduce(best, view, AX_X, ALU.max).then_inc(sem("dve_steps"), 1)
                seen = L.step()
                yield
                dve.wait_ge(sem("dve_steps"), seen)
                dve.tensor_tensor(tmp, view, bcast(best, width), ALU.is_equal).then_inc(sem("dve_steps"), 1)
                seen = L.step()
                yield
                dve.wait_ge(sem("dve_steps"), seen)
                dve.tensor_tensor(tmp, tmp, desc, ALU.mult).then_inc(sem("dve_steps"), 1)
                seen = L.step()
                yield
                dve.wait_ge(sem("dve_steps"), seen)
                dve.tensor_reduce(first, tmp, AX_X, ALU.max).then_inc(sem("dve_steps"), 1)
                seen = L.step()
                yield
                dve.wait_ge(sem("dve_steps"), seen)
                dve.tensor_tensor(hot, tmp, bcast(first, width), ALU.is_equal).then_inc(sem("dve_steps"), 1)
                seen = L.step()
                yield
                dve.wait_ge(sem("dve_steps"), seen)

            def route_stats(p, i):
                dve.wait_ge(sem("A_tok_copied" if p == "A_" else "C_tok_added"), i.b + 1)
                apart(dve)
                if some(i.b):
                    dve.wait_ge(sem(p + "rows_ready"), i.b)
                apart(dve)
                tok = lambda tt: tokens[:, bass.ds(i.b * TPI + tt, 1), :].rearrange("p a c -> p (a c)")
                yield from token_stats(tok, 1e-5, row_stats, sem(p + "row_stats"))

            def route_choose(p, i, choices, pause):
                for _ in range(pause):
                    yield
                lg = sm_b[:, 0:TPI * E].rearrange("p (t e) -> p t e", e=E)
                dve.wait_ge(sem(p + "logits_done"), i.b + 1)
                if choices == 1:
                    dve.tensor_tensor(shifted, lg, gate1_b.to_broadcast([P, TPI, E]), ALU.add).then_inc(sem("dve_steps"), 1)
                    seen = L.step()
                    yield
                    dve.wait_ge(sem("dve_steps"), seen)
                    lg = shifted
                dve.tensor_reduce(s8[0], lg, AX_X, ALU.max).then_inc(sem("dve_steps"), 1)
                seen = L.step()
                yield
                dve.wait_ge(sem("dve_steps"), seen)
                dve.tensor_tensor(shifted, lg, bcast(s8[0], E), ALU.subtract).then_inc(sem(p + "shifted"), 1)
                yield
                dve.wait_ge(sem(p + "exped"), i.b + 1)
                dve.tensor_reduce(s8[1], exped, AX_X, ALU.add).then_inc(sem("dve_steps"), 1)
                seen = L.step()
                yield
                dve.wait_ge(sem("dve_steps"), seen)
                dve.reciprocal(s8[2], s8[1]).then_inc(sem("dve_steps"), 1)
                seen = L.step()
                yield
                dve.wait_ge(sem("dve_steps"), seen)
                dve.tensor_tensor(probs, exped, bcast(s8[2], E), ALU.mult).then_inc(sem("dve_steps"), 1)
                seen = L.step()
                yield
                dve.wait_ge(sem("dve_steps"), seen)
                yield from top(probs, E, desc8, tmp8, hots[:, 0], bests[:, 0, :], s8[3])

            def route_second(p, i, choices):
                if choices == 2:
                    dve.scalar_tensor_tensor(out=probs, in0=hots[:, 0], scalar=-2.0, in1=probs, op0=ALU.mult, op1=ALU.add).then_inc(sem("dve_steps"), 1)
                    seen = L.step()
                    yield
                    dve.wait_ge(sem("dve_steps"), seen)
                    yield from top(probs, E, desc8, tmp8, hots[:, 1], bests[:, 1, :], s8[3])
                if choices == 2:
                    dve.tensor_tensor(mask, hots[:, 0], hots[:, 1], ALU.add).then_inc(sem(p + "mask_ready"), 1)
                else:
                    dve.tensor_copy(mask, hots[:, 0]).then_inc(sem(p + "mask_ready"), 1)

            def route_place(p, i, choices):
                dve.wait_ge(sem(p + ("rows2_ready" if choices == 2 else "rows_ready")), i.b + 1)
                bufs = [rows[row_buffer(p, i, k)] for k in range(choices)]
                for k, buf in enumerate(bufs):
                    dve.tensor_scalar(buf[:, :, C], idf, float(k * TOKENS), None, ALU.add)
                    if isinstance(i.b, int) and i.b < 3 - choices:
                        dve.memset(buf[:, :, C + 2:ROW], 0.0)
                if choices == 2:
                    dve.tensor_tensor(s8[4], bests[:, 0, :], bests[:, 1, :], ALU.add).then_inc(sem("dve_steps"), 1)
                    seen = L.step()
                    yield
                    dve.wait_ge(sem("dve_steps"), seen)
                    dve.tensor_scalar(s8[4], s8[4], 1e-9, None, ALU.add).then_inc(sem("dve_steps"), 1)
                    seen = L.step()
                    yield
                    dve.wait_ge(sem("dve_steps"), seen)
                    dve.reciprocal(s8[5], s8[4]).then_inc(sem("dve_steps"), 1)
                    seen = L.step()
                    yield
                    dve.wait_ge(sem("dve_steps"), seen)
                for k, buf in enumerate(bufs):
                    if choices == 2:
                        dve.tensor_tensor(buf[:, :, C + 1], bests[:, k, :], s8[5], ALU.mult)
                    else:
                        dve.tensor_copy(buf[:, :, C + 1], bests[:, k, :])
                dve.tensor_scalar(idf, idf, float(PIX), None, ALU.add)
                dve.wait_ge(sem(p + "mask_ready"), i.b + 1)
                dve.tensor_reduce(s8[6], mask.rearrange("p t e -> p e t"), AX_X, ALU.add).then_inc(sem("dve_steps"), 1)
                seen = L.step()
                yield
                dve.wait_ge(sem("dve_steps"), seen)
                dve.wait_ge(sem(p + "pos_done"), i.b + 1)
                pos = sm_b[:, 64:64 + TPI * E].rearrange("p (t e) -> p t e", e=E)
                dve.tensor_tensor(msum, msum, s8[6], ALU.add).then_inc(sem("dve_steps"), 1)
                summed = L.step()
                dve.tensor_tensor(place, pos, first_slot, ALU.add).then_inc(sem("dve_steps"), 1)
                seen = L.step()
                yield
                dve.wait_ge(sem("dve_steps"), seen)
                dve.wait_ge(sem("dve_steps"), summed)
                dve.tensor_copy(msum16, msum).then_inc(sem(p + "msum"), 1)
                every = place.unsqueeze(1).to_broadcast([P, choices, TPI, E])
                dve.tensor_tensor(prod2[:, 0:choices], every, hots[:, 0:choices], ALU.mult).then_inc(sem("dve_steps"), 1)
                seen = L.step()
                yield
                dve.wait_ge(sem("dve_steps"), seen)
                dve.tensor_reduce(slot_f[:, 0:choices, :], prod2[:, 0:choices], AX_X, ALU.add).then_inc(sem("dve_steps"), 1)
                seen = L.step()
                yield
                dve.wait_ge(sem("dve_steps"), seen)
                if choices == 1:
                    dve.tensor_tensor(tmp8, pos, hots[:, 0], ALU.mult).then_inc(sem("dve_steps"), 1)
                    seen = L.step()
                    yield
                    dve.wait_ge(sem("dve_steps"), seen)
                    dve.tensor_reduce(s8[7], tmp8, AX_X, ALU.add).then_inc(sem("dve_steps"), 1)
                    seen = L.step()
                    yield
                    dve.wait_ge(sem("dve_steps"), seen)
                    dve.tensor_scalar(s8[7], s8[7], float(CAP), float(2 * SLOTS), ALU.is_ge, ALU.mult).then_inc(sem("dve_steps"), 1)
                    seen = L.step()
                    yield
                    dve.wait_ge(sem("dve_steps"), seen)
                    dve.tensor_tensor(slot_f[:, 0, :], slot_f[:, 0, :], s8[7], ALU.add).then_inc(sem("dve_steps"), 1)
                    seen = L.step()
                    yield
                    dve.wait_ge(sem("dve_steps"), seen)
                first = 0 if choices == 2 else i.u
                dve.tensor_copy(slot_i[:, first:first + choices, :], slot_f[:, 0:choices, :]).then_inc(sem(p + "slots_known"), 1)
                dve.wait_ge(sem(p + "msum"), i.b + 1)

            def group_stats(i, j):
                par = of(j)
                dve.wait_ge(sem(f"A_conv_done{j}"), i.b + 1)
                dve.bn_stats(gst[:, par, 0:6], pair[par][:, 0:512])
                dve.bn_stats(gst[:, par, 6:12], pair[par][:, 512:1024]).then_inc(sem("dve_steps"), 1)
                seen = L.step()
                yield
                dve.wait_ge(sem("dve_steps"), seen)
                apart(dve)
                dve.bn_aggr(me2[:, par, :], gst[:, par, :]).then_inc(sem("dve_steps"), 1)
                seen = L.step()
                yield
                dve.wait_ge(sem("dve_steps"), seen)
                m = me2[:, par, 0:1]
                dve.scalar_tensor_tensor(out=me2[:, par, 1:2], in0=m, scalar=m, in1=me2[:, par, 1:2],
                                         op0=ALU.mult, op1=ALU.add).then_inc(sem(f"A_gstat{j}"), 1)

            def group_affine(i, j):
                par = of(j)
                gg, gv, gr, gt = (x[:, par, :] for x in (gmean, gvar, grstd, gtmp))
                dve.wait_ge(sem(f"A_gn_done{j}"), i.b + 1)
                if j == 0:
                    gs, ngs, beta = (gam[:, c, EC:EC + 1] for c in range(3))
                else:
                    gs, ngs, beta = (sel[:, i.u, j - 1, c:c + 1] for c in range(3))
                dve.tensor_copy(gg, sm_a[:, 0:2]).then_inc(sem(f"A_gn_read{j}"), 1)
                yield
                dve.wait_ge(sem(f"A_gn_read{j}"), i.b + 1)
                dve.scalar_tensor_tensor(out=gv, in0=gg[:, 0:1], scalar=gg[:, 0:1], in1=gg[:, 1:2], op0=ALU.mult, op1=ALU.subtract).then_inc(sem("dve_steps"), 1)
                seen = L.step()
                yield
                dve.wait_ge(sem("dve_steps"), seen)
                dve.tensor_scalar(gv, gv, neg_sq[:, (0 if j else 1):(1 if j else 2)], 1e-5, ALU.mult, ALU.add).then_inc(sem("dve_steps"), 1)
                seen = L.step()
                yield
                dve.wait_ge(sem("dve_steps"), seen)
                yield from rsqrt_column(gr, gv, gneg[:, par, :], gt)
                dve.tensor_tensor(gsb[:, par, 0:1], gr, gs, ALU.mult)
                dve.tensor_tensor(gt, gr, ngs, ALU.mult).then_inc(sem("dve_steps"), 1)
                seen = L.step()
                yield
                dve.wait_ge(sem("dve_steps"), seen)
                dve.scalar_tensor_tensor(out=gsb[:, par, 1:2], in0=gg[:, 0:1], scalar=gt, in1=beta,
                                         op0=ALU.mult, op1=ALU.add).then_inc(sem(f"A_gsb{j}"), 1)

            def accumulate(i, j, pause):
                par = of(j)
                for _ in range(pause):
                    yield
                dve.wait_ge(sem(f"A_silu{j}"), i.b + 1)
                dve.wait_ge(sem(f"A_acc{j - 1}"), i.b + 1)
                dve.scalar_tensor_tensor(out=acc[i.u], in0=act_o[par], scalar=gates[:, i.u, j - 1:j], in1=acc[i.u],
                                         op0=ALU.mult, op1=ALU.add).then_inc(sem(f"A_acc{j}"), 1)

            def a_gates(i):
                dve.wait_ge(sem("A_r2_done"), i.b + 1)
                dve.tensor_tensor(g_logit, sm_a[:, 16:16 + EC].unsqueeze(1), b2r, ALU.add).then_inc(sem("dve_steps"), 1)
                seen = L.step()
                yield
                dve.wait_ge(sem("dve_steps"), seen)
                dve.tensor_reduce(s4[0], g_logit, AX_X, ALU.max).then_inc(sem("dve_steps"), 1)
                seen = L.step()
                yield
                dve.wait_ge(sem("dve_steps"), seen)
                dve.tensor_tensor(g_shift, g_logit, bcast(s4[0], EC), ALU.subtract).then_inc(sem("A_gshift"), 1)
                yield
                dve.wait_ge(sem("A_gexp"), i.b + 1)
                dve.tensor_reduce(s4[1], g_exp, AX_X, ALU.add).then_inc(sem("dve_steps"), 1)
                seen = L.step()
                yield
                dve.wait_ge(sem("dve_steps"), seen)
                dve.reciprocal(s4[2], s4[1]).then_inc(sem("dve_steps"), 1)
                seen = L.step()
                yield
                dve.wait_ge(sem("dve_steps"), seen)
                dve.tensor_tensor(g_prob, g_exp, bcast(s4[2], EC), ALU.mult).then_inc(sem("dve_steps"), 1)
                seen = L.step()
                yield
                dve.wait_ge(sem("dve_steps"), seen)
                yield from top(g_prob, EC, desc4, g_tmp, g_hot[:, 0:1, :], g_best[:, 0:1], g_first[:, 0:1])
                dve.scalar_tensor_tensor(out=g_prob, in0=g_hot[:, 0:1, :], scalar=-2.0, in1=g_prob, op0=ALU.mult, op1=ALU.add).then_inc(sem("dve_steps"), 1)
                seen = L.step()
                yield
                dve.wait_ge(sem("dve_steps"), seen)
                yield from top(g_prob, EC, desc4, g_tmp, g_hot[:, 1:2, :], g_best[:, 1:2], g_first[:, 1:2])
                dve.tensor_scalar(eidx[:, i.u, :], g_first, -1.0, float(EC), ALU.mult, ALU.add).then_inc(sem("A_gate_ready"), 1)
                dve.tensor_tensor(s4[0], g_best[:, 0:1], g_best[:, 1:2], ALU.add).then_inc(sem("dve_steps"), 1)
                seen = L.step()
                yield
                dve.wait_ge(sem("dve_steps"), seen)
                dve.reciprocal(s4[1], s4[0]).then_inc(sem("dve_steps"), 1)
                seen = L.step()
                yield
                dve.wait_ge(sem("dve_steps"), seen)
                dve.tensor_scalar(g_best, g_best, s4[1], None, ALU.mult).then_inc(sem("dve_steps"), 1)
                seen = L.step()
                yield
                dve.wait_ge(sem("dve_steps"), seen)
                dve.scalar_tensor_tensor(out=gates[:, i.u, :], in0=g_best, scalar=0.01, in1=g_best, op0=ALU.is_ge, op1=ALU.mult)
                tables = gam[:, :, 0:EC].unsqueeze(1).to_broadcast([P, 2, 3, EC])
                dve.tensor_tensor(g_pick, g_hot.unsqueeze(2).to_broadcast([P, 2, 3, EC]), tables, ALU.mult).then_inc(sem("dve_steps"), 1)
                seen = L.step()
                yield
                dve.wait_ge(sem("dve_steps"), seen)
                dve.tensor_reduce(sel[:, i.u], g_pick, AX_X, ALU.add).then_inc(sem("dve_steps"), 1)
                seen = L.step()
                yield
                dve.wait_ge(sem("dve_steps"), seen)

            def route_rest(i):
                yield from route_second("A_", i, 2)
                yield from route_place("A_", i, 2)

            def shared_job(i, pause):
                for _ in range(pause):
                    yield
                yield from group_stats(i, 0)
                yield from group_affine(i, 0)

            def a_step(i):
                older, old, nxt = i + (-2), i + (-1), i + 1
                has_older, has_old, has, has_nxt = (live(x, IMAGES) for x in (older, old, i, nxt))
                weave(has_old and group_stats(old, 2))
                if has_nxt:
                    dve.wait_ge(sem("A_xt_done"), nxt.b + 1)
                    if some(nxt.b):
                        apart(dve)
                        dve.wait_ge(sem("A_ntm"), nxt.b)
                    apart(dve)
                weave(has_old and group_affine(old, 2),
                      has_nxt and token_stats(lambda tt: tp_tok[:, tt, :], 1e-6, image_stats, sem("A_image_stats")),
                      has_older and route_rest(older))
                weave(has_old and accumulate(old, 2, 0))
                weave(has_old and route_stats("A_", old),
                      has and group_stats(i, 1))
                if has_nxt:
                    dve.wait_ge(sem("A_padh_done"), nxt.b + 1)
                    inside = [x[nxt.u][:, 1:H + 1, 1:W + 1] for x in (pad_h, pad_l)]
                    dve.tensor_tensor(inside[1], tp.rearrange("p (h w) -> p h w", h=H), inside[0], ALU.subtract).then_inc(sem("A_padl_done"), 1)
                    dve.wait_ge(sem("A_h8"), nxt.b + 1)
                    dve.tensor_scalar(hb[0:8, nxt.u, :], ones_f[0:8, :], h8[0:8, nxt.u, :], None, ALU.mult).then_inc(sem("A_hb"), 1)
                weave(has and group_affine(i, 1))
                weave(has_nxt and a_gates(nxt),
                      has and accumulate(i, 1, 2),
                      has_nxt and shared_job(nxt, 3),
                      has_old and route_choose("A_", old, 2, 11))

            sweep(dve, IMAGES, a_step, L, STEPS_A)

            def table(p, src, limit):
                dve.wait_ge(sem(src + "counts_done"), 1)
                one = slice(0, 1)
                cnt, til, cum, ones8 = (x[one] for x in b_e)
                big, thr = b_big[one], b_thr[one]
                o1, o2, o3, o4 = (x[one] for x in b_one)
                dve.tensor_scalar(cnt, sm_a[one, 32:32 + E], float(limit), None, ALU.min).then_inc(sem("dve_steps"), 1)
                dve.wait_ge(sem("dve_steps"), L.step())
                dve.tensor_tensor(ones8, cnt, first_slot[one, 0, :], ALU.add).then_inc(sem("dve_steps"), 1)
                dve.wait_ge(sem("dve_steps"), L.step())
                dve.tensor_copy(tail_i[one], ones8).then_inc(sem("dve_steps"), 1)
                dve.wait_ge(sem("dve_steps"), L.step())
                dve.tensor_tensor(thr, bcast(cnt, 33), iota_j[one].unsqueeze(1).to_broadcast([1, E, 33]), ALU.is_gt).then_inc(sem("dve_steps"), 1)
                dve.wait_ge(sem("dve_steps"), L.step())
                dve.tensor_reduce(til, thr, AX_X, ALU.add).then_inc(sem("dve_steps"), 1)
                dve.wait_ge(sem("dve_steps"), L.step())
                dve.memset(ones8, 1.0).then_inc(sem("dve_steps"), 1)
                dve.wait_ge(sem("dve_steps"), L.step())
                dve.tensor_tensor_scan(cum, ones8, til, 0.0, ALU.mult, ALU.add).then_inc(sem("dve_steps"), 1)
                dve.wait_ge(sem("dve_steps"), L.step())
                dve.tensor_tensor(big, bcast(iota_i[one], E), cum.unsqueeze(1).to_broadcast([1, TILES0, E]), ALU.is_ge).then_inc(sem("dve_steps"), 1)
                dve.wait_ge(sem("dve_steps"), L.step())
                dve.tensor_reduce(o1, big, AX_X, ALU.add).then_inc(sem("dve_steps"), 1)
                dve.wait_ge(sem("dve_steps"), L.step())
                dve.tensor_tensor(big, big, til.unsqueeze(1).to_broadcast([1, TILES0, E]), ALU.mult).then_inc(sem("dve_steps"), 1)
                dve.wait_ge(sem("dve_steps"), L.step())
                dve.tensor_reduce(o2, big, AX_X, ALU.add).then_inc(sem("dve_steps"), 1)
                dve.wait_ge(sem("dve_steps"), L.step())
                dve.tensor_tensor(o3, iota_i[one], o2, ALU.subtract).then_inc(sem("dve_steps"), 1)
                dve.wait_ge(sem("dve_steps"), L.step())
                dve.tensor_scalar(o3, o3, float(TILE), None, ALU.mult).then_inc(sem("dve_steps"), 1)
                dve.wait_ge(sem("dve_steps"), L.step())
                dve.scalar_tensor_tensor(out=o4, in0=o1, scalar=float(REG), in1=o3, op0=ALU.mult, op1=ALU.add).then_inc(sem("dve_steps"), 1)
                dve.wait_ge(sem("dve_steps"), L.step())
                dve.tensor_scalar(tab_i[one, 0, :], o4, float(E * REG), None, ALU.min).then_inc(sem("dve_steps"), 1)
                dve.wait_ge(sem("dve_steps"), L.step())
                dve.tensor_scalar(tab_i[one, 1, :], o1, float(E - 1), None, ALU.min).then_inc(sem(p + "table_ready"), 1)

            def ffn(p, n, nj, gated, count):
                def low(i, j):
                    c = i.b * nj + j
                    if gated:
                        dve.wait_ge(sem(p + "gh_done"), c + 1)
                    dve.tensor_tensor(gl[i.u][:, j, :], g32[j], gh[i.u][:, j, :], ALU.subtract).then_inc(sem(p + "gl_done"), 1)

                def step(i):
                    nxt, older = i + 1, i + (-2)
                    if live(nxt, n):
                        dve.wait_ge(sem(p + "xh_done"), nxt.b + 1)
                        dve.tensor_tensor(xl[nxt.u], psum[:, nxt.u, :], xh[nxt.u], ALU.subtract).then_inc(sem(p + "xl_done"), 1)
                    for j in range(nj):
                        if live(i, n):
                            c = i.b * nj + j
                            m = (i.u * nj + j) % 2
                            if gated:
                                dve.wait_ge(sem(p + "silu"), c + 1)
                                if some(c + 1 - nj):
                                    dve.wait_ge(sem(p + "gl_done"), c + 1 - nj)
                                dve.scalar_tensor_tensor(out=g32[j], in0=psum[:, 3 + 2 * m, :], scalar=scale[:, NS + S1:NS + S1 + 1],
                                                         in1=sg[m], op0=ALU.mult, op1=ALU.mult).then_inc(sem(p + "g_done"), 1)
                                if j:
                                    low(i, j - 1)
                            else:
                                dve.wait_ge(sem(p + "up_read"), c + 1)
                                if some(i.b - 1):
                                    dve.wait_ge(sem(p + "y_done"), i.b - 1)
                                dve.tensor_copy(gh[i.u][:, j, :], g32[j]).then_inc(sem("dve_steps"), 1)
                                dve.wait_ge(sem("dve_steps"), L.step())
                                low(i, j)
                        if j == 0 and live(older, n):
                            dve.wait_ge(sem(p + "yt_done"), older.b + 1)
                            dve.wait_ge(sem(p + "ids_copied"), older.b * 2 + 2)
                            last = older + (-2)
                            if live(last, n):
                                dve.wait_ge(sem(f"{p}scattered{last.v}"), (last.w + 1) * (16 * QT))
                            gate = idg[older.v][:, :, 1:2].to_broadcast([P, QT, C])
                            dve.tensor_tensor(yt[older.u], psum[:, 7, :].rearrange("p (q c) -> p q c", q=QT), gate, ALU.mult).then_inc(sem(p + "yt_ready"), 1)
                    if live(i, n) and gated:
                        low(i, nj - 1)

                sweep(dve, n, step, L, count, per=4)

            table("B_", "A_", TOKENS)
            ffn("B_", TILES0, NJ0, True, 0)

            dve.memset(msum, 0.0).then_inc(sem("dve_steps"), 1)
            dve.wait_ge(sem("dve_steps"), L.step())
            dve.memset(msum16, 0.0).then_inc(sem("dve_steps"), 1)
            dve.wait_ge(sem("dve_steps"), L.step())
            dve.tensor_copy(idf, iota_t).then_inc(sem("dve_steps"), 1)
            dve.wait_ge(sem("dve_steps"), L.step())

            def diagonals(i, third):
                if some(i.b * 3 - 2 + third):
                    dve.wait_ge(sem("C_taps_done"), i.b * 3 - 2 + third)
                k = slice(3 * third, 3 * third + 3)
                dve.tensor_tensor(diag[:, k, :], ident.unsqueeze(1).to_broadcast([P, 3, P]), bcast(wd[:, k], P), ALU.mult).then_inc(sem("C_diag"), 1)

            def add_and_stats(i):
                dve.wait_ge(sem("C_y_summed"), i.b + 1)
                dst = tokens[:, bass.ds(i.b * TPI, TPI), :]
                dve.tensor_tensor(dst, dst, ya[i.u], ALU.add).then_inc(sem("C_added"), 1)
                dve.wait_ge(sem("C_added"), i.b + 1)
                apart(dve)
                if some(i.b):
                    dve.wait_ge(sem("C_ntm"), i.b)
                apart(dve)
                tok = lambda tt: tokens[:, bass.ds(i.b * TPI + tt, 1), :].rearrange("p a c -> p (a c)")
                weave(token_stats(tok, 1e-6, image_stats, sem("C_image_stats")))

            def c_step(i):
                older, old, nxt = i + (-2), i + (-1), i + 1
                has_older, has_old, has_nxt = (live(x, IMAGES) for x in (older, old, nxt))
                if isinstance(i.b, int) and i.b == -1:
                    add_and_stats(nxt)
                if has_old:
                    dve.wait_ge(sem("C_tok_done"), old.b + 1)
                    dst = tokens[:, bass.ds(old.b * TPI, TPI), :]
                    dve.tensor_tensor(dst, dst, tp_tok, ALU.add).then_inc(sem("C_tok_added"), 1)
                weave(has_old and route_stats("C_", old),
                      has_older and route_place("C_", older, 1))
                if has_nxt:
                    dve.wait_ge(sem("C_wd_done"), nxt.b + 1)
                    dve.tensor_tensor(wd, sm_a[:, 8:8 + TAPS], b2_taps, ALU.add).then_inc(sem("C_wd_read"), 1)
                    dve.wait_ge(sem("C_wd_read"), nxt.b + 1)
                    diagonals(nxt, 0)
                    diagonals(nxt, 1)
                if live(i + 2, IMAGES):
                    add_and_stats(i + 2)
                weave(has_old and route_choose("C_", old, 1, 0))
                weave(has_old and route_second("C_", old, 1))
                if has_nxt:
                    diagonals(nxt, 2)

            sweep(dve, IMAGES, c_step, L, STEPS_C)
            table("D_", "C_", CAP)
            ffn("D_", TILES1, NJ1, False, 4 * NJ1)

            def f_step(i):
                if not live(i, IMAGES):
                    return
                z = zf[i.u]
                dve.wait_ge(sem(f"F_loaded{i.u}"), i.h * 16 + 16)
                if some(i.b):
                    dve.wait_ge(sem("F_added"), i.b)
                dve.tensor_scalar(rep, z, FLT_MAX, 1e4, ALU.is_gt, ALU.mult).then_inc(sem("dve_steps"), 1)
                dve.wait_ge(sem("dve_steps"), L.step())
                dve.tensor_scalar(nn, z, -FLT_MAX, 1e4, ALU.is_lt, ALU.mult).then_inc(sem("dve_steps"), 1)
                dve.wait_ge(sem("dve_steps"), L.step())
                dve.tensor_tensor(rep, rep, nn, ALU.subtract).then_inc(sem("dve_steps"), 1)
                dve.wait_ge(sem("dve_steps"), L.step())
                dve.tensor_scalar(finite, z, 0.0, 0.0, ALU.mult, ALU.is_equal).then_inc(sem("dve_steps"), 1)
                dve.wait_ge(sem("dve_steps"), L.step())
                apart(dve)
                dve.copy_predicated(rep, finite, z).then_inc(sem("dve_steps"), 1)
                dve.wait_ge(sem("dve_steps"), L.step())
                if some(i.b - 1):
                    dve.wait_ge(sem("F_turned"), i.b - 1)
                dve.tensor_tensor(osum[i.u].rearrange("p (t c) -> p t c", t=TPI), tokens[:, bass.ds(i.b * TPI, TPI), :],
                                  rep.rearrange("p (t c) -> p t c", t=TPI), ALU.add).then_inc(sem("F_added"), 1)

            sweep(dve, IMAGES, f_step, L, 10)


_INS = ['x', 'L0_conv_router_w1', 'L0_conv_router_b1', 'L0_conv_router_w2', 'L0_conv_router_b2', 'L0_conv_expert_w',
        'L0_conv_expert_gn_gamma', 'L0_conv_expert_gn_beta', 'L0_conv_shared_w', 'L0_conv_shared_gn_gamma',
        'L0_conv_shared_gn_beta', 'L0_ffn_router_w', 'L0_ffn_w1', 'L0_ffn_w2', 'L0_ffn_w3', 'L1_conv_w1', 'L1_conv_b1',
        'L1_conv_w2', 'L1_conv_b2', 'L1_ffn_gate_w', 'L1_ffn_gate_b', 'L1_ffn_w1', 'L1_ffn_b1', 'L1_ffn_w2', 'L1_ffn_b2']


def kernel(**inputs):
    import concourse.bacc as bacc
    from concourse.bass_utils import run_bass_kernel_spmd

    nc = bacc.Bacc("TRN2", target_bir_lowering=False, num_devices=1)
    arrays, aps = {}, {}
    for name in _INS:
        x = np.ascontiguousarray(inputs[name])
        arrays[f"in_{name}"] = x
        aps[name] = nc.dram_tensor(f"in_{name}", x.shape, mybir.dt.from_np(x.dtype), kind="ExternalInput").ap()
    out = nc.dram_tensor("out_image", (IMAGES, C, H, W), F32, kind="ExternalOutput").ap()
    build(nc, aps, out)
    r = run_bass_kernel_spmd(nc, [arrays], core_ids=[0])
    return r.results[0]["out_image"]
```
